# Optimizing a Trainium2 kernel written in Bass

```python
import numpy as np
import jax
import jax.numpy as jnp

def _softmax(x, axis=-1):
    return jax.nn.softmax(x, axis=axis)

def _gelu(x):
    return jax.nn.gelu(x, approximate=True)

def _silu(x):
    return jax.nn.silu(x)

def _sigmoid(x):
    return jax.nn.sigmoid(x)

def _layernorm(x, axis=-1, eps=1e-05):
    m = jnp.mean(x, axis=axis, keepdims=True)
    v = jnp.var(x, axis=axis, keepdims=True)
    return (x - m) / jnp.sqrt(v + eps)

def _scatter_add(tgt, idx, src, axis=0):
    return tgt.at[idx].add(src)

def _segment_sum(src, seg, n):
    return jax.ops.segment_sum(src, seg, n)
kernel_name = 'mk_gnn_resnorm_d4_gnn_r32_60ffeb'

def setup_inputs(seed: int=0):
    np.random.seed(seed)
    _w = jnp.asarray

    def _rec_inputs():
        import jax
        import jax.numpy as jnp
        _gk = jax.random.key(seed)
        x = -0.000202 + 1 * jax.random.normal(jax.random.fold_in(_gk, 1), (50000, 128), jnp.float32)
        src = jax.random.randint(jax.random.fold_in(_gk, 2), (25000,), 0, 50000, jnp.int32)
        dst = jnp.minimum((50000 * jax.random.uniform(jax.random.fold_in(_gk, 3), (25000,)) ** 2.0).astype(jnp.int32), 49999)
        _o = jnp.argsort(dst, stable=True)
        src = src[_o]
        dst = dst[_o]
        edge_attr_128 = -8.16379e-05 + 0.999858 * jax.random.normal(jax.random.fold_in(_gk, 11), (25000, 128), jnp.float32)
        edge_type_1001 = jax.random.randint(jax.random.fold_in(_gk, 13), (25000,), 0, 1001, jnp.int32)
        edge_weight = jax.random.uniform(jax.random.fold_in(_gk, 14), (25000,), jnp.float32, 0.0, 0.999999)
        return (x, src, dst, edge_attr_128, edge_type_1001, edge_weight)
    x, src, dst, edge_attr_128, edge_type_1001, edge_weight = _rec_inputs()

    def _L0_gnn_setup():
        import jax, jax.numpy as jnp
        import numpy as np
        N_NODES = 50000
        N_EDGES = 50000
        D = 128
        N_LAYERS = 2
        NEG_SLOPE = 0.2

        def _gcn_layer(x, src, dst, ew, Ws, bs, Wn, bn, bias):
            n = x.shape[0]
            msg = x[src] * ew[:, None]
            agg = jax.ops.segment_sum(msg, dst, num_segments=n)
            agg = agg + x
            cnt = jax.ops.segment_sum(jnp.ones_like(ew), dst, num_segments=n) + 1.0
            neigh = agg / cnt[:, None]
            out = x @ Ws.T + bs + neigh @ Wn.T + bn + bias
            return jnp.where(out > 0, out, NEG_SLOPE * out)
        key = jax.random.key(seed)
        ks = jax.random.split(key, 10)
        user_embeddings = jax.random.normal(ks[0], (N_NODES, D), dtype=jnp.float32)
        social_edge_index = jax.random.randint(ks[1], (2, N_EDGES), 0, N_NODES, dtype=jnp.int64)
        social_edge_weights = jax.random.uniform(ks[2], (N_EDGES,), dtype=jnp.float32)
        s = 1.0 / np.sqrt(D)
        W_self = jax.random.uniform(ks[3], (N_LAYERS, D, D), minval=-s, maxval=s, dtype=jnp.float32)
        b_self = jax.random.uniform(ks[4], (N_LAYERS, D), minval=-s, maxval=s, dtype=jnp.float32)
        W_neigh = jax.random.uniform(ks[5], (N_LAYERS, D, D), minval=-s, maxval=s, dtype=jnp.float32)
        b_neigh = jax.random.uniform(ks[6], (N_LAYERS, D), minval=-s, maxval=s, dtype=jnp.float32)
        layer_bias = jnp.zeros((N_LAYERS, D), dtype=jnp.float32)
        W_agg = jax.random.uniform(ks[7], (D, D), minval=-s, maxval=s, dtype=jnp.float32)
        b_agg = jax.random.uniform(ks[8], (D,), minval=-s, maxval=s, dtype=jnp.float32)
        return {'user_embeddings': user_embeddings, 'social_edge_index': social_edge_index, 'social_edge_weights': social_edge_weights, 'W_self': W_self, 'b_self': b_self, 'W_neigh': W_neigh, 'b_neigh': b_neigh, 'layer_bias': layer_bias, 'W_agg': W_agg, 'b_agg': b_agg}
    _L0_gnn_all = _L0_gnn_setup()
    _L0_gnn_in = {k: v for k, v in _L0_gnn_all.items() if k in ('W_self', 'b_self', 'W_neigh', 'b_neigh', 'layer_bias', 'W_agg', 'b_agg')}
    del _L0_gnn_all

    def _L1_gnn_setup():
        import jax, jax.numpy as jnp
        import numpy as np
        N_NODES = 50000
        N_EDGES = 25000
        IN_DIM = 128
        OUT_DIM = 128
        key = jax.random.key(seed)
        ks = jax.random.split(key, 8)
        x = jax.random.normal(ks[0], (N_NODES, IN_DIM), dtype=jnp.float32)
        edge_index = jax.random.randint(ks[1], (2, N_EDGES), 0, N_NODES, dtype=jnp.int64)
        s_in = 1.0 / np.sqrt(IN_DIM)
        s_up = 1.0 / np.sqrt(2 * OUT_DIM)
        W_lin = jax.random.uniform(ks[2], (IN_DIM, OUT_DIM), jnp.float32, -s_in, s_in)
        b_lin = jax.random.uniform(ks[3], (OUT_DIM,), jnp.float32, -s_in, s_in)
        W_msg = jax.random.uniform(ks[4], (IN_DIM, OUT_DIM), jnp.float32, -s_in, s_in)
        b_msg = jax.random.uniform(ks[5], (OUT_DIM,), jnp.float32, -s_in, s_in)
        W_upd = jax.random.uniform(ks[6], (2 * OUT_DIM, OUT_DIM), jnp.float32, -s_up, s_up)
        b_upd = jax.random.uniform(ks[7], (OUT_DIM,), jnp.float32, -s_up, s_up)
        return {'x': x, 'edge_index': edge_index, 'W_lin': W_lin, 'b_lin': b_lin, 'W_msg': W_msg, 'b_msg': b_msg, 'W_upd': W_upd, 'b_upd': b_upd}
    _L1_gnn_all = _L1_gnn_setup()
    _L1_gnn_in = {k: v for k, v in _L1_gnn_all.items() if k in ('W_lin', 'b_lin', 'W_msg', 'b_msg', 'W_upd', 'b_upd')}
    del _L1_gnn_all

    def _L2_gnn_setup():
        import jax, jax.numpy as jnp
        import numpy as np
        LN_EPS = 1e-05

        def _layer_norm(x, g, b):
            mu = jnp.mean(x, axis=-1, keepdims=True)
            var = jnp.mean((x - mu) ** 2, axis=-1, keepdims=True)
            return (x - mu) * jax.lax.rsqrt(var + LN_EPS) * g + b
        key = jax.random.key(seed)
        ks = jax.random.split(key, 8)
        N, E = (50000, 25000)
        node_dim, edge_dim, hidden = (128, 128, 256)
        in_dim = node_dim + edge_dim
        s1 = 1.0 / np.sqrt(in_dim)
        s2 = 1.0 / np.sqrt(hidden)
        return {'node_feat': jax.random.normal(ks[0], (N, node_dim), dtype=jnp.float32), 'edge_attr': jax.random.normal(ks[1], (E, edge_dim), dtype=jnp.float32), 'edge_index': jax.random.randint(ks[2], (2, E), 0, N, dtype=jnp.int32), 'num_nodes': N, 'W1': jax.random.uniform(ks[3], (in_dim, hidden), jnp.float32, -s1, s1), 'b1': jax.random.uniform(ks[4], (hidden,), jnp.float32, -s1, s1), 'ln_g': jnp.ones((hidden,), jnp.float32), 'ln_b': jnp.zeros((hidden,), jnp.float32), 'W2': jax.random.uniform(ks[5], (hidden, node_dim), jnp.float32, -s2, s2), 'b2': jax.random.uniform(ks[6], (node_dim,), jnp.float32, -s2, s2)}
    _L2_gnn_all = _L2_gnn_setup()
    _L2_gnn_in = {k: v for k, v in _L2_gnn_all.items() if k in ('W1', 'b1', 'ln_g', 'ln_b', 'W2', 'b2')}
    del _L2_gnn_all

    def _L3_gnn_setup():
        import jax, jax.numpy as jnp
        import numpy as np
        N = 3125
        E = 50000
        D = 128
        TOTAL_RELS = 2 * 500 + 1
        LN_EPS = 1e-05

        def _xavier(key, shape):
            fan_in, fan_out = (shape[1], shape[0])
            lim = float(np.sqrt(6.0 / (fan_in + fan_out)))
            return jax.random.uniform(key, shape, jnp.float32, -lim, lim)

        def _layer(x, src, tgt, etype, rel_emb, W, gamma, beta, relu):
            nrm = jnp.sqrt(jnp.sum(rel_emb * rel_emb, axis=1, keepdims=True))
            rel = rel_emb / jnp.maximum(nrm, 1e-06)
            h_src = x[src]
            h_rel = rel[etype]
            dot = jnp.sum(h_src * h_rel, axis=1, keepdims=True)
            h_ref = h_src - 2.0 * dot * h_rel
            out = jax.ops.segment_sum(h_ref, tgt, num_segments=x.shape[0])
            deg = jax.ops.segment_sum(jnp.ones((tgt.shape[0],), x.dtype), tgt, num_segments=x.shape[0])
            out = out / jnp.maximum(deg, 1.0)[:, None]
            out = out @ W.T
            out = out + x
            mu = jnp.mean(out, axis=-1, keepdims=True)
            var = jnp.mean((out - mu) ** 2, axis=-1, keepdims=True)
            out = (out - mu) / jnp.sqrt(var + LN_EPS) * gamma + beta
            if relu:
                out = jax.nn.relu(out)
            return out
        key = jax.random.key(seed)
        ks = jax.random.split(key, 6)
        edge_index = jax.random.randint(ks[0], (2, E), 0, N, dtype=jnp.int64)
        edge_type = jax.random.randint(ks[1], (E,), 0, TOTAL_RELS, dtype=jnp.int64)
        x0 = _xavier(ks[2], (N, D))
        rel_emb = _xavier(ks[3], (TOTAL_RELS, D))
        W1 = _xavier(ks[4], (D, D))
        W2 = _xavier(ks[5], (D, D))
        ln1_g = jnp.ones((D,), jnp.float32)
        ln1_b = jnp.zeros((D,), jnp.float32)
        ln2_g = jnp.ones((D,), jnp.float32)
        ln2_b = jnp.zeros((D,), jnp.float32)
        return {'edge_index': edge_index, 'edge_type': edge_type, 'x0': x0, 'rel_emb': rel_emb, 'W1': W1, 'W2': W2, 'ln1_g': ln1_g, 'ln1_b': ln1_b, 'ln2_g': ln2_g, 'ln2_b': ln2_b}
    _L3_gnn_all = _L3_gnn_setup()
    _L3_gnn_in = {k: v for k, v in _L3_gnn_all.items() if k in ('rel_emb', 'W1', 'W2', 'ln1_g', 'ln1_b', 'ln2_g', 'ln2_b')}
    del _L3_gnn_all
    return {'x': x, 'src': src, 'dst': dst, 'edge_attr_128': edge_attr_128, 'edge_type_1001': edge_type_1001, 'edge_weight': edge_weight, 'L0_gnn_W_self': _L0_gnn_in['W_self'], 'L0_gnn_b_self': _L0_gnn_in['b_self'], 'L0_gnn_W_neigh': _L0_gnn_in['W_neigh'], 'L0_gnn_b_neigh': _L0_gnn_in['b_neigh'], 'L0_gnn_layer_bias': _L0_gnn_in['layer_bias'], 'L0_gnn_W_agg': _L0_gnn_in['W_agg'], 'L0_gnn_b_agg': _L0_gnn_in['b_agg'], 'L1_gnn_W_lin': _L1_gnn_in['W_lin'], 'L1_gnn_b_lin': _L1_gnn_in['b_lin'], 'L1_gnn_W_msg': _L1_gnn_in['W_msg'], 'L1_gnn_b_msg': _L1_gnn_in['b_msg'], 'L1_gnn_W_upd': _L1_gnn_in['W_upd'], 'L1_gnn_b_upd': _L1_gnn_in['b_upd'], 'L2_gnn_W1': _L2_gnn_in['W1'], 'L2_gnn_b1': _L2_gnn_in['b1'], 'L2_gnn_ln_g': _L2_gnn_in['ln_g'], 'L2_gnn_ln_b': _L2_gnn_in['ln_b'], 'L2_gnn_W2': _L2_gnn_in['W2'], 'L2_gnn_b2': _L2_gnn_in['b2'], 'L3_gnn_rel_emb': _L3_gnn_in['rel_emb'], 'L3_gnn_W1': _L3_gnn_in['W1'], 'L3_gnn_W2': _L3_gnn_in['W2'], 'L3_gnn_ln1_g': _L3_gnn_in['ln1_g'], 'L3_gnn_ln1_b': _L3_gnn_in['ln1_b'], 'L3_gnn_ln2_g': _L3_gnn_in['ln2_g'], 'L3_gnn_ln2_b': _L3_gnn_in['ln2_b']}

def reference(x, src, dst, edge_attr_128, edge_type_1001, edge_weight, L0_gnn_W_self, L0_gnn_b_self, L0_gnn_W_neigh, L0_gnn_b_neigh, L0_gnn_layer_bias, L0_gnn_W_agg, L0_gnn_b_agg, L1_gnn_W_lin, L1_gnn_b_lin, L1_gnn_W_msg, L1_gnn_b_msg, L1_gnn_W_upd, L1_gnn_b_upd, L2_gnn_W1, L2_gnn_b1, L2_gnn_ln_g, L2_gnn_ln_b, L2_gnn_W2, L2_gnn_b2, L3_gnn_rel_emb, L3_gnn_W1, L3_gnn_W2, L3_gnn_ln1_g, L3_gnn_ln1_b, L3_gnn_ln2_g, L3_gnn_ln2_b):
    import jax
    import jax.numpy as jnp

    def _L0_gnn_ref(user_embeddings, social_edge_index, social_edge_weights, W_self, b_self, W_neigh, b_neigh, layer_bias, W_agg, b_agg):
        import jax, jax.numpy as jnp
        import numpy as np
        N_NODES = 50000
        N_EDGES = 50000
        D = 128
        N_LAYERS = 2
        NEG_SLOPE = 0.2

        def _gcn_layer(x, src, dst, ew, Ws, bs, Wn, bn, bias):
            n = x.shape[0]
            msg = x[src] * ew[:, None]
            agg = jax.ops.segment_sum(msg, dst, num_segments=n)
            agg = agg + x
            cnt = jax.ops.segment_sum(jnp.ones_like(ew), dst, num_segments=n) + 1.0
            neigh = agg / cnt[:, None]
            out = x @ Ws.T + bs + neigh @ Wn.T + bn + bias
            return jnp.where(out > 0, out, NEG_SLOPE * out)
        src = social_edge_index[0]
        dst = social_edge_index[1]
        x = user_embeddings
        for l in range(N_LAYERS):
            x = _gcn_layer(x, src, dst, social_edge_weights, W_self[l], b_self[l], W_neigh[l], b_neigh[l], layer_bias[l])
        return x @ W_agg.T + b_agg

    def _L1_gnn_ref(x, edge_index, W_lin, b_lin, W_msg, b_msg, W_upd, b_upd):
        import jax, jax.numpy as jnp
        import numpy as np
        N_NODES = 50000
        N_EDGES = 25000
        IN_DIM = 128
        OUT_DIM = 128
        n_nodes = x.shape[0]
        row, col = (edge_index[0], edge_index[1])
        h_self = x @ W_lin + b_lin
        messages = x[col] @ W_msg + b_msg
        msg_sum = jax.ops.segment_sum(messages, row, num_segments=n_nodes)
        counts = jax.ops.segment_sum(jnp.ones((row.shape[0],), dtype=x.dtype), row, num_segments=n_nodes)
        h_agg = msg_sum / jnp.maximum(counts, 1.0)[:, None]
        h = jnp.concatenate([h_self, h_agg], axis=1) @ W_upd + b_upd
        return jax.nn.relu(h)

    def _L2_gnn_ref(node_feat, edge_attr, edge_index, num_nodes, W1, b1, ln_g, ln_b, W2, b2):
        import jax, jax.numpy as jnp
        import numpy as np
        LN_EPS = 1e-05

        def _layer_norm(x, g, b):
            mu = jnp.mean(x, axis=-1, keepdims=True)
            var = jnp.mean((x - mu) ** 2, axis=-1, keepdims=True)
            return (x - mu) * jax.lax.rsqrt(var + LN_EPS) * g + b
        dst = edge_index[1]
        aggregated = jax.ops.segment_sum(edge_attr, dst, num_segments=num_nodes)
        node_input = jnp.concatenate([node_feat, aggregated], axis=-1)
        h = node_input @ W1 + b1
        h = jax.nn.silu(_layer_norm(h, ln_g, ln_b))
        out = h @ W2 + b2
        return node_feat + out

    def _L3_gnn_ref(edge_index, edge_type, x0, rel_emb, W1, W2, ln1_g, ln1_b, ln2_g, ln2_b):
        import jax, jax.numpy as jnp
        import numpy as np
        N = 3125
        E = 50000
        D = 128
        TOTAL_RELS = 2 * 500 + 1
        LN_EPS = 1e-05

        def _xavier(key, shape):
            fan_in, fan_out = (shape[1], shape[0])
            lim = float(np.sqrt(6.0 / (fan_in + fan_out)))
            return jax.random.uniform(key, shape, jnp.float32, -lim, lim)

        def _layer(x, src, tgt, etype, rel_emb, W, gamma, beta, relu):
            nrm = jnp.sqrt(jnp.sum(rel_emb * rel_emb, axis=1, keepdims=True))
            rel = rel_emb / jnp.maximum(nrm, 1e-06)
            h_src = x[src]
            h_rel = rel[etype]
            dot = jnp.sum(h_src * h_rel, axis=1, keepdims=True)
            h_ref = h_src - 2.0 * dot * h_rel
            out = jax.ops.segment_sum(h_ref, tgt, num_segments=x.shape[0])
            deg = jax.ops.segment_sum(jnp.ones((tgt.shape[0],), x.dtype), tgt, num_segments=x.shape[0])
            out = out / jnp.maximum(deg, 1.0)[:, None]
            out = out @ W.T
            out = out + x
            mu = jnp.mean(out, axis=-1, keepdims=True)
            var = jnp.mean((out - mu) ** 2, axis=-1, keepdims=True)
            out = (out - mu) / jnp.sqrt(var + LN_EPS) * gamma + beta
            if relu:
                out = jax.nn.relu(out)
            return out
        src, tgt = (edge_index[0], edge_index[1])
        x = _layer(x0, src, tgt, edge_type, rel_emb, W1, ln1_g, ln1_b, relu=True)
        x = _layer(x, src, tgt, edge_type, rel_emb, W2, ln2_g, ln2_b, relu=False)
        return x
    edge_index = jnp.stack([src, dst])
    x = _layernorm(x + _L0_gnn_ref(x, edge_index, edge_weight, L0_gnn_W_self, L0_gnn_b_self, L0_gnn_W_neigh, L0_gnn_b_neigh, L0_gnn_layer_bias, L0_gnn_W_agg, L0_gnn_b_agg), axis=-1)
    x = _layernorm(x + _L1_gnn_ref(x, edge_index, L1_gnn_W_lin, L1_gnn_b_lin, L1_gnn_W_msg, L1_gnn_b_msg, L1_gnn_W_upd, L1_gnn_b_upd), axis=-1)
    x = _layernorm(x + _L2_gnn_ref(x, edge_attr_128, edge_index, 50000, L2_gnn_W1, L2_gnn_b1, L2_gnn_ln_g, L2_gnn_ln_b, L2_gnn_W2, L2_gnn_b2), axis=-1)
    x = _layernorm(x + _L3_gnn_ref(edge_index, edge_type_1001, x, L3_gnn_rel_emb, L3_gnn_W1, L3_gnn_W2, L3_gnn_ln1_g, L3_gnn_ln1_b, L3_gnn_ln2_g, L3_gnn_ln2_b), axis=-1)
    return x

_drawn_inputs = setup_inputs


def setup_inputs(seed=0):
    import zlib

    import numpy as np

    out = dict(_drawn_inputs(seed))
    spreads = {'L0_gnn_layer_bias': (0.0, 0.1),
     'L2_gnn_ln_g': (1.0, 0.2),
     'L2_gnn_ln_b': (0.0, 0.42),
     'L3_gnn_ln1_g': (1.0, 0.2),
     'L3_gnn_ln1_b': (0.0, 0.1),
     'L3_gnn_ln2_g': (1.0, 0.2),
     'L3_gnn_ln2_b': (0.0, 0.1)}
    factors = {'edge_weight': 4.156,
     'L1_gnn_b_lin': 3.53,
     'L1_gnn_b_msg': 4.384,
     'L2_gnn_b1': 3.381,
     'L2_gnn_b2': 2.898}
    for name, (base, spread) in spreads.items():
        noise = np.random.default_rng([zlib.crc32(name.encode()), seed]).standard_normal(out[name].shape)
        drawn = base * np.exp(spread * noise) if base else spread * noise
        out[name] = jnp.asarray(drawn.astype(out[name].dtype))
    for name, factor in factors.items():
        out[name] = (out[name] * factor).astype(out[name].dtype)
    return out
```

```python
from contextlib import ExitStack

import concourse.bass as bass
from concourse import mybir

F32 = mybir.dt.float32
BF16 = mybir.dt.bfloat16
I32 = mybir.dt.int32
ALU = mybir.AluOpType
ACT = mybir.ActivationFunctionType
AX_X = mybir.AxisListType.X

P = 128
D = 128
N = 50000
E = 25000
NREL = 1001
HID = 256
K = 4
ROWS = K * P
GROUPS = -(-N // ROWS)
STEPS = -(-E // ROWS)
LAST_NODES = (N - (GROUPS - 1) * ROWS) // K
LAST_EDGES = (E - (STEPS - 1) * ROWS) // K
TRASH = N
WIDE = 132
TABLE = 99 * ROWS
XROWS = GROUPS * ROWS
SLOPE = 0.2
EPS = 1e-5


def pipeline(engine, n, unroll, stages, tail=1):
    lag_max = max(lag for _, lag in stages)
    first = -(-(lag_max + 4) // unroll) * unroll
    end = (n - tail) // unroll * unroll

    def step(j, u):
        for stage, lag in stages:
            slot = (u - lag) % unroll
            q = j + (u - lag - slot) // unroll
            i = q * unroll + slot
            if not isinstance(i, int) or 0 <= i < n:
                stage(i, q, slot)

    for t in range(first):
        step(t // unroll, t % unroll)
    with engine.Fori(first // unroll, end // unroll) as j:
        for u in range(unroll):
            step(j, u)
    for t in range(end, n + lag_max):
        step(t // unroll, t % unroll)


def later(i, behind):
    return not isinstance(i, int) or i >= behind


def program(nc, t, out):
    ctx = ExitStack()
    with ctx:
        def sb(name, shape, dt=F32):
            return ctx.enter_context(nc.sbuf_tensor(name, shape, dt))

        def sem(name):
            return ctx.enter_context(nc.semaphore(name))

        def dram(name, shape, dt=F32):
            return nc.dram_tensor(name, shape, dt).ap()

        x1_d, xa_d, xb_d, xc_d, x5_d = (dram(f"nodes_{n}", (XROWS, D)) for n in ("l0", "a", "b", "c", "l3"))
        sum_d = {n: dram(f"sums_{n}", (TABLE, w)) for n, w in
                 (("l0a", WIDE), ("l0b", D), ("l1", WIDE), ("l2", D), ("l3a", D), ("l3b", D))}
        rel_d = dram("rel_unit", (NREL, D))
        rel_edge_d = dram("rel_of_edges", (STEPS * ROWS, D))

        ident = sb("ident", [P, P])
        zeros = sb("zeros", [P, 32 * WIDE])
        neg_half = sb("neg_half", [P, 4])
        pos_half = sb("pos_half", [P, 11])
        ones_bf = sb("ones_bf", [P, P], BF16)
        rev = sb("rev", [P, ROWS])
        rev_own = sb("rev_own", [P, K])
        trash = sb("trash", [P, K])
        w_self = sb("w_self", [P, 2, D])
        w_neigh = sb("w_neigh", [P, 2, D])
        w_agg = sb("w_agg", [P, D])
        w_linT = sb("w_linT", [P, D])
        w_msgT = sb("w_msgT", [P, D])
        w_upd = sb("w_upd", [P, 2, D])
        w_c1 = sb("w_c1", [P, D])
        w_c2 = sb("w_c2", [P, D])
        w_h = sb("w_h", [P, 2, HID])
        w_o = sb("w_o", [P, 2, D])
        w_r = sb("w_r", [P, 2, D])
        b_lin = sb("b_lin", [P, 1])
        b_msg = sb("b_msg", [P, 1])
        col3 = sb("col3", [P, 3])
        b_l0b = sb("b_l0b", [P, 1])
        b_below = sb("b_below", [P, 1])
        ln_g = sb("ln_g", [P, 2])
        ln_b = sb("ln_b", [P, 2])
        BL0, BAGG, BH, BO = 0, D, 2 * D, 2 * D + HID
        NB = BO + D
        brow = sb("brow", [1, 3, NB])
        bparts = sb("bparts", [1, 3, NB], BF16)
        bias3 = sb("bias3", [P, NB], BF16)
        brow_upd = sb("brow_upd", [1, D])
        bmrow = sb("bmrow", [1, 2, D])
        bm4 = sb("bm4", [4, D])
        g3 = sb("g3", [P, 2, D])
        b3 = sb("b3", [P, 2, D])
        rel_in = sb("rel_in", [91, 11, D])
        rel_sq = sb("rel_sq", [91, 11, D])
        rel_ss = sb("rel_ss", [91, 11])
        rel_nm = sb("rel_nm", [91, 11])
        eps4 = sb("eps4", [P, 4])

        src_i = sb("src_i", [P, STEPS, K], I32)
        dst_i = sb("dst_i", [P, STEPS, K], I32)
        type_i = sb("type_i", [P, STEPS, K], I32)
        weight = sb("weight", [P, STEPS, K])
        src_f = sb("src_f", [P, STEPS, K])
        dst_f = sb("dst_f", [P, STEPS, K])
        put_src = sb("put_src", [P, STEPS, K], I32)
        put_dst = sb("put_dst", [P, STEPS, K], I32)

        inv_l0 = sb("inv_l0", [P, GROUPS, K])
        inv_l3 = sb("inv_l3", [P, GROUPS, K])

        at_get = sb("at_get", [P, 2, K], I32)
        at_rel = sb("at_rel", [P, 2, K], I32)
        at_put = sb("at_put", [P, 2, K], I32)
        got = sb("got", [P, 2, K, D])
        rel = sb("rel", [P, 2, K, D])
        msg = sb("msg", [P, 2, K, WIDE])
        ids = sb("ids", [P, 2, ROWS], I32)
        same = sb("same", [P, 2, K, ROWS])
        merged = sb("merged", [P, 2, K, WIDE])
        hit = sb("hit", [P, ROWS])
        first4 = sb("first4", [P, 2, K])
        sel4 = sb("sel4", [P, 3, K])
        dot4 = sb("dot4", [P, 2, K])
        prod = sb("prod", [P, D])

        xin = sb("xin", [P, 4, K, D])
        xres = sb("xres", [P, 4, K, D])
        sums = sb("sums", [P, 4, K, WIDE])
        cnt4 = sb("cnt4", [P, 2, 2, K])
        neigh = sb("neigh", [P, 2, K, WIDE])
        xT = sb("xT", [P, 2, ROWS])
        nT = sb("nT", [P, 2, ROWS])
        fT = sb("fT", [4, 2, ROWS])
        x2T = sb("x2T", [P, 2, ROWS])
        above = sb("above", [P, 2, ROWS])
        below = sb("below", [P, 2, ROWS])
        res = sb("res", [P, 2, K, D])
        hid = sb("hid", [P, K, HID])
        hidT = sb("hidT", [P, 2, 2, ROWS])
        stat = sb("stat", [P, 3, K, 6])
        mv = sb("mv", [P, 3, 2, K, 2])
        rstd = sb("rstd", [P, 3, 2, K])
        vare = sb("vare", [P, 3, 2, K])
        aff = sb("aff", [P, 2, K, D])
        xout = sb("xout", [P, 4, K, D])

        ps = ctx.enter_context(nc.psum_tensor("ps", [P, 8, ROWS], F32))

        s_const = sem("s_const")
        s_cdve = sem("s_cdve")
        s_zero = {n: sem(f"s_zero_{n}") for n in sum_d}
        s_win = sem("s_win")
        s_rel_in = sem("s_rel_in")
        s_eload = sem("s_eload")
        s_ecast = sem("s_ecast")
        s_bpart = sem("s_bpart")
        s_brow = sem("s_brow")
        s_comb = sem("s_comb")
        s_combv = sem("s_combv")
        s_bm = sem("s_bm")
        s_relss = sem("s_relss")
        s_relnm = sem("s_relnm")
        s_relok = sem("s_relok")
        s_relst = sem("s_relst")
        pool_step = sem("pool_step")
        sp_step = sem("sp_step")
        pool_copied = sem("pool_copied")

        class Count:

            def __init__(self, semaphore, base):
                self.sem, self.base = semaphore, base

            def __call__(self, n):
                return self.sem, self.base + n

        def edge_totals(name):
            slots = [len(range(slot, STEPS, 2)) for slot in range(2)]
            gathered = {"l2": 0, "l3a": 128}.get(name, 64)
            kept = name in ("l2", "l3a", "l3b")
            return {
                "ids0": 16 * slots[0], "ids1": 16 * slots[1],
                "got0": gathered * slots[0], "got1": gathered * slots[1],
                "keep0": 16 * slots[0] * kept, "keep1": 16 * slots[1] * kept,
                "same": STEPS, "msg": STEPS,
                "merge": STEPS, "evac": STEPS,
                "index": (2 if name == "l3a" else 0 if name == "l2" else 1) * STEPS,
                "put": 64 * STEPS,
            }

        def node_totals(phase):
            slots = [len(range(slot, GROUPS, 4)) for slot in range(4)]
            loads = 3 if phase in ("d1", "d3b") else 2
            used = {"d0": "neigh tx tn xT nT mm act norm",
                    "d1": "neigh tx tn xT nT mm act x2 y res var rstd norm",
                    "d2a": "neigh tx tn xT nT mm res var rstd norm",
                    "d2b": "tx tn xT nT mm hst hrs hn th hT o res var rstd norm",
                    "d3a": "neigh tn nT mm res var rstd norm act",
                    "d3b": "neigh tn nT mm res var rstd o2 act norm"}[phase].split()
            made = {name: GROUPS for name in used}
            if phase == "d2a":
                made["xT"] = 2 * GROUPS
            for slot in range(4):
                made[f"in{slot}"] = 16 * loads * slots[slot]
                made[f"st{slot}"] = 16 * slots[slot]
            return made

        handles, reached = {}, {}

        def counts(kind, totals):
            made = {}
            for name, total in totals.items():
                key = f"{kind}_{name}"
                if key not in handles:
                    handles[key], reached[key] = sem(key), 0
                made[name] = Count(handles[key], reached[key])
                reached[key] += total
            return made

        edge_s = {name: counts("e", edge_totals(name)) for name in sum_d}
        node_s = {phase: counts("n", node_totals(phase)) for phase in ("d0", "d1", "d2a", "d2b", "d3a", "d3b")}

        SRC = {"l0a": t["x"], "l0b": x1_d, "l1": xa_d, "l3a": xc_d, "l3b": x5_d}
        BEFORE = {"l0b": "d0", "l1": "d1", "l3a": "d2b", "l3b": "d3a"}
        puts_before = {name: n * STEPS for n, name in enumerate(("l0a", "l0b", "l1", "l2", "l3a", "l3b"))}
        zero_jobs = []
        for n in ("l0a", "l0b", "l1", "l2", "l3a", "l3b"):
            w = sum_d[n].shape[1]
            r = 32 if w == WIDE else 33
            per = TABLE // P
            view = sum_d[n].rearrange("(p r) d -> p r d", p=P)
            done = 0
            while done < per:
                m = min(r, per - done)
                zero_jobs.append((n, view[:, done:done + m, :], zeros[:, 0:m * w].rearrange("p (r d) -> p r d", d=w)))
                done += m
        zero_count = {n: 16 * sum(job[0] == n for job in zero_jobs) for n in sum_d}

        def stores_done(engine, phase):
            for slot in range(4):
                engine.wait_ge(*node_s[phase][f"st{slot}"](16 * len(range(slot, GROUPS, 4))))

        small_loads = [
            (w_self, t["L0_gnn_W_self"].rearrange("l i o -> i l o")), (w_neigh, t["L0_gnn_W_neigh"].rearrange("l i o -> i l o")),
            (w_agg, t["L0_gnn_W_agg"]), (w_linT, t["L1_gnn_W_lin"]), (w_msgT, t["L1_gnn_W_msg"]),
            (w_upd, t["L1_gnn_W_upd"].rearrange("(h i) o -> i h o", i=D)),
            (w_h, t["L2_gnn_W1"].rearrange("(h i) o -> i h o", i=D)), (w_o, t["L2_gnn_W2"].rearrange("(h i) o -> i h o", i=D)),
            (w_r[:, 0, :], t["L3_gnn_W1"]), (w_r[:, 1, :], t["L3_gnn_W2"]),
            (b_lin, t["L1_gnn_b_lin"].rearrange("(p a) -> p a", a=1)), (b_msg, t["L1_gnn_b_msg"].rearrange("(p a) -> p a", a=1)),
            
            (g3[:, 0, :], t["L3_gnn_ln1_g"].partition_broadcast(P)), (g3[:, 1, :], t["L3_gnn_ln2_g"].partition_broadcast(P)),
            (b3[:, 0, :], t["L3_gnn_ln1_b"].partition_broadcast(P)), (b3[:, 1, :], t["L3_gnn_ln2_b"].partition_broadcast(P)),
            (brow_upd, t["L1_gnn_b_upd"].rearrange("(a n) -> a n", a=1)),
            (brow[:, 0, BAGG:BAGG + D], t["L0_gnn_b_agg"].rearrange("(a n) -> a n", a=1)),
            (brow[:, 0, BH:BH + HID], t["L2_gnn_b1"].rearrange("(a n) -> a n", a=1)),
            (brow[:, 0, BO:BO + D], t["L2_gnn_b2"].rearrange("(a n) -> a n", a=1)),
        ]
        for i, name in enumerate(("b_self", "b_neigh", "layer_bias")):
            b = t[f"L0_gnn_{name}"]
            small_loads.append((brow[:, i, BL0:BL0 + D], b[0:1, :]))
            small_loads.append((col3[:, i:i + 1], b[1, :].rearrange("(p a) -> p a", a=1)))
        for h in range(2):
            small_loads.append((ln_g[:, h:h + 1], t["L2_gnn_ln_g"][h * P:(h + 1) * P].rearrange("(p a) -> p a", a=1)))
            small_loads.append((ln_b[:, h:h + 1], t["L2_gnn_ln_b"][h * P:(h + 1) * P].rearrange("(p a) -> p a", a=1)))

        block = ctx.enter_context(nc.Block())

        @block.sync
        def _(sp):
            def held(semaphore, value):
                sp.wait_ge(semaphore, value)
                sp.sem_inc(sp_step, 1)

            full = (STEPS - 1) * ROWS
            sp.wait_ge(s_cdve, 1)
            for name, tile in (("src", src_i), ("dst", dst_i), ("edge_type_1001", type_i), ("edge_weight", weight)):
                v = t[name]
                sp.dma_start(tile[:, 0:STEPS - 1, :], v[0:full].rearrange("(s p k) -> p s k", p=P, k=K)).then_inc(s_eload, 16)
                sp.dma_start(tile[0:LAST_EDGES, STEPS - 1, :],
                             v[full:E].rearrange("(p k) -> p k", k=K)).then_inc(s_eload, 16)
            for tile, ap in small_loads:
                sp.dma_start(tile[tuple(slice(None) for _ in tile.shape)], ap).then_inc(s_win, 16)
            sp.dma_start(rel_in[:, :, :], t["L3_gnn_rel_emb"].rearrange("(p r) d -> p r d", r=11)).then_inc(s_rel_in, 16)
            sp.wait_ge(s_bpart, 1)
            for i in range(3):
                sp.dma_start(bias3[i:i + 1, :], bparts[0:1, i, :]).then_inc(s_brow, 16)
            sp.wait_ge(s_bm, 1)
            for i in range(2):
                sp.dma_start(bm4[i:i + 1, :], bmrow[0:1, i, :]).then_inc(s_brow, 16)
            sp.wait_ge(s_relok, 1)
            sp.dma_start(rel_d.rearrange("(p r) d -> p r d", r=11), rel_in[:, :, :]).then_inc(s_relst, 16)

            def edges(name):
                s = edge_s[name]
                nodes = t["src"] if name == "l1" else t["dst"]

                def ids_load(i, q, slot):
                    if later(i, 2):
                        held(*s["same"](i - 1))
                    if isinstance(i, int) and i == STEPS - 1:
                        src = nodes[full:E].rearrange("(a n) -> a n", a=1)[0, :].partition_broadcast(P)
                        sp.dma_start(ids[:, slot, 0:E - full], src).then_inc(s[f"ids{slot}"].sem, 16)
                        if name == "l2":
                            sp.wait_ge(*s["msg"](i - 1))
                            sp.dma_start(got[0:LAST_EDGES, slot, :, :],
                                         t["edge_attr_128"][full:E, :].rearrange("(p k) d -> p k d", k=K)).then_inc(s[f"keep{slot}"].sem, 16)
                        if name == "l3b":
                            sp.wait_ge(*s["msg"](i - 1))
                            sp.dma_start(rel[:, slot, :, :], rel_edge_d[full:full + ROWS, :].rearrange("(p k) d -> p k d", k=K))\
                              .then_inc(s[f"keep{slot}"].sem, 16)
                        return
                    sp.dma_start(ids[:, slot, :], nodes[bass.ds(i * ROWS, ROWS)].partition_broadcast(P)).then_inc(s[f"ids{slot}"].sem, 16)
                    if name == "l2":
                        if later(i, 2):
                            held(*s["msg"](i - 1))
                        sp.dma_start(got[:, slot, :, :],
                                     t["edge_attr_128"][bass.ds(i * ROWS, ROWS), :].rearrange("(p k) d -> p k d", k=K))\
                          .then_inc(s[f"keep{slot}"].sem, 16)
                    if name == "l3b":
                        if later(i, 2):
                            held(*s["msg"](i - 1))
                        sp.dma_start(rel[:, slot, :, :],
                                     rel_edge_d[bass.ds(i * ROWS, ROWS), :].rearrange("(p k) d -> p k d", k=K))\
                          .then_inc(s[f"keep{slot}"].sem, 16)

                def rel_keep(i, q, slot):
                    held(*s["msg"](i + 1))
                    sp.dma_start(rel_edge_d[bass.ds(i * ROWS, ROWS), :].rearrange("(p k) d -> p k d", k=K),
                                 rel[:, slot, :, :]).then_inc(s[f"keep{slot}"].sem, 16)

                if name == "l3b":
                    for slot in range(2):
                        sp.wait_ge(*edge_s["l3a"][f"keep{slot}"](16 * len(range(slot, STEPS, 2))))
                pipeline(sp, STEPS, 2, [(ids_load, 0)] + ([(rel_keep, 1)] if name == "l3a" else []))

            def nodes(phase, inputs, free, ready, dest, sums_name):
                s = node_s[phase]
                w = sum_d[sums_name].shape[1]
                sp.wait_ge(*edge_s[sums_name]["put"](64 * STEPS))
                if phase == "d2b":
                    stores_done(sp, "d2a")

                def load(i, q, slot):
                    if later(i, 4):
                        for f in free:
                            held(*s[f](i - 3))
                    last = isinstance(i, int) and i == GROUPS - 1
                    for buf, table, exact in inputs:
                        p = LAST_NODES if last and exact else P
                        rows = bass.ds(i * ROWS, p * K)
                        sp.dma_start(buf[0:p, slot, :, :], table[rows, :].rearrange("(p k) d -> p k d", k=K))\
                          .then_inc(s[f"in{slot}"].sem, 16)
                    sp.dma_start(sums[:, slot, :, 0:w],
                                 sum_d[sums_name][bass.ds(i * ROWS, ROWS), :].rearrange("(p k) d -> p k d", k=K))\
                      .then_inc(s[f"in{slot}"].sem, 16)

                def store(i, q, slot):
                    held(*s[ready](i + 1))
                    last = isinstance(i, int) and i == GROUPS - 1
                    p = LAST_NODES if last and dest is out else P
                    sp.dma_start(dest[bass.ds(i * ROWS, p * K), :].rearrange("(p k) d -> p k d", k=K),
                                 xout[0:p, slot, :, :]).then_inc(s[f"st{slot}"].sem, 16)

                pipeline(sp, GROUPS, 4, [(load, 0), (store, {"d0": 2, "d1": 3, "d2a": 3, "d2b": 3, "d3a": 3, "d3b": 3}[phase])])

            edges("l0a")
            nodes("d0", [(xin, t["x"], True)], ["tx", "neigh"], "norm", x1_d, "l0a")
            edges("l0b")
            nodes("d1", [(xin, x1_d, False), (xres, t["x"], True)], ["tx", "res"], "norm", xa_d, "l0b")
            edges("l1")
            nodes("d2a", [(xin, xa_d, False)], ["tx", "res"], "norm", xb_d, "l1")
            edges("l2")
            nodes("d2b", [(xin, xb_d, False)], ["tx", "tn", "res"], "norm", xc_d, "l2")
            edges("l3a")
            nodes("d3a", [(xin, xc_d, False)], ["res"], "act", x5_d, "l3a")
            edges("l3b")
            nodes("d3b", [(xin, x5_d, False), (xres, xc_d, False)], ["res", "o2"], "norm", out, "l3b")
            stores_done(sp, "d3b")

        @block.gpsimd
        def _(pool):
            def held(semaphore, value):
                pool.wait_ge(semaphore, value)
                pool.sem_inc(pool_step, 1)

            pool.memset(ident[:, :], 0.0).then_inc(s_const, 1)
            pool.wait_ge(s_const, 1)
            pool.affine_select(out=ident[:, :], in_=ident[:, :], compare_op=ALU.not_equal, fill=1.0, base=0,
                               pattern=[[-1, P]], channel_multiplier=1).then_inc(s_const, 1)
            pool.iota(rev[:, :], pattern=[[-1, ROWS]], base=ROWS, channel_multiplier=0,
                      allow_small_or_imprecise_dtypes=True).then_inc(s_const, 1)
            pool.iota(rev_own[:, :], pattern=[[-1, K]], base=ROWS, channel_multiplier=-K,
                      allow_small_or_imprecise_dtypes=True).then_inc(s_const, 1)
            pool.iota(trash[:, :], pattern=[[1, K]], base=TRASH, channel_multiplier=K,
                      allow_small_or_imprecise_dtypes=True).then_inc(s_const, 1)
            pool.memset(neg_half[:, :], -0.5).then_inc(s_const, 1)
            pool.memset(pos_half[:, :], 0.5).then_inc(s_const, 1)
            pool.wait_ge(s_relss, 1)
            pool.wait_ge(s_const, 7)
            pool.tensor_tensor(rel_nm[:, :], rel_ss[:, :], pos_half[0:91, :], ALU.pow).then_inc(s_relnm, 1)
            pool.wait_ge(s_eload, 128)

            def edges(name):
                s = edge_s[name]
                get_i = dst_i if name == "l1" else src_i
                put_i = put_src if name == "l1" else put_dst
                w = sum_d[name].shape[1]

                def get(i, q, slot):
                    if name == "l2":
                        return
                    if later(i, 2):
                        held(*s["msg"](i - 1))
                        if name == "l3a":
                            held(*s[f"keep{slot}"](16 * q))
                    pool.tensor_copy(at_get[:, slot, :], get_i[:, bass.ds(i, 1), :].rearrange("p a k -> p (a k)"))\
                        .then_inc(s["index"].sem, 1)
                    if name == "l3a":
                        pool.tensor_copy(at_rel[:, slot, :], type_i[:, bass.ds(i, 1), :].rearrange("p a k -> p (a k)"))\
                            .then_inc(s["index"].sem, 1)
                    held(*s["index"]((i + 1) * 2 if name == "l3a" else i + 1))
                    for k in range(K):
                        pool.indirect_dma_start(out=got[:, slot, k, :], out_offset=None, in_=SRC[name],
                                                in_offset=bass.IndirectOffsetOnAxis(ap=at_get[:, slot, k:k + 1], axis=0))\
                            .then_inc(s[f"got{slot}"].sem, 16)
                    if name == "l3a":
                        for k in range(K):
                            pool.indirect_dma_start(out=rel[:, slot, k, :], out_offset=None, in_=rel_d,
                                                    in_offset=bass.IndirectOffsetOnAxis(ap=at_rel[:, slot, k:k + 1], axis=0))\
                                .then_inc(s[f"got{slot}"].sem, 16)

                def put(i, q, slot):
                    held(*s["evac"](i + 1))
                    if later(i, 1):
                        held(*s["put"](64 * i))
                    pool.tensor_copy(at_put[:, slot, :], put_i[:, bass.ds(i, 1), :].rearrange("p a k -> p (a k)"))\
                        .then_inc(pool_copied, 1)
                    held(pool_copied, puts_before[name] + i + 1)
                    for k in range(K):
                        pool.indirect_dma_start(out=sum_d[name],
                                                out_offset=bass.IndirectOffsetOnAxis(ap=at_put[:, slot, k:k + 1], axis=0),
                                                in_=merged[:, slot, k, 0:w], in_offset=None, compute_op=ALU.add)\
                            .then_inc(s["put"].sem, 16)

                if name in BEFORE:
                    stores_done(pool, BEFORE[name])
                if name == "l3a":
                    pool.wait_ge(s_relst, 16)
                pool.wait_ge(s_zero[name], zero_count[name])
                pipeline(pool, STEPS, 2, [(get, 0), (put, 1)])

            def powers(phase, pairs, joins=[]):
                s = node_s[phase]

                def power(n, ready, done):
                    def stage(i, q, slot):
                        held(*s[ready](i + 1))
                        pool.tensor_tensor(rstd[:, n, slot % 2, :], vare[:, n, slot % 2, :], neg_half[:, :], ALU.pow)\
                            .then_inc(s[done].sem, 1)
                    return stage

                pipeline(pool, GROUPS, 4, joins + [(power(n, ready, done), lag) for n, ready, done, lag in pairs])

            def join(phase):
                s = node_s[phase]

                def stage(i, q, slot):
                    held(*s["act"](i + 1))
                    if phase == "d0":
                        if later(i, 4):
                            held(*s[f"st{slot}"](16 * q))
                        pool.tensor_tensor(xout[:, slot, :, :].rearrange("p k d -> p (k d)"), above[:, slot % 2, :],
                                           below[:, slot % 2, :], ALU.subtract).then_inc(s["norm"].sem, 1)
                    else:
                        if later(i, 2):
                            held(*s["y"](i - 1))
                        pool.tensor_tensor(x2T[:, slot % 2, :], above[:, slot % 2, :], below[:, slot % 2, :], ALU.subtract)\
                            .then_inc(s["x2"].sem, 1)
                return stage

            edges("l0a")
            pipeline(pool, GROUPS, 4, [(join("d0"), 0)])
            edges("l0b")
            powers("d1", [(0, "var", "rstd", 1)], [(join("d1"), 0)])
            edges("l1")
            powers("d2a", [(0, "var", "rstd", 0)])
            edges("l2")
            powers("d2b", [(1, "hst", "hrs", 0), (0, "var", "rstd", 2)])
            edges("l3a")
            powers("d3a", [(0, "var", "rstd", 0)])
            edges("l3b")
            powers("d3b", [(0, "var", "rstd", 0), (2, "o2", "act", 1)])

        @block.vector
        def _(dve):
            dve.memset(src_i[:, STEPS - 1, :], 0)
            dve.memset(dst_i[:, STEPS - 1, :], 0)
            dve.memset(type_i[:, STEPS - 1, :], 0)
            dve.memset(weight[:, STEPS - 1, :], 0.0)
            dve.memset(bias3[:, :], 0.0)
            dve.memset(bm4[:, :], 0.0)
            dve.memset(zeros[:, :], 0.0)
            dve.memset(brow[:, :, :], 0.0)
            dve.drain().then_inc(s_cdve, 1)
            dve.memset(ones_bf[:, :], 1.0)
            dve.memset(msg[:, :, :, D:WIDE], 0.0)
            dve.memset(xin[:, :, :, :], 0.0)
            dve.memset(xres[:, :, :, :], 0.0)
            dve.memset(neigh[:, :, :, D:WIDE], 0.0)
            dve.drain()
            dve.memset(msg[:, :, :, D:D + 1], 1.0)
            dve.memset(neigh[:, :, :, D + 1:D + 2], 1.0)
            dve.drain().then_inc(s_cdve, 1)

            dve.wait_ge(s_win, 16 * len(small_loads))
            dve.tensor_tensor(brow[:, 0, :], brow[:, 0, :], brow[:, 1, :], ALU.add)
            dve.tensor_tensor(b_l0b[:, :], col3[:, 0:1], col3[:, 1:2], ALU.add)
            dve.drain()
            dve.tensor_tensor(brow[:, 0, :], brow[:, 0, :], brow[:, 2, :], ALU.add)
            dve.tensor_tensor(b_l0b[:, :], b_l0b[:, :], col3[:, 2:3], ALU.add)
            dve.drain()
            dve.tensor_scalar(b_below[:, :], b_l0b[:, :], -SLOPE, None, ALU.mult)
            for i in range(3):
                dve.tensor_copy(bparts[:, i, :], brow[:, i % 2, :])
                dve.drain()
                if i < 2:
                    dve.tensor_tensor(brow[:, (i + 1) % 2, :], brow[:, i % 2, :], bparts[:, i, :], ALU.subtract)
                    dve.drain()
            dve.drain().then_inc(s_bpart, 1)

            dve.wait_ge(s_eload, 128)
            dve.tensor_copy(src_f[:, :, :], src_i[:, :, :])
            dve.tensor_copy(dst_f[:, :, :], dst_i[:, :, :])
            dve.drain()

            dve.wait_ge(s_rel_in, 16)
            dve.tensor_tensor(rel_sq[:, :, :], rel_in[:, :, :], rel_in[:, :, :], ALU.mult)
            dve.drain()
            dve.reduce_sum(rel_ss[:, :], rel_sq[:, :, :], axis=AX_X).then_inc(s_relss, 1)
            dve.wait_ge(s_relnm, 1)
            dve.tensor_scalar(rel_ss[:, :], rel_nm[:, :], 1e-6, None, ALU.max)
            dve.drain()
            dve.reciprocal(rel_nm[:, :], rel_ss[:, :])
            dve.drain()
            dve.tensor_tensor(rel_in[:, :, :], rel_in[:, :, :],
                              rel_nm[:, :].rearrange("p (r a) -> p r a", a=1).to_broadcast([91, 11, D]), ALU.mult)\
               .then_inc(s_relok, 1)

            dve.wait_ge(s_comb, 1)
            dve.tensor_copy(w_c1[:, :], ps[:, 0, 0:D])
            dve.tensor_copy(w_c2[:, :], ps[:, 1, 0:D])
            dve.tensor_tensor(bmrow[0:1, 1, :], ps[0:1, 2, 0:D], brow_upd[:, :], ALU.add)
            dve.tensor_copy(bmrow[0:1, 0, :], ps[0:1, 3, 0:D])
            dve.drain().then_inc(s_bm, 1)
            dve.wait_ge(s_const, 7)

            def edges(name):
                s = edge_s[name]
                node_f = src_f if name == "l1" else dst_f
                put_i = put_src if name == "l1" else put_dst
                index = name in ("l0a", "l1")
                gathered = {"l2": 0, "l3a": 128}.get(name, 64)

                def compare(i, q, slot):
                    dve.wait_ge(*s[f"ids{slot}"](16 * (q + 1)))
                    if later(i, 2):
                        dve.wait_ge(*s["merge"](i - 1))
                    if isinstance(i, int) and i == STEPS - 1:
                        dve.memset(ids[:, slot, E - i * ROWS:ROWS], -1)
                        dve.drain()
                    for k in range(K):
                        dve.tensor_scalar(same[:, slot, k, :], ids[:, slot, :],
                                          node_f[:, bass.ds(i, 1), k:k + 1].rearrange("p a k -> p (a k)"), None, ALU.is_equal)
                    dve.drain().then_inc(s["same"].sem, 1)
                    if not index:
                        return
                    for k in range(K):
                        dve.tensor_tensor_reduce(out=hit[:, :], in0=same[:, slot, k, :], in1=rev[:, :], scale=1.0, scalar=0.0,
                                                 op0=ALU.mult, op1=ALU.max, accum_out=first4[:, slot, k:k + 1])
                        dve.drain()
                    dve.tensor_tensor(sel4[:, 0, :], first4[:, slot, :], rev_own[:, :], ALU.is_equal)
                    dve.tensor_tensor(sel4[:, 1, :], node_f[:, bass.ds(i, 1), :].rearrange("p a k -> p (a k)"), trash[:, :], ALU.subtract)
                    dve.drain()
                    dve.tensor_tensor(sel4[:, 2, :], sel4[:, 0, :], sel4[:, 1, :], ALU.mult)
                    dve.drain()
                    dve.tensor_tensor(put_i[:, bass.ds(i, 1), :].rearrange("p a k -> p (a k)"), sel4[:, 2, :], trash[:, :], ALU.add)
                    dve.drain()

                def message(i, q, slot):
                    if name != "l2":
                        dve.wait_ge(*s[f"got{slot}"](gathered * (q + 1)))
                    if name in ("l2", "l3b"):
                        dve.wait_ge(*s[f"keep{slot}"](16 * (q + 1)))
                    if later(i, 2):
                        dve.wait_ge(*s["merge"](i - 1))
                    if name in ("l0a", "l0b"):
                        for k in range(K):
                            dve.tensor_scalar(msg[:, slot, k, 0:D], got[:, slot, k, :],
                                              weight[:, bass.ds(i, 1), k:k + 1].rearrange("p a k -> p (a k)"), None, ALU.mult)
                    elif name in ("l1", "l2"):
                        dve.tensor_copy(msg[:, slot, :, 0:D], got[:, slot, :, :])
                    else:
                        for k in range(K):
                            dve.tensor_tensor_reduce(out=prod[:, :], in0=got[:, slot, k, :], in1=rel[:, slot, k, :], scale=-2.0,
                                                     scalar=0.0, op0=ALU.mult, op1=ALU.add, accum_out=dot4[:, slot, k:k + 1])
                            dve.drain()
                        for k in range(K):
                            dve.scalar_tensor_tensor(out=msg[:, slot, k, 0:D], in0=rel[:, slot, k, :], scalar=dot4[:, slot, k:k + 1],
                                                     in1=got[:, slot, k, :], op0=ALU.mult, op1=ALU.add)
                    dve.drain().then_inc(s["msg"].sem, 1)

                pipeline(dve, STEPS, 2, [(compare, 0), (message, 0)])

            def row_stats(s, i, n, slot, rows, ready):
                for k in range(K):
                    dve.bn_stats(stat[:, n, k, :], rows[:, k, :])
                dve.drain()
                for k in range(K):
                    dve.bn_aggr(mv[:, n, slot % 2, k, :], stat[:, n, k, :])
                dve.drain()
                dve.tensor_scalar(vare[:, n, slot % 2, :], mv[:, n, slot % 2, :, 1:2].rearrange("p k a -> p (k a)"), EPS, None, ALU.add)\
                   .then_inc(s[ready].sem, 1)

            def loaded(s, q, slot, count):
                dve.wait_ge(*s[f"in{slot}"](16 * count * (q + 1)))

            def out_free(s, i, q, slot):
                if later(i, 4):
                    dve.wait_ge(*s[f"st{slot}"](16 * q))

            def wide(v, k=K):
                return v.rearrange("p (k a) -> p k a", a=1).to_broadcast([P, k, D])

            def copy_nT(s):
                def stage(i, q, slot):
                    dve.wait_ge(*s["tn"](i + 1))
                    if later(i, 2):
                        dve.wait_ge(*s["mm"](i - 1))
                    dve.tensor_copy(nT[:, slot % 2, :], ps[:, 2 + slot % 2, :]).then_inc(s["nT"].sem, 1)
                return stage

            def norm(s):
                def stage(i, q, slot):
                    dve.wait_ge(*s["rstd"](i + 1))
                    out_free(s, i, q, slot)
                    for k in range(K):
                        dve.tensor_scalar(xout[:, slot, k, :], res[:, slot % 2, k, :], mv[:, 0, slot % 2, k, 0:1],
                                          rstd[:, 0, slot % 2, k:k + 1], ALU.subtract, ALU.mult)
                    dve.drain().then_inc(s["norm"].sem, 1)
                return stage

            def d0():
                s = node_s["d0"]

                def average(i, q, slot):
                    loaded(s, q, slot, 2)
                    if later(i, 2):
                        dve.wait_ge(*s["tn"](i - 1))
                    c = cnt4[:, slot % 2, :, :]
                    count = sums[:, slot, :, D:D + 1].rearrange("p k a -> p (k a)")
                    dve.tensor_scalar(c[:, 0, :], count, 1.0, None, ALU.add)
                    dve.tensor_scalar(c[:, 1, :], count, 1.0, None, ALU.max)
                    dve.tensor_tensor(neigh[:, slot % 2, :, 0:D], sums[:, slot, :, 0:D], xin[:, slot, :, :], ALU.add)
                    dve.drain()
                    dve.reciprocal(inv_l0[:, bass.ds(i, 1), :].rearrange("p a k -> p (a k)"), c[:, 0, :])
                    dve.reciprocal(inv_l3[:, bass.ds(i, 1), :].rearrange("p a k -> p (a k)"), c[:, 1, :])
                    dve.drain()
                    dve.tensor_tensor(neigh[:, slot % 2, :, 0:D], neigh[:, slot % 2, :, 0:D],
                                      inv_l0[:, bass.ds(i, 1), :].rearrange("p a k -> p k a").to_broadcast([P, K, D]), ALU.mult)\
                       .then_inc(s["neigh"].sem, 1)

                pipeline(dve, GROUPS, 4, [(average, 0), (copy_nT(s), 1)])

            def d1():
                s = node_s["d1"]

                def average(i, q, slot):
                    loaded(s, q, slot, 3)
                    if later(i, 2):
                        dve.wait_ge(*s["tn"](i - 1))
                    dve.tensor_tensor(neigh[:, slot % 2, :, 0:D], sums[:, slot, :, 0:D], xin[:, slot, :, :], ALU.add)
                    dve.drain()
                    dve.tensor_tensor(neigh[:, slot % 2, :, 0:D], neigh[:, slot % 2, :, 0:D],
                                      inv_l0[:, bass.ds(i, 1), :].rearrange("p a k -> p k a").to_broadcast([P, K, D]), ALU.mult)\
                       .then_inc(s["neigh"].sem, 1)

                def residual(i, q, slot):
                    dve.wait_ge(*s["y"](i + 1))
                    r = res[:, slot % 2, :, :]
                    dve.tensor_tensor(r, ps[:, 6 + slot % 2, :].rearrange("p (k d) -> p k d", k=K), xres[:, slot, :, :], ALU.add)
                    dve.drain().then_inc(s["res"].sem, 1)
                    row_stats(s, i, 0, slot, r, "var")

                pipeline(dve, GROUPS, 4, [(average, 0), (copy_nT(s), 1), (residual, 2), (norm(s), 3)])

            def d2a():
                s = node_s["d2a"]

                def average(i, q, slot):
                    loaded(s, q, slot, 2)
                    if later(i, 2):
                        dve.wait_ge(*s["tn"](i - 1))
                    c = cnt4[:, slot % 2, :, :]
                    count = sums[:, slot, :, D:D + 1]
                    dve.tensor_scalar(c[:, 0, :], count.rearrange("p k a -> p (k a)"), 1.0, None, ALU.max)
                    dve.tensor_scalar(neigh[:, slot % 2, :, D:D + 1], count, 1.0, None, ALU.min)
                    dve.drain()
                    dve.reciprocal(c[:, 1, :], c[:, 0, :])
                    dve.drain()
                    dve.tensor_tensor(neigh[:, slot % 2, :, 0:D], sums[:, slot, :, 0:D], wide(c[:, 1, :]), ALU.mult)\
                       .then_inc(s["neigh"].sem, 1)

                def residual(i, q, slot):
                    dve.wait_ge(*s["mm"](i + 1))
                    r = res[:, slot % 2, :, :]
                    dve.scalar_tensor_tensor(out=r, in0=ps[:, 4 + slot % 2, :].rearrange("p (k d) -> p k d", k=K), scalar=0.0,
                                             in1=xin[:, slot, :, :], op0=ALU.max, op1=ALU.add)
                    dve.drain().then_inc(s["res"].sem, 1)
                    row_stats(s, i, 0, slot, r, "var")

                pipeline(dve, GROUPS, 4, [(average, 0), (copy_nT(s), 1), (residual, 2), (norm(s), 3)])

            def d2b():
                s = node_s["d2b"]

                def copy_sums(i, q, slot):
                    dve.wait_ge(*s["tn"](i + 1))
                    if later(i, 2):
                        dve.wait_ge(*s["mm"](i - 1))
                    dve.tensor_copy(nT[:, slot % 2, :], ps[:, 1, :]).then_inc(s["nT"].sem, 1)

                hrows = ps[:, 2:4, :].rearrange("p b (j d) -> p (b j) d", j=2)

                def hidden_stats(i, q, slot):
                    dve.wait_ge(*s["mm"](i + 1))
                    row_stats(s, i, 1, slot, hrows, "hst")

                def hidden_norm(i, q, slot):
                    dve.wait_ge(*s["hrs"](i + 1))
                    if later(i, 1):
                        dve.wait_ge(*s["th"](i))
                    for k in range(K):
                        dve.tensor_scalar(hid[:, k, :], hrows[:, k, :], mv[:, 1, slot % 2, k, 0:1],
                                          rstd[:, 1, slot % 2, k:k + 1], ALU.subtract, ALU.mult)
                    dve.drain().then_inc(s["hn"].sem, 1)

                def residual(i, q, slot):
                    dve.wait_ge(*s["o"](i + 1))
                    r = res[:, slot % 2, :, :]
                    dve.scalar_tensor_tensor(out=r, in0=xin[:, slot, :, :], scalar=2.0,
                                             in1=ps[:, 6 + slot % 2, :].rearrange("p (k d) -> p k d", k=K), op0=ALU.mult, op1=ALU.add)
                    dve.drain().then_inc(s["res"].sem, 1)
                    row_stats(s, i, 0, slot, r, "var")

                pipeline(dve, GROUPS, 4, [(copy_sums, 0), (norm(s), 3), (hidden_stats, 0), (residual, 2), (hidden_norm, 0)])

            def d3(phase, layer):
                s = node_s[phase]
                inputs = 3 if layer else 2

                def average(i, q, slot):
                    loaded(s, q, slot, inputs)
                    if later(i, 2):
                        dve.wait_ge(*s["tn"](i - 1))
                    dve.tensor_tensor(neigh[:, slot % 2, :, 0:D], sums[:, slot, :, 0:D],
                                      inv_l3[:, bass.ds(i, 1), :].rearrange("p a k -> p k a").to_broadcast([P, K, D]), ALU.mult)\
                       .then_inc(s["neigh"].sem, 1)

                def residual(i, q, slot):
                    dve.wait_ge(*s["mm"](i + 1))
                    r = res[:, slot % 2, :, :]
                    dve.tensor_tensor(r, ps[:, 4 + slot % 2, :].rearrange("p (k d) -> p k d", k=K), xin[:, slot, :, :], ALU.add)
                    dve.drain().then_inc(s["res"].sem, 1)
                    row_stats(s, i, 0, slot, r, "var")

                def affine(i, q, slot):
                    dve.wait_ge(*s["rstd"](i + 1))
                    if not layer and later(i, 2):
                        dve.wait_ge(*s["act"](i - 1))
                    a = aff[:, slot % 2, :, :]
                    for k in range(K):
                        dve.scalar_tensor_tensor(out=a[:, k, :], in0=res[:, slot % 2, k, :], scalar=mv[:, 0, slot % 2, k, 0:1],
                                                 in1=g3[:, layer, :], op0=ALU.subtract, op1=ALU.mult)
                    dve.drain()
                    for k in range(K):
                        dve.scalar_tensor_tensor(out=a[:, k, :], in0=a[:, k, :], scalar=rstd[:, 0, slot % 2, k:k + 1],
                                                 in1=b3[:, layer, :], op0=ALU.mult, op1=ALU.add)
                    if not layer:
                        dve.drain().then_inc(s["norm"].sem, 1)
                        return
                    dve.drain()
                    dve.tensor_tensor(a, a, xres[:, slot, :, :], ALU.add)
                    dve.drain()
                    row_stats(s, i, 2, slot, a, "o2")

                def last_norm(i, q, slot):
                    dve.wait_ge(*s["act"](i + 1))
                    out_free(s, i, q, slot)
                    for k in range(K):
                        dve.tensor_scalar(xout[:, slot, k, :], aff[:, slot % 2, k, :], mv[:, 2, slot % 2, k, 0:1],
                                          rstd[:, 2, slot % 2, k:k + 1], ALU.subtract, ALU.mult)
                    dve.drain().then_inc(s["norm"].sem, 1)

                stages = [(average, 0), (residual, 1), (affine, 2)]
                pipeline(dve, GROUPS, 4, stages + ([(last_norm, 3)] if layer else []))

            edges("l0a")
            d0()
            edges("l0b")
            d1()
            edges("l1")
            d2a()
            edges("l2")
            d2b()
            edges("l3a")
            d3("d3a", 0)
            edges("l3b")
            d3("d3b", 1)

        @block.scalar
        def _(act):
            act.wait_ge(s_cdve, 1)
            for n, dst, src in zero_jobs:
                act.dma_start(dst, src).then_inc(s_zero[n], 16)

            def edges(name):
                s = edge_s[name]
                w = sum_d[name].shape[1]

                def evacuate(i, q, slot):
                    act.wait_ge(*s["merge"](i + 1))
                    if later(i, 2):
                        act.wait_ge(*s["put"](64 * (i - 1)))
                    act.activation(merged[:, slot, :, 0:w],
                                   ps[:, 2 * slot:2 * slot + 2, :].rearrange("p b (j d) -> p (b j) d", j=2)[:, :, 0:w],
                                   ACT.Copy).then_inc(s["evac"].sem, 1)

                pipeline(act, STEPS, 2, [(evacuate, 0)])

            def copy_xT(s, bank, wide):
                def stage(i, q, slot):
                    act.wait_ge(*s["tx"](i + 1))
                    if later(i, 2):
                        act.wait_ge(*s["mm"](i - 1))
                    act.activation(xT[:, slot % 2, :], ps[:, bank + (slot % 2 if wide else 0), :], ACT.Copy).then_inc(s["xT"].sem, 1)
                return stage

            def d0():
                s = node_s["d0"]

                def leaky(i, q, slot):
                    act.wait_ge(*s["mm"](i + 1))
                    if later(i, 2):
                        act.wait_ge(*s["norm"](i - 1))
                    act.activation(above[:, slot % 2, :], ps[:, 4 + slot % 2, :], ACT.Relu)
                    act.activation(below[:, slot % 2, :], ps[:, 4 + slot % 2, :], ACT.Relu, scale=-SLOPE).then_inc(s["act"].sem, 1)

                pipeline(act, GROUPS, 4, [(copy_xT(s, 0, True), 0), (leaky, 1)])

            def d1():
                s = node_s["d1"]

                def leaky(i, q, slot):
                    act.wait_ge(*s["mm"](i + 1))
                    if later(i, 2):
                        act.wait_ge(*s["x2"](i - 1))
                    act.activation(above[:, slot % 2, :], ps[:, 4 + slot % 2, :], ACT.Relu, bias=b_l0b[:, :])
                    act.activation(below[:, slot % 2, :], ps[:, 4 + slot % 2, :], ACT.Relu, bias=b_below[:, :], scale=-SLOPE)\
                       .then_inc(s["act"].sem, 1)

                pipeline(act, GROUPS, 4, [(copy_xT(s, 0, True), 0), (leaky, 1)])

            def d2a():
                s = node_s["d2a"]

                def copy_fT(i, q, slot):
                    act.wait_ge(*s["tn"](i + 1))
                    if later(i, 2):
                        act.wait_ge(*s["mm"](i - 1))
                    act.activation(fT[:, slot % 2, :], ps[0:4, 6 + slot % 2, :], ACT.Copy).then_inc(s["xT"].sem, 1)

                def copy_x(i, q, slot):
                    act.wait_ge(*s["tx"](i + 1))
                    if later(i, 2):
                        act.wait_ge(*s["mm"](i - 1))
                    act.activation(xT[:, slot % 2, :], ps[:, slot % 2, :], ACT.Copy).then_inc(s["xT"].sem, 1)

                pipeline(act, GROUPS, 4, [(copy_x, 0), (copy_fT, 0)])

            def d2b():
                s = node_s["d2b"]

                def silu(i, q, slot):
                    act.wait_ge(*s["th"](i + 1))
                    if later(i, 2):
                        act.wait_ge(*s["o"](i - 1))
                    for h in range(2):
                        last = act.activation(hidT[:, slot % 2, h, :], ps[:, 4 + h, :], ACT.Silu, bias=ln_b[:, h:h + 1], scale=ln_g[:, h:h + 1])
                    last.then_inc(s["hT"].sem, 1)

                pipeline(act, GROUPS, 4, [(copy_xT(s, 0, False), 0), (silu, 1)])

            def d3(phase, layer):
                s = node_s[phase]

                def copy_n(i, q, slot):
                    act.wait_ge(*s["tn"](i + 1))
                    if later(i, 2):
                        act.wait_ge(*s["mm"](i - 1))
                    act.activation(nT[:, slot % 2, :], ps[:, 2 + slot % 2, :], ACT.Copy).then_inc(s["nT"].sem, 1)

                def relu(i, q, slot):
                    act.wait_ge(*s["norm"](i + 1))
                    if later(i, 4):
                        act.wait_ge(*s[f"st{slot}"](16 * q))
                    act.activation(xout[:, slot, :, :], aff[:, slot % 2, :, :], ACT.Relu).then_inc(s["act"].sem, 1)

                pipeline(act, GROUPS, 4, [(copy_n, 0)] + ([] if layer else [(relu, 2)]))

            act.wait_ge(s_win, 16 * len(small_loads))
            edges("l0a")
            d0()
            edges("l0b")
            d1()
            edges("l1")
            d2a()
            edges("l2")
            d2b()
            edges("l3a")
            d3("d3a", 0)
            edges("l3b")
            d3("d3b", 1)

        @block.tensor
        def _(pe):
            pe.wait_ge(s_win, 16 * len(small_loads))
            pe.matmul(ps[:, 0, 0:D], w_linT[:, :], w_upd[:, 0, :], start=True, stop=True)
            pe.matmul(ps[:, 1, 0:D], w_msgT[:, :], w_upd[:, 1, :], start=True, stop=True)
            pe.matmul(ps[0:1, 2, 0:D], b_lin[:, :], w_upd[:, 0, :], start=True, stop=True)
            pe.matmul(ps[0:1, 3, 0:D], b_msg[:, :], w_upd[:, 1, :], start=True, stop=True).then_inc(s_comb, 1)
            pe.wait_ge(s_bm, 1)
            pe.wait_ge(s_brow, 16 * 5)
            pe.wait_ge(s_const, 7)
            pe.wait_ge(s_cdve, 2)

            def edges(name):
                s = edge_s[name]
                w = sum_d[name].shape[1]

                def merge(i, q, slot):
                    pe.wait_ge(*s["same"](i + 1))
                    pe.wait_ge(*s["msg"](i + 1))
                    if later(i, 2):
                        pe.wait_ge(*s["evac"](i - 1))
                    for k in range(K):
                        for j in range(K):
                            last = pe.matmul(ps[:, 2 * slot + k // 2, (k % 2) * 256:(k % 2) * 256 + w], same[:, slot, j, k:ROWS:K],
                                             msg[:, slot, j, 0:w], start=(j == 0), stop=(j == K - 1), skip_group_check=True)
                    last.then_inc(s["merge"].sem, 1)

                pipeline(pe, STEPS, 2, [(merge, 0)])

            def transposes(s, bank, rows, loaded_count, free, done, wide=True):
                def stage(i, q, slot):
                    if loaded_count:
                        pe.wait_ge(*s[f"in{slot}"](16 * loaded_count * (q + 1)))
                    else:
                        pe.wait_ge(*s["neigh"](i + 1))
                    behind = 2 if wide else 1
                    if later(i, behind):
                        for name, per in free:
                            pe.wait_ge(*s[name](per * (i - behind + 1)))
                    for k in range(K):
                        last = pe.transpose(ps[:, bank + (slot % 2 if wide else 0), k * P:(k + 1) * P], rows(slot)[:, k, 0:D], ident[:, :])
                    last.then_inc(s[done].sem, 1)
                return stage

            def bias(bank, lo, n, width):
                pe.matmul(ps[:, bank, 0:ROWS], ones_bf[:, :],
                          bias3[:, lo:lo + width].rearrange("p (a d) -> p a d", a=1).to_broadcast([P, n, width]),
                          start=True, stop=False, skip_group_check=True)

            def d0():
                s = node_s["d0"]

                def products(i, q, slot):
                    pe.wait_ge(*s["xT"](i + 1))
                    pe.wait_ge(*s["nT"](i + 1))
                    if later(i, 2):
                        pe.wait_ge(*s["act"](i - 1))
                    b = 4 + slot % 2
                    bias(b, BL0, K, D)
                    for k in range(K):
                        c = slice(k * P, (k + 1) * P)
                        pe.matmul(ps[:, b, c], xT[:, slot % 2, c], w_self[:, 0, :], start=False, stop=False, skip_group_check=True)
                        last = pe.matmul(ps[:, b, c], nT[:, slot % 2, c], w_neigh[:, 0, :], start=False, stop=(k == K - 1),
                                         skip_group_check=True)
                    last.then_inc(s["mm"].sem, 1)

                pipeline(pe, GROUPS, 4, [(transposes(s, 0, lambda c: xin[:, c, :, :], 2, [("xT", 1)], "tx"), 0),
                                         (transposes(s, 2, lambda c: neigh[:, c % 2, :, :], 0, [("nT", 1)], "tn"), 0), (products, 1)])

            def d1():
                s = node_s["d1"]

                def products(i, q, slot):
                    pe.wait_ge(*s["xT"](i + 1))
                    pe.wait_ge(*s["nT"](i + 1))
                    if later(i, 2):
                        pe.wait_ge(*s["act"](i - 1))
                    b = 4 + slot % 2
                    pe.matmul(ps[:, b, :], w_self[:, 1, :], xT[:, slot % 2, :], start=True, stop=False)
                    pe.matmul(ps[:, b, :], w_neigh[:, 1, :], nT[:, slot % 2, :], start=False, stop=True).then_inc(s["mm"].sem, 1)

                def final(i, q, slot):
                    pe.wait_ge(*s["x2"](i + 1))
                    if later(i, 2):
                        pe.wait_ge(*s["res"](i - 1))
                    b = 6 + slot % 2
                    bias(b, BAGG, K, D)
                    for k in range(K):
                        c = slice(k * P, (k + 1) * P)
                        last = pe.matmul(ps[:, b, c], x2T[:, slot % 2, c], w_agg[:, :], start=False, stop=(k == K - 1), skip_group_check=True)
                    last.then_inc(s["y"].sem, 1)

                pipeline(pe, GROUPS, 4, [(transposes(s, 0, lambda c: xin[:, c, :, :], 3, [("xT", 1)], "tx"), 0),
                                         (transposes(s, 2, lambda c: neigh[:, c % 2, :, :], 0, [("nT", 1)], "tn"), 0),
                                         (products, 1), (final, 2)])

            def d2a():
                s = node_s["d2a"]

                def turn_sums(i, q, slot):
                    pe.wait_ge(*s["neigh"](i + 1))
                    if later(i, 2):
                        pe.wait_ge(*s["nT"](i - 1))
                        pe.wait_ge(*s["xT"](2 * (i - 1)))
                    for k in range(K):
                        c = slice(k * P, (k + 1) * P)
                        pe.transpose(ps[:, 2 + slot % 2, c], neigh[:, slot % 2, k, 0:D], ident[:, :])
                        last = pe.transpose(ps[0:4, 6 + slot % 2, c], neigh[:, slot % 2, k, D:WIDE], ident[:, :])
                    last.then_inc(s["tn"].sem, 1)

                def products(i, q, slot):
                    pe.wait_ge(*s["xT"](2 * (i + 1)))
                    pe.wait_ge(*s["nT"](i + 1))
                    if later(i, 2):
                        pe.wait_ge(*s["res"](i - 1))
                    for k in range(K):
                        c = slice(k * P, (k + 1) * P)
                        o = ps[:, 4 + slot % 2, c]
                        pe.matmul(o, xT[:, slot % 2, c], w_c1[:, :], start=True, stop=False, skip_group_check=True)
                        pe.matmul(o, nT[:, slot % 2, c], w_c2[:, :], start=False, stop=False, skip_group_check=True)
                        last = pe.matmul(o, fT[:, slot % 2, c], bm4[:, :], start=False, stop=True, skip_group_check=True)
                    last.then_inc(s["mm"].sem, 1)

                pipeline(pe, GROUPS, 4, [(transposes(s, 0, lambda c: xin[:, c, :, :], 2, [("xT", 2)], "tx"), 0),
                                         (turn_sums, 0), (products, 1)])

            def d2b():
                s = node_s["d2b"]

                def products(i, q, slot):
                    pe.wait_ge(*s["xT"](i + 1))
                    pe.wait_ge(*s["nT"](i + 1))
                    if later(i, 1):
                        pe.wait_ge(*s["hn"](i))
                    for b in range(2):
                        bias(2 + b, BH, 2, HID)
                        for j in range(2):
                            k = 2 * b + j
                            c = slice(k * P, (k + 1) * P)
                            o = ps[:, 2 + b, j * HID:(j + 1) * HID]
                            pe.matmul(o, xT[:, slot % 2, c], w_h[:, 0, :], start=False, stop=False, skip_group_check=True)
                            last = pe.matmul(o, nT[:, slot % 2, c], w_h[:, 1, :], start=False, stop=(j == 1), skip_group_check=True)
                    last.then_inc(s["mm"].sem, 1)

                def turn_hidden(i, q, slot):
                    pe.wait_ge(*s["hn"](i + 1))
                    if later(i, 1):
                        pe.wait_ge(*s["hT"](i))
                    for h in range(2):
                        for k in range(K):
                            last = pe.transpose(ps[:, 4 + h, k * P:(k + 1) * P], hid[:, k, h * P:(h + 1) * P], ident[:, :])
                    last.then_inc(s["th"].sem, 1)

                def last_products(i, q, slot):
                    pe.wait_ge(*s["hT"](i + 1))
                    if later(i, 2):
                        pe.wait_ge(*s["res"](i - 1))
                    b = 6 + slot % 2
                    bias(b, BO, K, D)
                    for k in range(K):
                        c = slice(k * P, (k + 1) * P)
                        for h in range(2):
                            last = pe.matmul(ps[:, b, c], hidT[:, slot % 2, h, c], w_o[:, h, :], start=False,
                                             stop=(k == K - 1 and h == 1), skip_group_check=True)
                    last.then_inc(s["o"].sem, 1)

                pipeline(pe, GROUPS, 4, [(transposes(s, 0, lambda c: xin[:, c, :, :], 2, [("xT", 1)], "tx", False), 0),
                                         (transposes(s, 1, lambda c: sums[:, c, :, :], 2, [("nT", 1)], "tn", False), 0),
                                         (turn_hidden, 1), (products, 0), (last_products, 1)])

            def d3(phase, layer):
                s = node_s[phase]

                def products(i, q, slot):
                    pe.wait_ge(*s["nT"](i + 1))
                    if later(i, 2):
                        pe.wait_ge(*s["res"](i - 1))
                    for k in range(K):
                        c = slice(k * P, (k + 1) * P)
                        last = pe.matmul(ps[:, 4 + slot % 2, c], nT[:, slot % 2, c], w_r[:, layer, :], start=True, stop=True,
                                         skip_group_check=True)
                    last.then_inc(s["mm"].sem, 1)

                pipeline(pe, GROUPS, 4, [(transposes(s, 2, lambda c: neigh[:, c % 2, :, :], 0, [("nT", 1)], "tn"), 0), (products, 1)])

            edges("l0a")
            d0()
            edges("l0b")
            d1()
            edges("l1")
            d2a()
            edges("l2")
            d2b()
            edges("l3a")
            d3("d3a", 0)
            edges("l3b")
            d3("d3b", 1)


_TURNED = ("L0_gnn_W_self", "L0_gnn_W_neigh", "L0_gnn_W_agg", "L1_gnn_W_lin", "L1_gnn_W_msg", "L3_gnn_W1", "L3_gnn_W2")


def kernel(**inputs):
    import numpy as _np
    import concourse.bacc as _bacc
    from concourse import mybir as _mybir
    from concourse.bass_utils import run_bass_kernel_spmd as _run

    nc = _bacc.Bacc("TRN2", target_bir_lowering=False, num_devices=1)
    arrays, tensors = {}, {}
    for name, value in inputs.items():
        a = _np.asarray(value)
        if name in _TURNED:
            a = _np.swapaxes(a, -1, -2)
        a = _np.ascontiguousarray(a)
        arrays[f"in_{name}"] = a
        tensors[name] = nc.dram_tensor(f"in_{name}", a.shape, _mybir.dt.from_np(a.dtype), kind="ExternalInput").ap()
    out = nc.dram_tensor("out_0", (N, D), F32, kind="ExternalOutput").ap()
    program(nc, tensors, out)
    r = _run(nc, [arrays], core_ids=[0])
    return r.results[0]["out_0"]
```

```python
from contextlib import ExitStack

import concourse.bass as bass
from concourse import mybir

F32 = mybir.dt.float32
BF16 = mybir.dt.bfloat16
I32 = mybir.dt.int32
ALU = mybir.AluOpType
ACT = mybir.ActivationFunctionType
AX_X = mybir.AxisListType.X

P = 128
D = 128
N = 50000
E = 25000
NREL = 1001
HID = 256
K = 4
ROWS = K * P
GROUPS = -(-N // ROWS)
STEPS = -(-E // ROWS)
LAST_NODES = (N - (GROUPS - 1) * ROWS) // K
LAST_EDGES = (E - (STEPS - 1) * ROWS) // K
TRASH = N
WIDE = 132
TABLE = 99 * ROWS
XROWS = GROUPS * ROWS
SLOPE = 0.2
EPS = 1e-5


def pipeline(engine, n, unroll, stages, tail=1):
    ahead = min(lag for _, lag in stages)
    stages = [(stage, lag - ahead) for stage, lag in stages]
    lag_max = max(lag for _, lag in stages)
    first = -(-(lag_max + 4) // unroll) * unroll
    end = (n - tail) // unroll * unroll

    def step(j, u):
        for stage, lag in stages:
            slot = (u - lag) % unroll
            q = j + (u - lag - slot) // unroll
            i = q * unroll + slot
            if not isinstance(i, int) or 0 <= i < n:
                stage(i, q, slot)

    for t in range(first):
        step(t // unroll, t % unroll)
    with engine.Fori(first // unroll, end // unroll) as j:
        for u in range(unroll):
            step(j, u)
    for t in range(end, n + lag_max):
        step(t // unroll, t % unroll)


def later(i, behind):
    return not isinstance(i, int) or i >= behind


def program(nc, t, out):
    ctx = ExitStack()
    with ctx:
        def sb(name, shape, dt=F32):
            return ctx.enter_context(nc.sbuf_tensor(name, shape, dt))

        def sem(name):
            return ctx.enter_context(nc.semaphore(name))

        def dram(name, shape, dt=F32):
            return nc.dram_tensor(name, shape, dt).ap()

        x1_d, xa_d, xb_d, xc_d, x5_d = (dram(f"nodes_{n}", (XROWS, D)) for n in ("l0", "a", "b", "c", "l3"))
        sum_d = {n: dram(f"sums_{n}", (TABLE, w)) for n, w in
                 (("l0a", WIDE), ("l0b", D), ("l1", WIDE), ("l2", D), ("l3a", D), ("l3b", D))}
        rel_d = dram("rel_unit", (NREL, D))
        rel_edge_d = dram("rel_of_edges", (STEPS * ROWS, D))

        ident = sb("ident", [P, P])
        zeros = sb("zeros", [P, 32 * WIDE])
        neg_half = sb("neg_half", [P, 4])
        pos_half = sb("pos_half", [P, 11])
        ones_bf = sb("ones_bf", [P, P], BF16)
        rev = sb("rev", [P, ROWS])
        rev_own = sb("rev_own", [P, K])
        trash = sb("trash", [P, K])
        w_self = sb("w_self", [P, 2, D])
        w_neigh = sb("w_neigh", [P, 2, D])
        w_agg = sb("w_agg", [P, D])
        w_linT = sb("w_linT", [P, D])
        w_msgT = sb("w_msgT", [P, D])
        w_upd = sb("w_upd", [P, 2, D])
        w_c1 = sb("w_c1", [P, D])
        w_c2 = sb("w_c2", [P, D])
        w_h = sb("w_h", [P, 2, HID])
        w_o = sb("w_o", [P, 2, D])
        w_r = sb("w_r", [P, 2, D])
        b_lin = sb("b_lin", [P, 1])
        b_msg = sb("b_msg", [P, 1])
        col3 = sb("col3", [P, 3])
        b_l0b = sb("b_l0b", [P, 1])
        b_below = sb("b_below", [P, 1])
        ln_g = sb("ln_g", [P, 2])
        ln_b = sb("ln_b", [P, 2])
        BL0, BAGG, BH, BO = 0, D, 2 * D, 2 * D + HID
        NB = BO + D
        brow = sb("brow", [1, 3, NB])
        bparts = sb("bparts", [1, 3, NB], BF16)
        bias3 = sb("bias3", [P, NB], BF16)
        brow_upd = sb("brow_upd", [1, D])
        bmrow = sb("bmrow", [1, 2, D])
        bm4 = sb("bm4", [4, D])
        g3 = sb("g3", [P, 2, D])
        b3 = sb("b3", [P, 2, D])
        rel_in = sb("rel_in", [91, 11, D])
        rel_sq = sb("rel_sq", [91, 11, D])
        rel_ss = sb("rel_ss", [91, 11])
        rel_nm = sb("rel_nm", [91, 11])
        eps4 = sb("eps4", [P, 4])

        src_i = sb("src_i", [P, STEPS, K], I32)
        dst_i = sb("dst_i", [P, STEPS, K], I32)
        type_i = sb("type_i", [P, STEPS, K], I32)
        weight = sb("weight", [P, STEPS, K])
        src_f = sb("src_f", [P, STEPS, K])
        dst_f = sb("dst_f", [P, STEPS, K])
        put_src = sb("put_src", [P, STEPS, K], I32)
        put_dst = sb("put_dst", [P, STEPS, K], I32)

        inv_l0 = sb("inv_l0", [P, GROUPS, K])
        inv_l3 = sb("inv_l3", [P, GROUPS, K])

        at_get = sb("at_get", [P, 2, K], I32)
        at_rel = sb("at_rel", [P, 2, K], I32)
        at_put = sb("at_put", [P, 2, K], I32)
        got = sb("got", [P, 2, K, D])
        rel = sb("rel", [P, 2, K, D])
        msg = sb("msg", [P, 2, K, WIDE])
        ids = sb("ids", [P, 2, ROWS], I32)
        same = sb("same", [P, 2, K, ROWS])
        merged = sb("merged", [P, 2, K, WIDE])
        hit = sb("hit", [P, ROWS])
        first4 = sb("first4", [P, 2, K])
        sel4 = sb("sel4", [P, 3, K])
        dot4 = sb("dot4", [P, 2, K])
        prod = sb("prod", [P, D])

        xin = sb("xin", [P, 4, K, D])
        xres = sb("xres", [P, 4, K, D])
        sums = sb("sums", [P, 4, K, WIDE])
        cnt4 = sb("cnt4", [P, 2, 2, K])
        neigh = sb("neigh", [P, 4, K, WIDE])
        xT = sb("xT", [P, 2, ROWS])
        nT = sb("nT", [P, 2, ROWS])
        fT = sb("fT", [4, 2, ROWS])
        x2T = sb("x2T", [P, 2, ROWS])
        above = sb("above", [P, 2, ROWS])
        below = sb("below", [P, 2, ROWS])
        res = sb("res", [P, 4, K, D])
        hid = sb("hid", [P, K, HID])
        hidT = sb("hidT", [P, 2, 2, ROWS])
        stat = sb("stat", [P, 3, K, 6])
        mv = sb("mv", [P, 3, 4, K, 2])
        shift = sb("shift", [P, 3, 4, K])
        rstd = sb("rstd", [P, 3, 4, K])
        vare = sb("vare", [P, 3, 4, K])
        negmean = sb("negmean", [P, 3, 4, K])
        aff = sb("aff", [P, 4, K, D])
        xout = sb("xout", [P, 4, K, D])

        ps = ctx.enter_context(nc.psum_tensor("ps", [P, 8, ROWS], F32))

        s_const = sem("s_const")
        s_cdve = sem("s_cdve")
        s_zero = {n: sem(f"s_zero_{n}") for n in sum_d}
        s_win = sem("s_win")
        s_rel_in = sem("s_rel_in")
        s_eload = sem("s_eload")
        s_ecast = sem("s_ecast")
        s_bpart = sem("s_bpart")
        s_brow = sem("s_brow")
        s_comb = sem("s_comb")
        s_combv = sem("s_combv")
        s_bm = sem("s_bm")
        s_relss = sem("s_relss")
        s_relnm = sem("s_relnm")
        s_relok = sem("s_relok")
        s_relst = sem("s_relst")
        pool_step = sem("pool_step")
        sp_step = sem("sp_step")
        pool_copied = sem("pool_copied")

        class Count:

            def __init__(self, semaphore, base):
                self.sem, self.base = semaphore, base

            def __call__(self, n):
                return self.sem, self.base + n

        def edge_totals(name):
            slots = [len(range(slot, STEPS, 2)) for slot in range(2)]
            gathered = {"l2": 0, "l3a": 128}.get(name, 64)
            kept = name in ("l2", "l3a", "l3b")
            return {
                "ids0": 16 * slots[0], "ids1": 16 * slots[1],
                "got0": gathered * slots[0], "got1": gathered * slots[1],
                "keep0": 16 * slots[0] * kept, "keep1": 16 * slots[1] * kept,
                "same": STEPS, "msg": STEPS,
                "merge": STEPS, "evac": STEPS,
                "index": (2 if name == "l3a" else 0 if name == "l2" else 1) * STEPS,
                "put": 64 * STEPS,
            }

        def node_totals(phase):
            slots = [len(range(slot, GROUPS, 4)) for slot in range(4)]
            front, late_a, late_b = {"d0": (2, 0, 0), "d1": (2, 1, 0), "d2a": (2, 1, 0), "d2b": (2, 1, 0),
                                     "d3a": (1, 1, 0), "d3b": (1, 1, 1)}[phase]
            used = {"d0": "neigh tx tn xT nT mm act norm",
                    "d1": "root0 total neigh tx tn xT nT mm act x2 y res var rstd norm",
                    "d2a": "root0 neigh tx tn xT nT mm res var rstd norm",
                    "d2b": "root0 root1 tx tn xT nT mm hst hrs hn th hT o res var rstd norm",
                    "d3a": "root0 neigh tn nT mm res var rstd unit scaled norm act",
                    "d3b": "root0 root2 neigh tn nT mm res var rstd unit scaled res2 o2 rstd2 norm"}[phase].split()
            made = {name: GROUPS for name in used}
            if phase == "d2a":
                made["xT"] = 2 * GROUPS
            for slot in range(4):
                made[f"in{slot}"] = 16 * front * slots[slot]
                made[f"ra{slot}"] = 16 * late_a * slots[slot]
                made[f"rb{slot}"] = 16 * late_b * slots[slot]
                made[f"st{slot}"] = 16 * slots[slot]
            return made

        handles, reached = {}, {}

        def counts(kind, totals):
            made = {}
            for name, total in totals.items():
                key = f"{kind}_{name}"
                if key not in handles:
                    handles[key], reached[key] = sem(key), 0
                made[name] = Count(handles[key], reached[key])
                reached[key] += total
            return made

        edge_s = {name: counts("e", edge_totals(name)) for name in sum_d}
        node_s = {phase: counts("n", node_totals(phase)) for phase in ("d0", "d1", "d2a", "d2b", "d3a", "d3b")}

        SRC = {"l0a": t["x"], "l0b": x1_d, "l1": xa_d, "l3a": xc_d, "l3b": x5_d}
        BEFORE = {"l0b": "d0", "l1": "d1", "l3a": "d2b", "l3b": "d3a"}
        puts_before = {name: n * STEPS for n, name in enumerate(("l0a", "l0b", "l1", "l2", "l3a", "l3b"))}
        zero_jobs = []
        for n in ("l0a", "l0b", "l1", "l2", "l3a", "l3b"):
            w = sum_d[n].shape[1]
            r = 32 if w == WIDE else 33
            per = TABLE // P
            view = sum_d[n].rearrange("(p r) d -> p r d", p=P)
            done = 0
            while done < per:
                m = min(r, per - done)
                zero_jobs.append((n, view[:, done:done + m, :], zeros[:, 0:m * w].rearrange("p (r d) -> p r d", d=w)))
                done += m
        zero_count = {n: 16 * sum(job[0] == n for job in zero_jobs) for n in sum_d}

        def stores_done(engine, phase):
            for slot in range(4):
                engine.wait_ge(*node_s[phase][f"st{slot}"](16 * len(range(slot, GROUPS, 4))))

        small_loads = [
            (w_self, t["L0_gnn_W_self"].rearrange("l i o -> i l o")), (w_neigh, t["L0_gnn_W_neigh"].rearrange("l i o -> i l o")),
            (w_agg, t["L0_gnn_W_agg"]), (w_linT, t["L1_gnn_W_lin"]), (w_msgT, t["L1_gnn_W_msg"]),
            (w_upd, t["L1_gnn_W_upd"].rearrange("(h i) o -> i h o", i=D)),
            (w_h, t["L2_gnn_W1"].rearrange("(h i) o -> i h o", i=D)), (w_o, t["L2_gnn_W2"].rearrange("(h i) o -> i h o", i=D)),
            (w_r[:, 0, :], t["L3_gnn_W1"]), (w_r[:, 1, :], t["L3_gnn_W2"]),
            (b_lin, t["L1_gnn_b_lin"].rearrange("(p a) -> p a", a=1)), (b_msg, t["L1_gnn_b_msg"].rearrange("(p a) -> p a", a=1)),
            
            (g3[:, 0, :], t["L3_gnn_ln1_g"].partition_broadcast(P)), (g3[:, 1, :], t["L3_gnn_ln2_g"].partition_broadcast(P)),
            (b3[:, 0, :], t["L3_gnn_ln1_b"].partition_broadcast(P)), (b3[:, 1, :], t["L3_gnn_ln2_b"].partition_broadcast(P)),
            (brow_upd, t["L1_gnn_b_upd"].rearrange("(a n) -> a n", a=1)),
            (brow[:, 0, BAGG:BAGG + D], t["L0_gnn_b_agg"].rearrange("(a n) -> a n", a=1)),
            (brow[:, 0, BH:BH + HID], t["L2_gnn_b1"].rearrange("(a n) -> a n", a=1)),
            (brow[:, 0, BO:BO + D], t["L2_gnn_b2"].rearrange("(a n) -> a n", a=1)),
        ]
        for i, name in enumerate(("b_self", "b_neigh", "layer_bias")):
            b = t[f"L0_gnn_{name}"]
            small_loads.append((brow[:, i, BL0:BL0 + D], b[0:1, :]))
            small_loads.append((col3[:, i:i + 1], b[1, :].rearrange("(p a) -> p a", a=1)))
        for h in range(2):
            small_loads.append((ln_g[:, h:h + 1], t["L2_gnn_ln_g"][h * P:(h + 1) * P].rearrange("(p a) -> p a", a=1)))
            small_loads.append((ln_b[:, h:h + 1], t["L2_gnn_ln_b"][h * P:(h + 1) * P].rearrange("(p a) -> p a", a=1)))

        block = ctx.enter_context(nc.Block())

        @block.sync
        def _(sp):
            def held(semaphore, value):
                sp.wait_ge(semaphore, value)
                sp.sem_inc(sp_step, 1)

            full = (STEPS - 1) * ROWS
            sp.wait_ge(s_cdve, 1)
            for name, tile in (("src", src_i), ("dst", dst_i), ("edge_type_1001", type_i), ("edge_weight", weight)):
                v = t[name]
                sp.dma_start(tile[:, 0:STEPS - 1, :], v[0:full].rearrange("(s p k) -> p s k", p=P, k=K)).then_inc(s_eload, 16)
                sp.dma_start(tile[0:LAST_EDGES, STEPS - 1, :],
                             v[full:E].rearrange("(p k) -> p k", k=K)).then_inc(s_eload, 16)
            for tile, ap in small_loads:
                sp.dma_start(tile[tuple(slice(None) for _ in tile.shape)], ap).then_inc(s_win, 16)
            sp.dma_start(rel_in[:, :, :], t["L3_gnn_rel_emb"].rearrange("(p r) d -> p r d", r=11)).then_inc(s_rel_in, 16)
            sp.wait_ge(s_bpart, 1)
            for i in range(3):
                sp.dma_start(bias3[i:i + 1, :], bparts[0:1, i, :]).then_inc(s_brow, 16)
            sp.wait_ge(s_bm, 1)
            for i in range(2):
                sp.dma_start(bm4[i:i + 1, :], bmrow[0:1, i, :]).then_inc(s_brow, 16)
            sp.wait_ge(s_relok, 1)
            sp.dma_start(rel_d.rearrange("(p r) d -> p r d", r=11), rel_in[:, :, :]).then_inc(s_relst, 16)

            def edges(name):
                s = edge_s[name]
                nodes = t["src"] if name == "l1" else t["dst"]

                def ids_load(i, q, slot):
                    if later(i, 2):
                        held(*s["same"](i - 1))
                    if isinstance(i, int) and i == STEPS - 1:
                        src = nodes[full:E].rearrange("(a n) -> a n", a=1)[0, :].partition_broadcast(P)
                        sp.dma_start(ids[:, slot, 0:E - full], src).then_inc(s[f"ids{slot}"].sem, 16)
                        if name == "l2":
                            sp.wait_ge(*s["msg"](i - 1))
                            sp.dma_start(got[0:LAST_EDGES, slot, :, :],
                                         t["edge_attr_128"][full:E, :].rearrange("(p k) d -> p k d", k=K)).then_inc(s[f"keep{slot}"].sem, 16)
                        if name == "l3b":
                            sp.wait_ge(*s["msg"](i - 1))
                            sp.dma_start(rel[:, slot, :, :], rel_edge_d[full:full + ROWS, :].rearrange("(p k) d -> p k d", k=K))\
                              .then_inc(s[f"keep{slot}"].sem, 16)
                        return
                    sp.dma_start(ids[:, slot, :], nodes[bass.ds(i * ROWS, ROWS)].partition_broadcast(P)).then_inc(s[f"ids{slot}"].sem, 16)
                    if name == "l2":
                        if later(i, 2):
                            held(*s["msg"](i - 1))
                        sp.dma_start(got[:, slot, :, :],
                                     t["edge_attr_128"][bass.ds(i * ROWS, ROWS), :].rearrange("(p k) d -> p k d", k=K))\
                          .then_inc(s[f"keep{slot}"].sem, 16)
                    if name == "l3b":
                        if later(i, 2):
                            held(*s["msg"](i - 1))
                        sp.dma_start(rel[:, slot, :, :],
                                     rel_edge_d[bass.ds(i * ROWS, ROWS), :].rearrange("(p k) d -> p k d", k=K))\
                          .then_inc(s[f"keep{slot}"].sem, 16)

                def rel_keep(i, q, slot):
                    held(*s["msg"](i + 1))
                    sp.dma_start(rel_edge_d[bass.ds(i * ROWS, ROWS), :].rearrange("(p k) d -> p k d", k=K),
                                 rel[:, slot, :, :]).then_inc(s[f"keep{slot}"].sem, 16)

                if name == "l3b":
                    for slot in range(2):
                        sp.wait_ge(*edge_s["l3a"][f"keep{slot}"](16 * len(range(slot, STEPS, 2))))
                pipeline(sp, STEPS, 2, [(ids_load, 0)] + ([(rel_keep, 1)] if name == "l3a" else []))

            def nodes(phase, front, front_free, late, ready, dest, sums_name, lag):
                s = node_s[phase]
                w = sum_d[sums_name].shape[1]
                sp.wait_ge(*edge_s[sums_name]["put"](64 * STEPS))
                if phase == "d2b":
                    stores_done(sp, "d2a")

                def fetch(buf, table, exact, i, slot, semaphore):
                    p = LAST_NODES if exact and isinstance(i, int) and i == GROUPS - 1 else P
                    w = buf.shape[3] if table.shape[1] == WIDE else D
                    sp.dma_start(buf[0:p, slot, :, 0:w], table[bass.ds(i * ROWS, p * K), :].rearrange("(p k) d -> p k d", k=K))\
                      .then_inc(semaphore, 16)

                def load(i, q, slot):
                    if later(i, 4):
                        for f in front_free:
                            held(*s[f](i - 3))
                    for buf, table, exact in front:
                        fetch(buf, table, exact, i, slot, s[f"in{slot}"].sem)
                    fetch(sums, sum_d[sums_name], False, i, slot, s[f"in{slot}"].sem)

                def late_load(buf, table, exact, name, free):
                    def stage(i, q, slot):
                        if later(i, 4):
                            held(*s[free](i - 3))
                        fetch(buf, table, exact, i, slot, s[f"{name}{slot}"].sem)
                    return stage

                def store(i, q, slot):
                    held(*s[ready](i + 1))
                    p = LAST_NODES if dest is out and isinstance(i, int) and i == GROUPS - 1 else P
                    sp.dma_start(dest[bass.ds(i * ROWS, p * K), :].rearrange("(p k) d -> p k d", k=K),
                                 xout[0:p, slot, :, :]).then_inc(s[f"st{slot}"].sem, 16)

                pipeline(sp, GROUPS, 4, [(load, 0)] + [(late_load(*item[:-1]), item[-1]) for item in late] + [(store, lag)])

            edges("l0a")
            nodes("d0", [(xin, t["x"], True)], ["tx", "neigh"], [], "norm", x1_d, "l0a", 9)
            edges("l0b")
            nodes("d1", [(xin, x1_d, False)], ["tx", "total"], [(xres, t["x"], True, "ra", "res", 6)], "norm", xa_d, "l0b", 14)
            edges("l1")
            nodes("d2a", [(xin, xa_d, False)], ["tx", "neigh"], [(xres, xa_d, False, "ra", "res", 3)], "norm", xb_d, "l1", 10)
            edges("l2")
            nodes("d2b", [(xin, xb_d, False)], ["tx", "tn"], [(xres, xb_d, False, "ra", "res", 6)], "norm", xc_d, "l2", 13)
            edges("l3a")
            nodes("d3a", [], ["neigh"], [(xin, xc_d, False, "ra", "res", 2)], "act", x5_d, "l3a", 14)
            edges("l3b")
            nodes("d3b", [], ["neigh"], [(xin, x5_d, False, "ra", "res", 2), (xres, xc_d, False, "rb", "res2", 6)],
                  "norm", out, "l3b", 14)
            stores_done(sp, "d3b")

        @block.gpsimd
        def _(pool):
            def held(semaphore, value):
                pool.wait_ge(semaphore, value)
                pool.sem_inc(pool_step, 1)

            pool.memset(ident[:, :], 0.0).then_inc(s_const, 1)
            pool.wait_ge(s_const, 1)
            pool.affine_select(out=ident[:, :], in_=ident[:, :], compare_op=ALU.not_equal, fill=1.0, base=0,
                               pattern=[[-1, P]], channel_multiplier=1).then_inc(s_const, 1)
            pool.iota(rev[:, :], pattern=[[-1, ROWS]], base=ROWS, channel_multiplier=0,
                      allow_small_or_imprecise_dtypes=True).then_inc(s_const, 1)
            pool.iota(rev_own[:, :], pattern=[[-1, K]], base=ROWS, channel_multiplier=-K,
                      allow_small_or_imprecise_dtypes=True).then_inc(s_const, 1)
            pool.iota(trash[:, :], pattern=[[1, K]], base=TRASH, channel_multiplier=K,
                      allow_small_or_imprecise_dtypes=True).then_inc(s_const, 1)
            pool.memset(neg_half[:, :], -0.5).then_inc(s_const, 1)
            pool.memset(pos_half[:, :], 0.5).then_inc(s_const, 1)
            pool.wait_ge(s_relss, 1)
            pool.wait_ge(s_const, 7)
            pool.tensor_tensor(rel_nm[:, :], rel_ss[:, :], pos_half[0:91, :], ALU.pow).then_inc(s_relnm, 1)
            pool.wait_ge(s_eload, 128)

            def edges(name):
                s = edge_s[name]
                get_i = dst_i if name == "l1" else src_i
                put_i = put_src if name == "l1" else put_dst
                w = sum_d[name].shape[1]

                def get(i, q, slot):
                    if name == "l2":
                        return
                    if later(i, 2):
                        held(*s["msg"](i - 1))
                        if name == "l3a":
                            held(*s[f"keep{slot}"](16 * q))
                    pool.tensor_copy(at_get[:, slot, :], get_i[:, bass.ds(i, 1), :].rearrange("p a k -> p (a k)"))\
                        .then_inc(s["index"].sem, 1)
                    if name == "l3a":
                        pool.tensor_copy(at_rel[:, slot, :], type_i[:, bass.ds(i, 1), :].rearrange("p a k -> p (a k)"))\
                            .then_inc(s["index"].sem, 1)
                    held(*s["index"]((i + 1) * 2 if name == "l3a" else i + 1))
                    for k in range(K):
                        pool.indirect_dma_start(out=got[:, slot, k, :], out_offset=None, in_=SRC[name],
                                                in_offset=bass.IndirectOffsetOnAxis(ap=at_get[:, slot, k:k + 1], axis=0))\
                            .then_inc(s[f"got{slot}"].sem, 16)
                    if name == "l3a":
                        for k in range(K):
                            pool.indirect_dma_start(out=rel[:, slot, k, :], out_offset=None, in_=rel_d,
                                                    in_offset=bass.IndirectOffsetOnAxis(ap=at_rel[:, slot, k:k + 1], axis=0))\
                                .then_inc(s[f"got{slot}"].sem, 16)

                def put(i, q, slot):
                    held(*s["evac"](i + 1))
                    if later(i, 1):
                        held(*s["put"](64 * i))
                    pool.tensor_copy(at_put[:, slot, :], put_i[:, bass.ds(i, 1), :].rearrange("p a k -> p (a k)"))\
                        .then_inc(pool_copied, 1)
                    held(pool_copied, puts_before[name] + i + 1)
                    for k in range(K):
                        pool.indirect_dma_start(out=sum_d[name],
                                                out_offset=bass.IndirectOffsetOnAxis(ap=at_put[:, slot, k:k + 1], axis=0),
                                                in_=merged[:, slot, k, 0:w], in_offset=None, compute_op=ALU.add)\
                            .then_inc(s["put"].sem, 16)

                if name in BEFORE:
                    stores_done(pool, BEFORE[name])
                if name == "l3a":
                    pool.wait_ge(s_relst, 16)
                pool.wait_ge(s_zero[name], zero_count[name])
                pipeline(pool, STEPS, 2, [(get, 0), (put, 1)])

            def power(phase, n, ready, done):
                s = node_s[phase]

                def stage(i, q, slot):
                    held(*s[ready](i + 1))
                    pool.tensor_tensor(rstd[:, n, slot, :], vare[:, n, slot, :], neg_half[:, :], ALU.pow)\
                        .then_inc(s[f"root{n}"].sem, 1)
                    held(*s[f"root{n}"](i + 1))
                    pool.tensor_tensor(shift[:, n, slot, :], negmean[:, n, slot, :], rstd[:, n, slot, :], ALU.mult)\
                        .then_inc(s[done].sem, 1)
                return stage

            def join(phase):
                s = node_s[phase]

                def stage(i, q, slot):
                    held(*s["act"](i + 1))
                    if phase == "d0":
                        if later(i, 4):
                            held(*s[f"st{slot}"](16 * q))
                        pool.tensor_tensor(xout[:, slot, :, :].rearrange("p k d -> p (k d)"), above[:, slot % 2, :],
                                           below[:, slot % 2, :], ALU.subtract).then_inc(s["norm"].sem, 1)
                    else:
                        if later(i, 2):
                            held(*s["y"](i - 1))
                        pool.tensor_tensor(x2T[:, slot % 2, :], above[:, slot % 2, :], below[:, slot % 2, :], ALU.subtract)\
                            .then_inc(s["x2"].sem, 1)
                return stage

            def add_self(i, q, slot):
                s = node_s["d1"]
                held(*s[f"in{slot}"](32 * (q + 1)))
                if later(i, 4):
                    held(*s["tn"](i - 3))
                pool.tensor_tensor(neigh[:, slot, :, 0:D], sums[:, slot, :, 0:D], xin[:, slot, :, :], ALU.add)\
                    .then_inc(s["total"].sem, 1)

            def scale(phase, layer):
                s = node_s[phase]

                def stage(i, q, slot):
                    held(*s["unit"](i + 1))
                    pool.tensor_tensor(aff[:, slot, :, :], aff[:, slot, :, :],
                                       g3[:, layer:layer + 1, :].to_broadcast([P, K, D]), ALU.mult).then_inc(s["scaled"].sem, 1)
                return stage

            edges("l0a")
            pipeline(pool, GROUPS, 4, [(join("d0"), 6)])
            edges("l0b")
            pipeline(pool, GROUPS, 4, [(power("d1", 0, "var", "rstd"), 10), (join("d1"), 7), (add_self, 1)])
            edges("l1")
            pipeline(pool, GROUPS, 4, [(power("d2a", 0, "var", "rstd"), 6)])
            edges("l2")
            pipeline(pool, GROUPS, 4, [(power("d2b", 0, "var", "rstd"), 9), (power("d2b", 1, "hst", "hrs"), 4)])
            edges("l3a")
            pipeline(pool, GROUPS, 4, [(scale("d3a", 0), 8), (power("d3a", 0, "var", "rstd"), 6)])
            edges("l3b")
            pipeline(pool, GROUPS, 4, [(power("d3b", 2, "o2", "rstd2"), 10), (scale("d3b", 1), 8), (power("d3b", 0, "var", "rstd"), 6)])

        @block.vector
        def _(dve):
            dve.memset(src_i[:, STEPS - 1, :], 0)
            dve.memset(dst_i[:, STEPS - 1, :], 0)
            dve.memset(type_i[:, STEPS - 1, :], 0)
            dve.memset(weight[:, STEPS - 1, :], 0.0)
            dve.memset(bias3[:, :], 0.0)
            dve.memset(bm4[:, :], 0.0)
            dve.memset(zeros[:, :], 0.0)
            dve.memset(brow[:, :, :], 0.0)
            dve.drain().then_inc(s_cdve, 1)
            dve.memset(ones_bf[:, :], 1.0)
            dve.memset(msg[:, :, :, D:WIDE], 0.0)
            dve.memset(xin[:, :, :, :], 0.0)
            dve.memset(xres[:, :, :, :], 0.0)
            dve.memset(neigh[:, :, :, D:WIDE], 0.0)
            dve.drain()
            dve.memset(msg[:, :, :, D:D + 1], 1.0)
            dve.memset(neigh[:, :, :, D + 1:D + 2], 1.0)
            dve.drain().then_inc(s_cdve, 1)

            dve.wait_ge(s_win, 16 * len(small_loads))
            dve.tensor_tensor(brow[:, 0, :], brow[:, 0, :], brow[:, 1, :], ALU.add)
            dve.tensor_tensor(b_l0b[:, :], col3[:, 0:1], col3[:, 1:2], ALU.add)
            dve.drain()
            dve.tensor_tensor(brow[:, 0, :], brow[:, 0, :], brow[:, 2, :], ALU.add)
            dve.tensor_tensor(b_l0b[:, :], b_l0b[:, :], col3[:, 2:3], ALU.add)
            dve.drain()
            dve.tensor_scalar(b_below[:, :], b_l0b[:, :], -SLOPE, None, ALU.mult)
            for i in range(3):
                dve.tensor_copy(bparts[:, i, :], brow[:, i % 2, :])
                dve.drain()
                if i < 2:
                    dve.tensor_tensor(brow[:, (i + 1) % 2, :], brow[:, i % 2, :], bparts[:, i, :], ALU.subtract)
                    dve.drain()
            dve.drain().then_inc(s_bpart, 1)

            dve.wait_ge(s_eload, 128)
            dve.tensor_copy(src_f[:, :, :], src_i[:, :, :])
            dve.tensor_copy(dst_f[:, :, :], dst_i[:, :, :])
            dve.drain()

            dve.wait_ge(s_rel_in, 16)
            dve.tensor_tensor(rel_sq[:, :, :], rel_in[:, :, :], rel_in[:, :, :], ALU.mult)
            dve.drain()
            dve.reduce_sum(rel_ss[:, :], rel_sq[:, :, :], axis=AX_X).then_inc(s_relss, 1)
            dve.wait_ge(s_relnm, 1)
            dve.tensor_scalar(rel_ss[:, :], rel_nm[:, :], 1e-6, None, ALU.max)
            dve.drain()
            dve.reciprocal(rel_nm[:, :], rel_ss[:, :])
            dve.drain()
            dve.tensor_tensor(rel_in[:, :, :], rel_in[:, :, :],
                              rel_nm[:, :].rearrange("p (r a) -> p r a", a=1).to_broadcast([91, 11, D]), ALU.mult)\
               .then_inc(s_relok, 1)

            dve.wait_ge(s_comb, 1)
            dve.tensor_copy(w_c1[:, :], ps[:, 0, 0:D])
            dve.tensor_copy(w_c2[:, :], ps[:, 1, 0:D])
            dve.tensor_tensor(bmrow[0:1, 1, :], ps[0:1, 2, 0:D], brow_upd[:, :], ALU.add)
            dve.tensor_copy(bmrow[0:1, 0, :], ps[0:1, 3, 0:D])
            dve.drain().then_inc(s_bm, 1)
            dve.wait_ge(s_const, 7)

            def edges(name):
                s = edge_s[name]
                node_f = src_f if name == "l1" else dst_f
                put_i = put_src if name == "l1" else put_dst
                index = name in ("l0a", "l1")
                gathered = {"l2": 0, "l3a": 128}.get(name, 64)

                def compare(i, q, slot):
                    dve.wait_ge(*s[f"ids{slot}"](16 * (q + 1)))
                    if later(i, 2):
                        dve.wait_ge(*s["merge"](i - 1))
                    if isinstance(i, int) and i == STEPS - 1:
                        dve.memset(ids[:, slot, E - i * ROWS:ROWS], -1)
                        dve.drain()
                    for k in range(K):
                        dve.tensor_scalar(same[:, slot, k, :], ids[:, slot, :],
                                          node_f[:, bass.ds(i, 1), k:k + 1].rearrange("p a k -> p (a k)"), None, ALU.is_equal)
                    dve.drain().then_inc(s["same"].sem, 1)
                    if not index:
                        return
                    for k in range(K):
                        dve.tensor_tensor_reduce(out=hit[:, :], in0=same[:, slot, k, :], in1=rev[:, :], scale=1.0, scalar=0.0,
                                                 op0=ALU.mult, op1=ALU.max, accum_out=first4[:, slot, k:k + 1])
                        dve.drain()
                    dve.tensor_tensor(sel4[:, 0, :], first4[:, slot, :], rev_own[:, :], ALU.is_equal)
                    dve.tensor_tensor(sel4[:, 1, :], node_f[:, bass.ds(i, 1), :].rearrange("p a k -> p (a k)"), trash[:, :], ALU.subtract)
                    dve.drain()
                    dve.tensor_tensor(sel4[:, 2, :], sel4[:, 0, :], sel4[:, 1, :], ALU.mult)
                    dve.drain()
                    dve.tensor_tensor(put_i[:, bass.ds(i, 1), :].rearrange("p a k -> p (a k)"), sel4[:, 2, :], trash[:, :], ALU.add)
                    dve.drain()

                def message(i, q, slot):
                    if name != "l2":
                        dve.wait_ge(*s[f"got{slot}"](gathered * (q + 1)))
                    if name in ("l2", "l3b"):
                        dve.wait_ge(*s[f"keep{slot}"](16 * (q + 1)))
                    if later(i, 2):
                        dve.wait_ge(*s["merge"](i - 1))
                    if name in ("l0a", "l0b"):
                        for k in range(K):
                            dve.tensor_scalar(msg[:, slot, k, 0:D], got[:, slot, k, :],
                                              weight[:, bass.ds(i, 1), k:k + 1].rearrange("p a k -> p (a k)"), None, ALU.mult)
                    elif name in ("l1", "l2"):
                        dve.tensor_copy(msg[:, slot, :, 0:D], got[:, slot, :, :])
                    else:
                        for k in range(K):
                            dve.tensor_tensor_reduce(out=prod[:, :], in0=got[:, slot, k, :], in1=rel[:, slot, k, :], scale=-2.0,
                                                     scalar=0.0, op0=ALU.mult, op1=ALU.add, accum_out=dot4[:, slot, k:k + 1])
                            dve.drain()
                        for k in range(K):
                            dve.scalar_tensor_tensor(out=msg[:, slot, k, 0:D], in0=rel[:, slot, k, :], scalar=dot4[:, slot, k:k + 1],
                                                     in1=got[:, slot, k, :], op0=ALU.mult, op1=ALU.add)
                    dve.drain().then_inc(s["msg"].sem, 1)

                pipeline(dve, STEPS, 2, [(compare, 0), (message, 0)])

            def row_stats(i, n, slot, rows, done):
                for k in range(K):
                    dve.bn_stats(stat[:, n, k, :], rows[:, k, :])
                dve.drain()
                for k in range(K):
                    dve.bn_aggr(mv[:, n, slot, k, :], stat[:, n, k, :])
                dve.drain()
                dve.tensor_scalar(negmean[:, n, slot, :], mv[:, n, slot, :, 0:1].rearrange("p k a -> p (k a)"), -1.0, None, ALU.mult)
                dve.tensor_scalar(vare[:, n, slot, :], mv[:, n, slot, :, 1:2].rearrange("p k a -> p (k a)"), EPS, None, ALU.add)\
                   .then_inc(done.sem, 1)

            def loaded(s, q, slot, count, name="in"):
                dve.wait_ge(*s[f"{name}{slot}"](16 * count * (q + 1)))

            def rows_of(bank):
                return ps[:, bank, :].rearrange("p (k d) -> p k d", k=K)

            def per_row(table, i):
                return table[:, bass.ds(i, 1), :].rearrange("p a k -> p k a").to_broadcast([P, K, D])

            def copy_nT(s, bank=2, slots=2):
                def stage(i, q, slot):
                    dve.wait_ge(*s["tn"](i + 1))
                    if later(i, 2):
                        dve.wait_ge(*s["mm"](i - 1))
                    dve.tensor_copy(nT[:, slot % 2, :], ps[:, bank + slot % slots, :]).then_inc(s["nT"].sem, 1)
                return stage

            def d0():
                s = node_s["d0"]

                def average(i, q, slot):
                    loaded(s, q, slot, 2)
                    if later(i, 4):
                        dve.wait_ge(*s["tn"](i - 3))
                    c = cnt4[:, slot % 2, :, :]
                    count = sums[:, slot, :, D:D + 1].rearrange("p k a -> p (k a)")
                    dve.tensor_scalar(c[:, 0, :], count, 1.0, None, ALU.add)
                    dve.tensor_scalar(c[:, 1, :], count, 1.0, None, ALU.max)
                    dve.tensor_tensor(neigh[:, slot, :, 0:D], sums[:, slot, :, 0:D], xin[:, slot, :, :], ALU.add)
                    dve.drain()
                    dve.reciprocal(inv_l0[:, bass.ds(i, 1), :].rearrange("p a k -> p (a k)"), c[:, 0, :])
                    dve.reciprocal(inv_l3[:, bass.ds(i, 1), :].rearrange("p a k -> p (a k)"), c[:, 1, :])
                    dve.drain()
                    dve.tensor_tensor(neigh[:, slot, :, 0:D], neigh[:, slot, :, 0:D], per_row(inv_l0, i), ALU.mult)\
                       .then_inc(s["neigh"].sem, 1)

                pipeline(dve, GROUPS, 4, [(copy_nT(s), 3), (average, 1)])

            def d1():
                s = node_s["d1"]

                def average(i, q, slot):
                    dve.wait_ge(*s["total"](i + 1))
                    dve.tensor_tensor(neigh[:, slot, :, 0:D], neigh[:, slot, :, 0:D], per_row(inv_l0, i), ALU.mult)\
                       .then_inc(s["neigh"].sem, 1)

                def residual(i, q, slot):
                    dve.wait_ge(*s["y"](i + 1))
                    loaded(s, q, slot, 1, "ra")
                    if later(i, 4):
                        dve.wait_ge(*s["norm"](i - 3))
                    dve.tensor_tensor(res[:, slot, :, :], rows_of(6 + slot % 2), xres[:, slot, :, :], ALU.add)
                    dve.drain().then_inc(s["res"].sem, 1)
                    row_stats(i, 0, slot, res[:, slot, :, :], s["var"])

                pipeline(dve, GROUPS, 4, [(residual, 9), (copy_nT(s), 4), (average, 2)])

            def d2a():
                s = node_s["d2a"]

                def average(i, q, slot):
                    loaded(s, q, slot, 2)
                    if later(i, 4):
                        dve.wait_ge(*s["tn"](i - 3))
                    c = cnt4[:, slot % 2, :, :]
                    count = sums[:, slot, :, D:D + 1]
                    dve.tensor_scalar(c[:, 0, :], count.rearrange("p k a -> p (k a)"), 1.0, None, ALU.max)
                    dve.tensor_scalar(neigh[:, slot, :, D:D + 1], count, 1.0, None, ALU.min)
                    dve.drain()
                    dve.reciprocal(c[:, 1, :], c[:, 0, :])
                    dve.drain()
                    dve.tensor_tensor(neigh[:, slot, :, 0:D], sums[:, slot, :, 0:D],
                                      c[:, 1, :].rearrange("p (k a) -> p k a", a=1).to_broadcast([P, K, D]), ALU.mult)\
                       .then_inc(s["neigh"].sem, 1)

                def residual(i, q, slot):
                    dve.wait_ge(*s["mm"](i + 1))
                    loaded(s, q, slot, 1, "ra")
                    if later(i, 4):
                        dve.wait_ge(*s["norm"](i - 3))
                    dve.scalar_tensor_tensor(out=res[:, slot, :, :], in0=rows_of(4 + slot % 2), scalar=0.0,
                                             in1=xres[:, slot, :, :], op0=ALU.max, op1=ALU.add)
                    dve.drain().then_inc(s["res"].sem, 1)
                    row_stats(i, 0, slot, res[:, slot, :, :], s["var"])

                pipeline(dve, GROUPS, 4, [(residual, 5), (copy_nT(s), 3), (average, 1)])

            def d2b():
                s = node_s["d2b"]
                hrows = ps[:, 2:4, :].rearrange("p b (j d) -> p (b j) d", j=2)

                def hidden_stats(i, q, slot):
                    dve.wait_ge(*s["mm"](i + 1))
                    row_stats(i, 1, slot, hrows, s["hst"])

                def hidden_norm(i, q, slot):
                    dve.wait_ge(*s["hrs"](i + 1))
                    if later(i, 1):
                        dve.wait_ge(*s["th"](i))
                    for k in range(K):
                        dve.tensor_scalar(hid[:, k, :], hrows[:, k, :], mv[:, 1, slot, k, 0:1],
                                          rstd[:, 1, slot, k:k + 1], ALU.subtract, ALU.mult)
                    dve.drain().then_inc(s["hn"].sem, 1)

                def residual(i, q, slot):
                    dve.wait_ge(*s["o"](i + 1))
                    loaded(s, q, slot, 1, "ra")
                    if later(i, 4):
                        dve.wait_ge(*s["norm"](i - 3))
                    dve.scalar_tensor_tensor(out=res[:, slot, :, :], in0=xres[:, slot, :, :], scalar=2.0,
                                             in1=rows_of(6 + slot % 2), op0=ALU.mult, op1=ALU.add)
                    dve.drain().then_inc(s["res"].sem, 1)
                    row_stats(i, 0, slot, res[:, slot, :, :], s["var"])

                pipeline(dve, GROUPS, 4, [(hidden_stats, 4), (copy_nT(s, 1, 1), 2), (residual, 8), (hidden_norm, 4)])

            def d3(phase, layer):
                s = node_s[phase]

                def average(i, q, slot):
                    loaded(s, q, slot, 1)
                    if later(i, 4):
                        dve.wait_ge(*s["tn"](i - 3))
                    dve.tensor_tensor(neigh[:, slot, :, 0:D], sums[:, slot, :, 0:D], per_row(inv_l3, i), ALU.mult)\
                       .then_inc(s["neigh"].sem, 1)

                def residual(i, q, slot):
                    dve.wait_ge(*s["mm"](i + 1))
                    loaded(s, q, slot, 1, "ra")
                    if later(i, 4):
                        dve.wait_ge(*s["unit"](i - 3))
                    dve.tensor_tensor(res[:, slot, :, :], rows_of(4 + slot % 2), xin[:, slot, :, :], ALU.add)
                    dve.drain().then_inc(s["res"].sem, 1)
                    row_stats(i, 0, slot, res[:, slot, :, :], s["var"])

                def add_beta(i, q, slot):
                    dve.wait_ge(*s["scaled"](i + 1))
                    if layer:
                        loaded(s, q, slot, 1, "rb")
                    a = aff[:, slot, :, :]
                    dve.tensor_tensor(a, a, b3[:, layer:layer + 1, :].to_broadcast([P, K, D]), ALU.add)
                    if not layer:
                        dve.drain().then_inc(s["norm"].sem, 1)
                        return
                    dve.drain()
                    dve.tensor_tensor(a, a, xres[:, slot, :, :], ALU.add)
                    dve.drain().then_inc(s["res2"].sem, 1)
                    row_stats(i, 2, slot, a, s["o2"])

                def last_norm(i, q, slot):
                    dve.wait_ge(*s["rstd2"](i + 1))
                    if later(i, 4):
                        dve.wait_ge(*s[f"st{slot}"](16 * q))
                    for k in range(K):
                        dve.tensor_scalar(xout[:, slot, k, :], aff[:, slot, k, :], mv[:, 2, slot, k, 0:1],
                                          rstd[:, 2, slot, k:k + 1], ALU.subtract, ALU.mult)
                    dve.drain().then_inc(s["norm"].sem, 1)

                pipeline(dve, GROUPS, 4, ([(last_norm, 11)] if layer else []) + [(add_beta, 9), (residual, 5), (average, 1)])

            edges("l0a")
            d0()
            edges("l0b")
            d1()
            edges("l1")
            d2a()
            edges("l2")
            d2b()
            edges("l3a")
            d3("d3a", 0)
            edges("l3b")
            d3("d3b", 1)

        @block.scalar
        def _(act):
            act.wait_ge(s_cdve, 1)

            def clear(name):
                for n, dst, src in zero_jobs:
                    if n == name:
                        act.dma_start(dst, src).then_inc(s_zero[n], 16)

            def norm(phase, dest, done, free):
                s = node_s[phase]

                def stage(i, q, slot):
                    act.wait_ge(*s["rstd"](i + 1))
                    if later(i, 4):
                        if free:
                            act.wait_ge(*s[free](i - 3))
                        else:
                            act.wait_ge(*s[f"st{slot}"](16 * q))
                    for k in range(K):
                        last = act.activation(dest[:, slot, k, :], res[:, slot, k, :], ACT.Identity, bias=shift[:, 0, slot, k:k + 1],
                                              scale=rstd[:, 0, slot, k:k + 1])
                    last.then_inc(s[done].sem, 1)
                return stage

            clear("l0a")

            def edges(name):
                s = edge_s[name]
                w = sum_d[name].shape[1]

                def evacuate(i, q, slot):
                    act.wait_ge(*s["merge"](i + 1))
                    if later(i, 2):
                        act.wait_ge(*s["put"](64 * (i - 1)))
                    act.activation(merged[:, slot, :, 0:w],
                                   ps[:, 2 * slot:2 * slot + 2, :].rearrange("p b (j d) -> p (b j) d", j=2)[:, :, 0:w],
                                   ACT.Copy).then_inc(s["evac"].sem, 1)

                pipeline(act, STEPS, 2, [(evacuate, 0)])

            def copy_xT(s, bank, wide):
                def stage(i, q, slot):
                    act.wait_ge(*s["tx"](i + 1))
                    if later(i, 2):
                        act.wait_ge(*s["mm"](i - 1))
                    act.activation(xT[:, slot % 2, :], ps[:, bank + (slot % 2 if wide else 0), :], ACT.Copy).then_inc(s["xT"].sem, 1)
                return stage

            def d0():
                s = node_s["d0"]

                def leaky(i, q, slot):
                    act.wait_ge(*s["mm"](i + 1))
                    if later(i, 2):
                        act.wait_ge(*s["norm"](i - 1))
                    act.activation(above[:, slot % 2, :], ps[:, 4 + slot % 2, :], ACT.Relu)
                    act.activation(below[:, slot % 2, :], ps[:, 4 + slot % 2, :], ACT.Relu, scale=-SLOPE).then_inc(s["act"].sem, 1)

                pipeline(act, GROUPS, 4, [(leaky, 5), (copy_xT(s, 0, True), 3)])

            def d1():
                s = node_s["d1"]

                def leaky(i, q, slot):
                    act.wait_ge(*s["mm"](i + 1))
                    if later(i, 2):
                        act.wait_ge(*s["x2"](i - 1))
                    act.activation(above[:, slot % 2, :], ps[:, 4 + slot % 2, :], ACT.Relu, bias=b_l0b[:, :])
                    act.activation(below[:, slot % 2, :], ps[:, 4 + slot % 2, :], ACT.Relu, bias=b_below[:, :], scale=-SLOPE)\
                       .then_inc(s["act"].sem, 1)

                pipeline(act, GROUPS, 4, [(norm("d1", xout, "norm", None), 11), (leaky, 6), (copy_xT(s, 0, True), 4)])

            def d2a():
                s = node_s["d2a"]

                def copy_fT(i, q, slot):
                    act.wait_ge(*s["tn"](i + 1))
                    if later(i, 2):
                        act.wait_ge(*s["mm"](i - 1))
                    act.activation(fT[:, slot % 2, :], ps[0:4, 6 + slot % 2, :], ACT.Copy).then_inc(s["xT"].sem, 1)

                def copy_x(i, q, slot):
                    act.wait_ge(*s["tx"](i + 1))
                    if later(i, 2):
                        act.wait_ge(*s["mm"](i - 1))
                    act.activation(xT[:, slot % 2, :], ps[:, slot % 2, :], ACT.Copy).then_inc(s["xT"].sem, 1)

                pipeline(act, GROUPS, 4, [(norm("d2a", xout, "norm", None), 7), (copy_x, 3), (copy_fT, 3)])

            def d2b():
                s = node_s["d2b"]

                def silu(i, q, slot):
                    act.wait_ge(*s["th"](i + 1))
                    if later(i, 2):
                        act.wait_ge(*s["o"](i - 1))
                    for h in range(2):
                        last = act.activation(hidT[:, slot % 2, h, :], ps[:, 4 + h, :], ACT.Silu, bias=ln_b[:, h:h + 1], scale=ln_g[:, h:h + 1])
                    last.then_inc(s["hT"].sem, 1)

                pipeline(act, GROUPS, 4, [(norm("d2b", xout, "norm", None), 10), (silu, 6), (copy_xT(s, 0, False), 2)])

            def d3(phase, layer):
                s = node_s[phase]

                def copy_n(i, q, slot):
                    act.wait_ge(*s["tn"](i + 1))
                    if later(i, 2):
                        act.wait_ge(*s["mm"](i - 1))
                    act.activation(nT[:, slot % 2, :], ps[:, 2 + slot % 2, :], ACT.Copy).then_inc(s["nT"].sem, 1)

                def relu(i, q, slot):
                    act.wait_ge(*s["norm"](i + 1))
                    if later(i, 4):
                        act.wait_ge(*s[f"st{slot}"](16 * q))
                    act.activation(xout[:, slot, :, :], aff[:, slot, :, :], ACT.Relu).then_inc(s["act"].sem, 1)

                pipeline(act, GROUPS, 4, ([] if layer else [(relu, 10)]) +
                         [(norm(phase, aff, "unit", "norm" if layer else "act"), 7), (copy_n, 3)])

            act.wait_ge(s_win, 16 * len(small_loads))
            clear("l0b")
            edges("l0a")
            clear("l1")
            d0()
            clear("l2")
            edges("l0b")
            clear("l3a")
            d1()
            clear("l3b")
            edges("l1")
            d2a()
            edges("l2")
            d2b()
            edges("l3a")
            d3("d3a", 0)
            edges("l3b")
            d3("d3b", 1)

        @block.tensor
        def _(pe):
            pe.wait_ge(s_win, 16 * len(small_loads))
            pe.matmul(ps[:, 0, 0:D], w_linT[:, :], w_upd[:, 0, :], start=True, stop=True)
            pe.matmul(ps[:, 1, 0:D], w_msgT[:, :], w_upd[:, 1, :], start=True, stop=True)
            pe.matmul(ps[0:1, 2, 0:D], b_lin[:, :], w_upd[:, 0, :], start=True, stop=True)
            pe.matmul(ps[0:1, 3, 0:D], b_msg[:, :], w_upd[:, 1, :], start=True, stop=True).then_inc(s_comb, 1)
            pe.wait_ge(s_bm, 1)
            pe.wait_ge(s_brow, 16 * 5)
            pe.wait_ge(s_const, 7)
            pe.wait_ge(s_cdve, 2)

            def edges(name):
                s = edge_s[name]
                w = sum_d[name].shape[1]

                def merge(i, q, slot):
                    pe.wait_ge(*s["same"](i + 1))
                    pe.wait_ge(*s["msg"](i + 1))
                    if later(i, 2):
                        pe.wait_ge(*s["evac"](i - 1))
                    for k in range(K):
                        for j in range(K):
                            last = pe.matmul(ps[:, 2 * slot + k // 2, (k % 2) * 256:(k % 2) * 256 + w], same[:, slot, j, k:ROWS:K],
                                             msg[:, slot, j, 0:w], start=(j == 0), stop=(j == K - 1), skip_group_check=True)
                    last.then_inc(s["merge"].sem, 1)

                pipeline(pe, STEPS, 2, [(merge, 0)])

            def transposes(s, bank, rows, loaded_count, free, done, wide=True):
                def stage(i, q, slot):
                    if loaded_count:
                        pe.wait_ge(*s[f"in{slot}"](16 * loaded_count * (q + 1)))
                    else:
                        pe.wait_ge(*s["neigh"](i + 1))
                    behind = 2 if wide else 1
                    if later(i, behind):
                        for name, per in free:
                            pe.wait_ge(*s[name](per * (i - behind + 1)))
                    for k in range(K):
                        last = pe.transpose(ps[:, bank + (slot % 2 if wide else 0), k * P:(k + 1) * P], rows(slot)[:, k, 0:D], ident[:, :])
                    last.then_inc(s[done].sem, 1)
                return stage

            def bias(bank, lo, n, width):
                pe.matmul(ps[:, bank, 0:ROWS], ones_bf[:, :],
                          bias3[:, lo:lo + width].rearrange("p (a d) -> p a d", a=1).to_broadcast([P, n, width]),
                          start=True, stop=False, skip_group_check=True)

            def d0():
                s = node_s["d0"]

                def products(i, q, slot):
                    pe.wait_ge(*s["xT"](i + 1))
                    pe.wait_ge(*s["nT"](i + 1))
                    if later(i, 2):
                        pe.wait_ge(*s["act"](i - 1))
                    b = 4 + slot % 2
                    bias(b, BL0, K, D)
                    for k in range(K):
                        c = slice(k * P, (k + 1) * P)
                        pe.matmul(ps[:, b, c], xT[:, slot % 2, c], w_self[:, 0, :], start=False, stop=False, skip_group_check=True)
                        last = pe.matmul(ps[:, b, c], nT[:, slot % 2, c], w_neigh[:, 0, :], start=False, stop=(k == K - 1),
                                         skip_group_check=True)
                    last.then_inc(s["mm"].sem, 1)

                pipeline(pe, GROUPS, 4, [(products, 4), (transposes(s, 0, lambda c: xin[:, c, :, :], 2, [("xT", 1)], "tx"), 2),
                                         (transposes(s, 2, lambda c: neigh[:, c, :, :], 0, [("nT", 1)], "tn"), 2)])

            def d1():
                s = node_s["d1"]

                def products(i, q, slot):
                    pe.wait_ge(*s["xT"](i + 1))
                    pe.wait_ge(*s["nT"](i + 1))
                    if later(i, 2):
                        pe.wait_ge(*s["act"](i - 1))
                    b = 4 + slot % 2
                    pe.matmul(ps[:, b, :], w_self[:, 1, :], xT[:, slot % 2, :], start=True, stop=False)
                    pe.matmul(ps[:, b, :], w_neigh[:, 1, :], nT[:, slot % 2, :], start=False, stop=True).then_inc(s["mm"].sem, 1)

                def final(i, q, slot):
                    pe.wait_ge(*s["x2"](i + 1))
                    if later(i, 2):
                        pe.wait_ge(*s["res"](i - 1))
                    b = 6 + slot % 2
                    bias(b, BAGG, K, D)
                    for k in range(K):
                        c = slice(k * P, (k + 1) * P)
                        last = pe.matmul(ps[:, b, c], x2T[:, slot % 2, c], w_agg[:, :], start=False, stop=(k == K - 1), skip_group_check=True)
                    last.then_inc(s["y"].sem, 1)

                pipeline(pe, GROUPS, 4, [(final, 8), (products, 5),
                                         (transposes(s, 0, lambda c: xin[:, c, :, :], 2, [("xT", 1)], "tx"), 3),
                                         (transposes(s, 2, lambda c: neigh[:, c, :, :], 0, [("nT", 1)], "tn"), 3)])

            def d2a():
                s = node_s["d2a"]

                def turn_sums(i, q, slot):
                    pe.wait_ge(*s["neigh"](i + 1))
                    if later(i, 2):
                        pe.wait_ge(*s["nT"](i - 1))
                        pe.wait_ge(*s["xT"](2 * (i - 1)))
                    for k in range(K):
                        c = slice(k * P, (k + 1) * P)
                        pe.transpose(ps[:, 2 + slot % 2, c], neigh[:, slot, k, 0:D], ident[:, :])
                        last = pe.transpose(ps[0:4, 6 + slot % 2, c], neigh[:, slot, k, D:WIDE], ident[:, :])
                    last.then_inc(s["tn"].sem, 1)

                def products(i, q, slot):
                    pe.wait_ge(*s["xT"](2 * (i + 1)))
                    pe.wait_ge(*s["nT"](i + 1))
                    if later(i, 2):
                        pe.wait_ge(*s["res"](i - 1))
                    for k in range(K):
                        c = slice(k * P, (k + 1) * P)
                        o = ps[:, 4 + slot % 2, c]
                        pe.matmul(o, xT[:, slot % 2, c], w_c1[:, :], start=True, stop=False, skip_group_check=True)
                        pe.matmul(o, nT[:, slot % 2, c], w_c2[:, :], start=False, stop=False, skip_group_check=True)
                        last = pe.matmul(o, fT[:, slot % 2, c], bm4[:, :], start=False, stop=True, skip_group_check=True)
                    last.then_inc(s["mm"].sem, 1)

                pipeline(pe, GROUPS, 4, [(products, 4), (transposes(s, 0, lambda c: xin[:, c, :, :], 2, [("xT", 2)], "tx"), 2),
                                         (turn_sums, 2)])

            def d2b():
                s = node_s["d2b"]

                def products(i, q, slot):
                    pe.wait_ge(*s["xT"](i + 1))
                    pe.wait_ge(*s["nT"](i + 1))
                    if later(i, 1):
                        pe.wait_ge(*s["hn"](i))
                    for b in range(2):
                        bias(2 + b, BH, 2, HID)
                        for j in range(2):
                            k = 2 * b + j
                            c = slice(k * P, (k + 1) * P)
                            o = ps[:, 2 + b, j * HID:(j + 1) * HID]
                            pe.matmul(o, xT[:, slot % 2, c], w_h[:, 0, :], start=False, stop=False, skip_group_check=True)
                            last = pe.matmul(o, nT[:, slot % 2, c], w_h[:, 1, :], start=False, stop=(j == 1), skip_group_check=True)
                    last.then_inc(s["mm"].sem, 1)

                def turn_hidden(i, q, slot):
                    pe.wait_ge(*s["hn"](i + 1))
                    if later(i, 1):
                        pe.wait_ge(*s["hT"](i))
                    for h in range(2):
                        for k in range(K):
                            last = pe.transpose(ps[:, 4 + h, k * P:(k + 1) * P], hid[:, k, h * P:(h + 1) * P], ident[:, :])
                    last.then_inc(s["th"].sem, 1)

                def last_products(i, q, slot):
                    pe.wait_ge(*s["hT"](i + 1))
                    if later(i, 2):
                        pe.wait_ge(*s["res"](i - 1))
                    b = 6 + slot % 2
                    bias(b, BO, K, D)
                    for k in range(K):
                        c = slice(k * P, (k + 1) * P)
                        for h in range(2):
                            last = pe.matmul(ps[:, b, c], hidT[:, slot % 2, h, c], w_o[:, h, :], start=False,
                                             stop=(k == K - 1 and h == 1), skip_group_check=True)
                    last.then_inc(s["o"].sem, 1)

                pipeline(pe, GROUPS, 4, [(last_products, 7), (turn_hidden, 5),
                                         (transposes(s, 0, lambda c: xin[:, c, :, :], 2, [("xT", 1)], "tx", False), 1),
                                         (transposes(s, 1, lambda c: sums[:, c, :, :], 2, [("nT", 1)], "tn", False), 1),
                                         (products, 3)])

            def d3(phase, layer):
                s = node_s[phase]

                def products(i, q, slot):
                    pe.wait_ge(*s["nT"](i + 1))
                    if later(i, 2):
                        pe.wait_ge(*s["res"](i - 1))
                    for k in range(K):
                        c = slice(k * P, (k + 1) * P)
                        last = pe.matmul(ps[:, 4 + slot % 2, c], nT[:, slot % 2, c], w_r[:, layer, :], start=True, stop=True,
                                         skip_group_check=True)
                    last.then_inc(s["mm"].sem, 1)

                pipeline(pe, GROUPS, 4, [(products, 4), (transposes(s, 2, lambda c: neigh[:, c, :, :], 0, [("nT", 1)], "tn"), 2)])

            edges("l0a")
            d0()
            edges("l0b")
            d1()
            edges("l1")
            d2a()
            edges("l2")
            d2b()
            edges("l3a")
            d3("d3a", 0)
            edges("l3b")
            d3("d3b", 1)


_TURNED = ("L0_gnn_W_self", "L0_gnn_W_neigh", "L0_gnn_W_agg", "L1_gnn_W_lin", "L1_gnn_W_msg", "L3_gnn_W1", "L3_gnn_W2")


def kernel(**inputs):
    import numpy as _np
    import concourse.bacc as _bacc
    from concourse import mybir as _mybir
    from concourse.bass_utils import run_bass_kernel_spmd as _run

    nc = _bacc.Bacc("TRN2", target_bir_lowering=False, num_devices=1)
    arrays, tensors = {}, {}
    for name, value in inputs.items():
        a = _np.asarray(value)
        if name in _TURNED:
            a = _np.swapaxes(a, -1, -2)
        a = _np.ascontiguousarray(a)
        arrays[f"in_{name}"] = a
        tensors[name] = nc.dram_tensor(f"in_{name}", a.shape, _mybir.dt.from_np(a.dtype), kind="ExternalInput").ap()
    out = nc.dram_tensor("out_0", (N, D), F32, kind="ExternalOutput").ap()
    program(nc, tensors, out)
    r = _run(nc, [arrays], core_ids=[0])
    return r.results[0]["out_0"]
```

```python
from contextlib import ExitStack

import concourse.bass as bass
from concourse import mybir

F32 = mybir.dt.float32
BF16 = mybir.dt.bfloat16
I32 = mybir.dt.int32
ALU = mybir.AluOpType
ACT = mybir.ActivationFunctionType
AX_X = mybir.AxisListType.X

P = 128
D = 128
N = 50000
E = 25000
NREL = 1001
HID = 256
K = 4
ROWS = K * P
GROUPS = -(-N // ROWS)
STEPS = -(-E // ROWS)
LAST_NODES = (N - (GROUPS - 1) * ROWS) // K
LAST_EDGES = (E - (STEPS - 1) * ROWS) // K
TRASH = N
WIDE = 132
TABLE = 99 * ROWS
XROWS = GROUPS * ROWS
SLOPE = 0.2
EPS = 1e-5
SETTLE = None


def pipeline(engine, n, unroll, stages, tail=1):
    ahead = min(item[1] for item in stages if item)
    stages = [item and (item[0], item[1] - ahead) for item in stages]
    lag_max = max(item[1] for item in stages if item)
    body = 2 * unroll
    first = -(-(lag_max + 4) // body) * body
    end = (n - tail) // body * body

    def step(j, u):
        for item in stages:
            if item is SETTLE:
                engine.drain()
                continue
            stage, lag = item
            slot = (u - lag) % unroll
            q = j + (u - lag - slot) // unroll
            i = q * unroll + slot
            if not isinstance(i, int) or 0 <= i < n:
                stage(i, q, slot)

    for t in range(first):
        step(t // unroll, t % unroll)
    with engine.Fori(first // body, end // body) as j:
        for u in range(body):
            step(2 * j + u // unroll, u % unroll)
    for t in range(end, n + lag_max):
        step(t // unroll, t % unroll)


def in_pairs(stage):
    def paired(i, q, slot):
        if slot % 2 == 0:
            stage(2 * q + slot // 2, q, slot // 2)
    return paired


def later(i, behind):
    return not isinstance(i, int) or i >= behind


def program(nc, t, out):
    ctx = ExitStack()
    with ctx:
        def sb(name, shape, dt=F32):
            return ctx.enter_context(nc.sbuf_tensor(name, shape, dt))

        def sem(name):
            return ctx.enter_context(nc.semaphore(name))

        def dram(name, shape, dt=F32):
            return nc.dram_tensor(name, shape, dt).ap()

        x1_d, self_d, xa_d, own_d, xb_d, xc_d, x5_d = (dram(f"nodes_{n}", (XROWS, D))
                                                       for n in ("l0", "self", "a", "own", "b", "c", "l3"))
        sum_d = {n: dram(f"sums_{n}", (TABLE, w)) for n, w in
                 (("l0a", WIDE), ("l2", D), ("l0b", D), ("l1", WIDE), ("l3a", D), ("l3b", D))}
        rel_d = dram("rel_unit", (NREL, D))
        rel_edge_d = dram("rel_of_edges", (STEPS * ROWS, D))

        ident = sb("ident", [P, P])
        zeros = sb("zeros", [P, K * WIDE])
        neg_half = sb("neg_half", [P, 4])
        pos_half = sb("pos_half", [P, 11])
        ones_bf = sb("ones_bf", [P, P], BF16)
        rev = sb("rev", [P, ROWS])
        rev_own = sb("rev_own", [P, K])
        trash = sb("trash", [P, K])
        w_self = sb("w_self", [P, 2, D])
        w_neigh = sb("w_neigh", [P, 2, D])
        w_agg = sb("w_agg", [P, D])
        w_linT = sb("w_linT", [P, D])
        w_msgT = sb("w_msgT", [P, D])
        w_upd = sb("w_upd", [P, 2, D])
        w_c1 = sb("w_c1", [P, D])
        w_c2 = sb("w_c2", [P, D])
        w_h = sb("w_h", [P, 2, HID])
        w_o = sb("w_o", [P, 2, D])
        w_r = sb("w_r", [P, 2, D])
        b_lin = sb("b_lin", [P, 1])
        b_msg = sb("b_msg", [P, 1])
        col3 = sb("col3", [P, 3])
        b_l0b = sb("b_l0b", [P, 1])
        b_below = sb("b_below", [P, 1])
        ln_g = sb("ln_g", [P, 2])
        ln_b = sb("ln_b", [P, 2])
        BL0, BAGG, BO = 0, D, 2 * D
        BUPD, BMSG = BO + D, BO + 2 * D
        BLN = BMSG + D
        NB = BLN + D
        brow = sb("brow", [1, 3, NB])
        bparts = sb("bparts", [1, 3, NB], BF16)
        bias3 = sb("bias3", [P, NB], BF16)
        brow_upd = sb("brow_upd", [1, D])
        bmsg_k = sb("bmsg_k", [3 * K, ROWS], BF16)
        ident_bf = sb("ident_bf", [P, P], BF16)
        b_hid = sb("b_hid", [P, HID])
        g3 = sb("g3", [P, 2, D])
        b3 = sb("b3", [P, 2, D])
        rel_in = sb("rel_in", [91, 11, D])
        rel_ss = sb("rel_ss", [91, 11])
        rel_nm = sb("rel_nm", [91, 11])

        src_i = sb("src_i", [P, STEPS, K], I32)
        dst_i = sb("dst_i", [P, STEPS, K], I32)
        type_i = sb("type_i", [P, STEPS, K], I32)
        weight = sb("weight", [P, STEPS, K])
        src_f = sb("src_f", [P, STEPS, K])
        dst_f = sb("dst_f", [P, STEPS, K])
        put_dst = sb("put_dst", [P, STEPS, K], I32)

        inv_l0 = sb("inv_l0", [P, GROUPS, K])
        inv_l3 = sb("inv_l3", [P, GROUPS, K])

        at_get = sb("at_get", [P, 2, K], I32)
        at_rel = sb("at_rel", [P, 2, K], I32)
        at_put = sb("at_put", [P, 2, K], I32)
        got = sb("got", [P, 2, K, WIDE])
        rel = sb("rel", [P, 2, K, D])
        msg = sb("msg", [P, 2, K, WIDE])
        ids = sb("ids", [P, 2, ROWS], I32)
        same = sb("same", [P, 2, K, ROWS])
        merged = sb("merged", [P, 2, K, WIDE])
        hit = sb("hit", [P, K, ROWS], BF16)
        first4 = sb("first4", [P, 2, K])
        sel4 = sb("sel4", [P, 3, K])
        dot4 = sb("dot4", [P, 2, K])
        prod = sb("prod", [P, K, D])

        xin = sb("xin", [P, 4, K, D])
        xres = sb("xres", [P, 4, K, D])
        sums = sb("sums", [P, 4, K, WIDE])
        cnt4 = sb("cnt4", [P, 2, 2, K])
        neigh = sb("neigh", [P, 4, K, D])
        xT = sb("xT", [P, 2, ROWS])
        nT = sb("nT", [P, 2, ROWS])
        linked = sb("linked", [P, 4, 3, K], BF16)
        linkedT = sb("linkedT", [3 * K, 2, P], BF16)
        x2T = sb("x2T", [P, 2, ROWS])
        above = sb("above", [P, 2, ROWS])
        below = sb("below", [P, 2, ROWS])
        res = sb("res", [P, 4, K, D])
        hid = sb("hid", [P, 4, K, HID])
        rel_sq = hid[0:91, :, :, :].rearrange("p a k d -> p (a k d)")[:, 0:11 * D].rearrange("p (r d) -> p r d", d=D)
        hidT = sb("hidT", [P, 2, 2, ROWS])
        stat = sb("stat", [P, 3, K, 6])
        mv = sb("mv", [P, 3, 4, K, 2])
        shift = sb("shift", [P, 3, 4, K])
        rstd = sb("rstd", [P, 3, 4, K])
        vare = sb("vare", [P, 3, 4, K])
        negmean = sb("negmean", [P, 3, 4, K])
        aff = sb("aff", [P, 4, K, D])
        xout = sb("xout", [P, 4, K, D])

        ps = ctx.enter_context(nc.psum_tensor("ps", [P, 8, ROWS], F32))
        products_d3 = ps[:, 2:6, :].rearrange("p b (k d) -> p b k d", k=K)

        s_const = sem("s_const")
        s_cdve = sem("s_cdve")
        s_zero = {n: sem(f"s_zero_{n}") for n in sum_d}
        s_zero_odd = sem("s_zero_odd")
        s_win = sem("s_win")
        s_rel_in = sem("s_rel_in")
        s_eload = sem("s_eload")
        s_ecast = sem("s_ecast")
        s_bpart = sem("s_bpart")
        s_brow = sem("s_brow")
        s_comb = sem("s_comb")
        s_combv = sem("s_combv")
        s_bm = sem("s_bm")
        s_relss = sem("s_relss")
        s_relnm = sem("s_relnm")
        s_relok = sem("s_relok")
        s_relst = sem("s_relst")
        pool_step = sem("pool_step")
        sp_step = sem("sp_step")
        rel_indexed = sem("rel_indexed")
        rel_got = [sem(f"rel_got{slot}") for slot in range(2)]
        rel_stored = [sem(f"rel_stored{slot}") for slot in range(2)]

        class Count:

            def __init__(self, semaphore, base):
                self.sem, self.base = semaphore, base

            def __call__(self, n):
                return self.sem, self.base + n

        STORED = {"d0": 32}

        def edge_totals(name):
            slots = [len(range(slot, STEPS, 2)) for slot in range(2)]
            gathered = 0 if name == "l2" else 64
            kept = name in ("l2", "l3a", "l3b")
            return {
                "ids0": 16 * slots[0], "ids1": 16 * slots[1],
                "got0": gathered * slots[0], "got1": gathered * slots[1],
                "keep0": 16 * slots[0] * kept, "keep1": 16 * slots[1] * kept,
                "same": STEPS, "msg": STEPS * (name not in ("l1", "l2")),
                "target": STEPS,
                "merge": STEPS, "evac": STEPS,
                "index": STEPS * (name != "l2"),
                "put": 64 * STEPS,
            }

        def node_totals(phase):
            slots = [len(range(slot, GROUPS, 4)) for slot in range(4)]
            front, late_a, late_b = {"d0": (2, 0, 0), "self": (1, 0, 0), "d1": (1, 1, 1), "own": (1, 0, 0), "d2a": (1, 1, 1), "d2b": (2, 1, 0),
                                     "d3a": (1, 1, 0), "d3b": (1, 1, 1)}[phase]
            used = {"d0": "neigh tx tn xT nT mm act norm",
                    "self": "tx xT mm act",
                    "d1": "root0 neigh tn nT mm act x2 y res var rstd norm",
                    "own": "tx xT mm act",
                    "d2a": "root0 inv neigh tn xT nT mm res var rstd norm",
                    "d2b": "root0 root1 hc tx tn xT nT mm hst hrs hn th hT o res var rstd norm",
                    "d3a": "root0 neigh tn nT mm var rstd unit scaled norm act",
                    "d3b": "root0 root2 shifted neigh tn nT mm var rstd unit scaled res2 o2 rstd2 norm"}[phase].split()
            made = {name: GROUPS for name in used}
            for slot in range(4):
                made[f"in{slot}"] = 16 * front * slots[slot]
                made[f"ra{slot}"] = 16 * late_a * slots[slot]
                made[f"rb{slot}"] = 16 * late_b * slots[slot]
                made[f"st{slot}"] = STORED.get(phase, 16) * slots[slot]
            return made

        handles, reached = {}, {}

        def counts(kind, totals):
            made = {}
            for name, total in totals.items():
                key = f"{kind}_{name}"
                if key not in handles:
                    handles[key], reached[key] = sem(key), 0
                made[name] = Count(handles[key], reached[key])
                reached[key] += total
            return made

        edge_s = {name: counts("e", edge_totals(name)) for name in sum_d}
        node_s = {phase: counts("n", node_totals(phase)) for phase in ("d0", "self", "d1", "own", "d2a", "d2b", "d3a", "d3b")}

        SRC = {"l0a": t["x"], "l0b": x1_d, "l1": xa_d, "l3a": xc_d, "l3b": x5_d}
        BEFORE = {"l0b": "d0", "l1": "d1", "l3a": "d2b", "l3b": "d3a"}
        AFTER = {"self": "d0", "d1": "self", "own": "d1", "d2a": "own", "d2b": "d2a"}
        BLOCKS = TABLE // ROWS
        PIECES = 33
        per_piece = TABLE // (ROWS * PIECES)
        CLEARED = {name: 16 * BLOCKS for name in sum_d}
        CLEARED["l0a"] = 16 * (PIECES - PIECES // 2)
        CLEARED["l0b"] = 16

        def stores_done(engine, phase):
            for slot in range(4):
                engine.wait_ge(*node_s[phase][f"st{slot}"](STORED.get(phase, 16) * len(range(slot, GROUPS, 4))))

        small_loads = [
            (w_self, t["L0_gnn_W_self"].rearrange("l i o -> i l o")), (w_neigh, t["L0_gnn_W_neigh"].rearrange("l i o -> i l o")),
            (w_agg, t["L0_gnn_W_agg"]), (w_linT, t["L1_gnn_W_lin"]), (w_msgT, t["L1_gnn_W_msg"]),
            (w_upd, t["L1_gnn_W_upd"].rearrange("(h i) o -> i h o", i=D)),
            (w_h, t["L2_gnn_W1"].rearrange("(h i) o -> i h o", i=D)), (w_o, t["L2_gnn_W2"].rearrange("(h i) o -> i h o", i=D)),
            (w_r[:, 0, :], t["L3_gnn_W1"]), (w_r[:, 1, :], t["L3_gnn_W2"]),
            (b_lin, t["L1_gnn_b_lin"].rearrange("(p a) -> p a", a=1)), (b_msg, t["L1_gnn_b_msg"].rearrange("(p a) -> p a", a=1)),
            (g3[:, 0, :], t["L3_gnn_ln1_g"].partition_broadcast(P)), (g3[:, 1, :], t["L3_gnn_ln2_g"].partition_broadcast(P)),
            (b3[:, 0, :], t["L3_gnn_ln1_b"].partition_broadcast(P)), (b3[:, 1, :], t["L3_gnn_ln2_b"].partition_broadcast(P)),
            (brow_upd, t["L1_gnn_b_upd"].rearrange("(a n) -> a n", a=1)),
            (brow[:, 0, BAGG:BAGG + D], t["L0_gnn_b_agg"].rearrange("(a n) -> a n", a=1)),
            (b_hid, t["L2_gnn_b1"].partition_broadcast(P)),
            (brow[:, 0, BO:BO + D], t["L2_gnn_b2"].rearrange("(a n) -> a n", a=1)),
            (brow[:, 0, BLN:BLN + D], t["L3_gnn_ln2_b"].rearrange("(a n) -> a n", a=1)),
        ]
        for i, name in enumerate(("b_self", "b_neigh", "layer_bias")):
            b = t[f"L0_gnn_{name}"]
            small_loads.append((brow[:, i, BL0:BL0 + D], b[0:1, :]))
            small_loads.append((col3[:, i:i + 1], b[1, :].rearrange("(p a) -> p a", a=1)))
        for h in range(2):
            small_loads.append((ln_g[:, h:h + 1], t["L2_gnn_ln_g"][h * P:(h + 1) * P].rearrange("(p a) -> p a", a=1)))
            small_loads.append((ln_b[:, h:h + 1], t["L2_gnn_ln_b"][h * P:(h + 1) * P].rearrange("(p a) -> p a", a=1)))

        block = ctx.enter_context(nc.Block())

        @block.sync
        def _(sp):
            def held(semaphore, value):
                sp.wait_ge(semaphore, value)
                sp.sem_inc(sp_step, 1)

            full = (STEPS - 1) * ROWS
            sp.wait_ge(s_cdve, 1)
            for name, tile in (("src", src_i), ("dst", dst_i), ("edge_type_1001", type_i), ("edge_weight", weight)):
                v = t[name]
                sp.dma_start(tile[:, 0:STEPS - 1, :], v[0:full].rearrange("(s p k) -> p s k", p=P, k=K)).then_inc(s_eload, 16)
                sp.dma_start(tile[0:LAST_EDGES, STEPS - 1, :],
                             v[full:E].rearrange("(p k) -> p k", k=K)).then_inc(s_eload, 16)
            for tile, ap in small_loads:
                sp.dma_start(tile[tuple(slice(None) for _ in tile.shape)], ap).then_inc(s_win, 16)
            sp.dma_start(rel_in[:, :, :], t["L3_gnn_rel_emb"].rearrange("(p r) d -> p r d", r=11)).then_inc(s_rel_in, 16)
            sp.wait_ge(s_bpart, 1)
            for i in range(3):
                sp.dma_start(bias3[i:i + 1, :], bparts[0:1, i, :]).then_inc(s_brow, 16)
            for i in range(3):
                for k in range(K):
                    sp.dma_start(bmsg_k[K * i + k:K * i + k + 1, k * D:(k + 1) * D], bparts[0:1, i, BMSG:BMSG + D]).then_inc(s_brow, 16)
            sp.wait_ge(s_relok, 1)
            sp.dma_start(rel_d.rearrange("(p r) d -> p r d", r=11), rel_in[:, :, :]).then_inc(s_relst, 16)

            def edge_stages(name):
                s = edge_s[name]
                ids_of = t["src"] if name == "l1" else t["dst"]
                rows_of, buf, free = {"l2": (t["edge_attr_128"], got, "merge"), "l3a": (rel_edge_d, rel, "msg"),
                                      "l3b": (rel_edge_d, rel, "msg")}.get(name, (None, None, None))

                def load(i, q, slot):
                    if later(i, 2):
                        held(*s["same"](i - 1))
                    last = isinstance(i, int) and i == STEPS - 1
                    count = E - full if last else ROWS
                    sp.dma_start(ids[:, slot, 0:count], ids_of[bass.ds(i * ROWS, count)].partition_broadcast(P))\
                      .then_inc(s[f"ids{slot}"].sem, 16)
                    if rows_of is None:
                        return
                    if later(i, 2):
                        held(*s[free](i - 1))
                    p = LAST_EDGES if last and name == "l2" else P
                    sp.dma_start(buf[0:p, slot, :, 0:D], rows_of[bass.ds(i * ROWS, p * K), :].rearrange("(p k) d -> p k d", k=K))\
                      .then_inc(s[f"keep{slot}"].sem, 16)

                return [(load, 0)]

            def edges(name):
                pipeline(sp, STEPS, 2, edge_stages(name))

            def rel_store(i, q, slot):
                if slot % 2:
                    held(rel_got[slot // 2], 64 * (q + 1))
                    sp.dma_start(rel_edge_d[bass.ds((2 * q + slot // 2) * ROWS, ROWS), :].rearrange("(p k) d -> p k d", k=K),
                                 rel[:, slot // 2, :, :]).then_inc(rel_stored[slot // 2], 16)

            def nodes(phase, front, front_free, late, ready, dest, sums_name, lag, others=[]):
                s = node_s[phase]
                if sums_name:
                    sp.wait_ge(*edge_s[sums_name]["put"](64 * STEPS))
                if phase in AFTER:
                    stores_done(sp, AFTER[phase])

                def fetch(buf, table, exact, i, slot, semaphore):
                    p = LAST_NODES if exact and isinstance(i, int) and i == GROUPS - 1 else P
                    w = buf.shape[3] if table.shape[1] == WIDE else D
                    sp.dma_start(buf[0:p, slot, :, 0:w], table[bass.ds(i * ROWS, p * K), :].rearrange("(p k) d -> p k d", k=K))\
                      .then_inc(semaphore, 16)

                def load(i, q, slot):
                    if later(i, 4):
                        for f in front_free:
                            held(*s[f](i - 3))
                    for buf, table, exact in front:
                        fetch(buf, table, exact, i, slot, s[f"in{slot}"].sem)
                    if sums_name:
                        fetch(sums, sum_d[sums_name], False, i, slot, s[f"in{slot}"].sem)

                def late_load(buf, table, exact, name, free):
                    def stage(i, q, slot):
                        if later(i, 4):
                            held(*s[free](i - 3))
                        fetch(buf, table, exact, i, slot, s[f"{name}{slot}"].sem)
                    return stage

                def store(i, q, slot):
                    held(*s[ready](i + 1))
                    p = LAST_NODES if dest is out and isinstance(i, int) and i == GROUPS - 1 else P
                    for table in (dest, sum_d["l0b"]) if phase == "d0" else (dest,):
                        sp.dma_start(table[bass.ds(i * ROWS, p * K), :].rearrange("(p k) d -> p k d", k=K),
                                     xout[0:p, slot, :, :]).then_inc(s[f"st{slot}"].sem, 16)

                pipeline(sp, GROUPS, 4, [(load, 0)] + others + [(late_load(*item[:-1]), item[-1]) for item in late] + [(store, lag)])

            edges("l0a")
            nodes("d0", [(xin, t["x"], True)], ["tx", "neigh"], [], "norm", x1_d, "l0a", 9,
                  [(in_pairs(edge_stages("l2")[0][0]), 0)])
            nodes("self", [(xin, x1_d, False)], ["tx"], [], "act", self_d, None, 7, [(in_pairs(edge_stages("l0b")[0][0]), 0)])
            nodes("d1", [], ["neigh"], [(xin, self_d, False, "rb", "mm", 2), (xres, t["x"], True, "ra", "res", 5)],
                  "norm", xa_d, "l0b", 14)
            nodes("own", [(xin, xa_d, False)], ["tx"], [], "act", own_d, None, 7, [(in_pairs(edge_stages("l1")[0][0]), 0)])
            nodes("d2a", [], ["neigh"], [(xin, own_d, False, "rb", "mm", 2), (xres, xa_d, False, "ra", "res", 4)],
                  "norm", xb_d, "l1", 12)
            nodes("d2b", [(xin, xb_d, False)], ["tx", "tn"], [(xres, xb_d, False, "ra", "res", 8)], "norm", xc_d, "l2", 15,
                  [(rel_store, 4)])
            for slot in range(2):
                sp.wait_ge(rel_stored[slot], 16 * len(range(slot, STEPS, 2)))
            edges("l3a")
            nodes("d3a", [], ["neigh"], [(xin, xc_d, False, "ra", "mm", 2)], "act", x5_d, "l3a", 14)
            edges("l3b")
            nodes("d3b", [], ["neigh"], [(xin, x5_d, False, "ra", "mm", 2), (xres, xc_d, False, "rb", "shifted", 5)],
                  "norm", out, "l3b", 15)
            stores_done(sp, "d3b")

        @block.gpsimd
        def _(pool):
            def held(semaphore, value):
                pool.wait_ge(semaphore, value)
                pool.sem_inc(pool_step, 1)

            pool.memset(ident[:, :], 0.0).then_inc(s_const, 1)
            pool.wait_ge(s_const, 1)
            pool.affine_select(out=ident[:, :], in_=ident[:, :], compare_op=ALU.not_equal, fill=1.0, base=0,
                               pattern=[[-1, P]], channel_multiplier=1).then_inc(s_const, 1)
            pool.iota(rev[:, :], pattern=[[-1, ROWS]], base=ROWS, channel_multiplier=0,
                      allow_small_or_imprecise_dtypes=True).then_inc(s_const, 1)
            pool.iota(rev_own[:, :], pattern=[[-1, K]], base=ROWS, channel_multiplier=-K,
                      allow_small_or_imprecise_dtypes=True).then_inc(s_const, 1)
            pool.iota(trash[:, :], pattern=[[1, K]], base=TRASH, channel_multiplier=K,
                      allow_small_or_imprecise_dtypes=True).then_inc(s_const, 1)
            pool.memset(neg_half[:, :], -0.5).then_inc(s_const, 1)
            pool.memset(pos_half[:, :], 0.5).then_inc(s_const, 1)
            pool.wait_ge(s_relss, 1)
            pool.wait_ge(s_const, 7)
            pool.tensor_tensor(rel_nm[:, :], rel_ss[:, :], pos_half[0:91, :], ALU.pow).then_inc(s_relnm, 1)
            pool.wait_ge(s_eload, 128)

            def edge_stages(name):
                s = edge_s[name]
                w = sum_d[name].shape[1]

                def get(i, q, slot):
                    held(*s["index"](i + 1))
                    for k in range(K):
                        pool.indirect_dma_start(out=got[:, slot, k, 0:D], out_offset=None, in_=SRC[name],
                                                in_offset=bass.IndirectOffsetOnAxis(ap=at_get[:, slot, k:k + 1], axis=0))\
                            .then_inc(s[f"got{slot}"].sem, 16)

                def put(i, q, slot):
                    if isinstance(i, int) and i == 0:
                        held(s_zero[name], CLEARED[name])
                        if name == "l0a":
                            held(s_zero_odd, 16 * (PIECES // 2))
                    held(*s["evac"](i + 1))
                    if later(i, 1):
                        held(*s["put"](64 * i))
                    held(*s["target"](i + 1))
                    for k in range(K):
                        pool.indirect_dma_start(out=sum_d[name],
                                                out_offset=bass.IndirectOffsetOnAxis(ap=at_put[:, slot, k:k + 1], axis=0),
                                                in_=merged[:, slot, k, 0:w], in_offset=None, compute_op=ALU.add)\
                            .then_inc(s["put"].sem, 16)

                return [get, put]

            def edges(name):
                if name in BEFORE:
                    stores_done(pool, BEFORE[name])
                get, put = edge_stages(name)
                pipeline(pool, STEPS, 2, [(get, 0), (put, 2)])

            def edges_beside(name):
                stores_done(pool, BEFORE[name])
                get, put = edge_stages(name)
                pipeline(pool, GROUPS, 4, [(in_pairs(get), 0), (in_pairs(put), 4)])

            def rel_get(i, q, slot):
                at = slot // 2
                if slot % 2 == 0:
                    if later(i, 4):
                        held(rel_stored[at], 16 * q)
                    pool.tensor_copy(at_rel[:, at, :], type_i[:, bass.ds(2 * q + at, 1), :].rearrange("p a k -> p (a k)"))\
                        .then_inc(rel_indexed, 1)
                    held(rel_indexed, 2 * q + at + 1)
                for k in range(2 * (slot % 2), 2 * (slot % 2) + 2):
                    pool.indirect_dma_start(out=rel[:, at, k, :], out_offset=None, in_=rel_d,
                                            in_offset=bass.IndirectOffsetOnAxis(ap=at_rel[:, at, k:k + 1], axis=0))\
                        .then_inc(rel_got[at], 16)

            def power(phase, n, ready, done):
                s = node_s[phase]

                def stage(i, q, slot):
                    held(*s[ready](i + 1))
                    pool.tensor_tensor(rstd[:, n, slot, :], vare[:, n, slot, :], neg_half[:, :], ALU.pow)\
                        .then_inc(s[f"root{n}"].sem, 1)
                    held(*s[f"root{n}"](i + 1))
                    pool.tensor_tensor(shift[:, n, slot, :], negmean[:, n, slot, :], rstd[:, n, slot, :], ALU.mult)\
                        .then_inc(s[done].sem, 1)
                return stage

            def join(phase):
                s = node_s[phase]

                def stage(i, q, slot):
                    held(*s["act"](i + 1))
                    if phase == "d0":
                        if later(i, 4):
                            held(*s[f"st{slot}"](STORED[phase] * q))
                        pool.tensor_tensor(xout[:, slot, :, :].rearrange("p k d -> p (k d)"), above[:, slot % 2, :],
                                           below[:, slot % 2, :], ALU.subtract).then_inc(s["norm"].sem, 1)
                    else:
                        if later(i, 2):
                            held(*s["y"](i - 1))
                        pool.tensor_tensor(x2T[:, slot % 2, :], above[:, slot % 2, :], below[:, slot % 2, :], ALU.subtract)\
                            .then_inc(s["x2"].sem, 1)
                return stage

            def average(i, q, slot):
                s = node_s["d2a"]
                held(*s["inv"](i + 1))
                if later(i, 4):
                    held(*s["tn"](i - 3))
                pool.tensor_tensor(neigh[:, slot, :, :], sums[:, slot, :, 0:D],
                                   cnt4[:, slot % 2, 1, :].rearrange("p (k a) -> p k a", a=1).to_broadcast([P, K, D]), ALU.mult)\
                    .then_inc(s["neigh"].sem, 1)

            def scale(phase, layer):
                s = node_s[phase]

                def stage(i, q, slot):
                    held(*s["unit"](i + 1))
                    pool.tensor_tensor(aff[:, slot, :, :], aff[:, slot, :, :],
                                       g3[:, layer:layer + 1, :].to_broadcast([P, K, D]), ALU.mult).then_inc(s["scaled"].sem, 1)
                return stage

            edges("l0a")
            pipeline(pool, GROUPS, 4, [(join("d0"), 6), (in_pairs(edge_stages("l2")[1]), 6)])
            edges_beside("l0b")
            pipeline(pool, GROUPS, 4, [(join("d1"), 6), (power("d1", 0, "var", "rstd"), 10)])
            edges_beside("l1")
            pipeline(pool, GROUPS, 4, [(average, 2), (power("d2a", 0, "var", "rstd"), 7)])
            pool.wait_ge(s_relst, 16)
            pipeline(pool, GROUPS, 4, [(power("d2b", 1, "hst", "hrs"), 5), (power("d2b", 0, "var", "rstd"), 10), (rel_get, 1)])
            edges("l3a")
            pipeline(pool, GROUPS, 4, [(scale("d3a", 0), 8), (power("d3a", 0, "var", "rstd"), 6)])
            edges("l3b")
            pipeline(pool, GROUPS, 4, [(scale("d3b", 1), 8), (power("d3b", 0, "var", "rstd"), 6),
                                       (power("d3b", 2, "o2", "rstd2"), 10)])

        @block.vector
        def _(dve):
            dve.memset(src_i[:, STEPS - 1, :], 0)
            dve.memset(dst_i[:, STEPS - 1, :], 0)
            dve.memset(type_i[:, STEPS - 1, :], 0)
            dve.memset(weight[:, STEPS - 1, :], 0.0)
            dve.memset(bias3[:, :], 0.0)
            dve.memset(bmsg_k[:, :], 0.0)
            dve.memset(zeros[:, :], 0.0)
            dve.memset(brow[:, :, :], 0.0)
            dve.drain().then_inc(s_cdve, 1)
            dve.memset(ones_bf[:, :], 1.0)
            dve.memset(msg[:, :, :, D:WIDE], 0.0)
            dve.memset(got[:, :, :, :], 0.0)
            dve.memset(xin[:, :, :, :], 0.0)
            dve.memset(xres[:, :, :, :], 0.0)
            dve.drain()
            dve.memset(msg[:, :, :, D:D + 1], 1.0)
            dve.memset(got[:, :, :, D:D + 1], 1.0)
            dve.drain().then_inc(s_cdve, 1)

            dve.wait_ge(s_win, 16 * len(small_loads))
            dve.wait_ge(s_comb, 1)
            dve.tensor_copy(w_c1[:, :], ps[:, 0, 0:D])
            dve.tensor_copy(w_c2[:, :], ps[:, 1, 0:D])
            dve.tensor_tensor(brow[:, 0, BUPD:BUPD + D], ps[0:1, 2, 0:D], brow_upd[:, :], ALU.add)
            dve.tensor_copy(brow[:, 0, BMSG:BMSG + D], ps[0:1, 3, 0:D])
            dve.drain().then_inc(s_bm, 1)

            dve.tensor_tensor(brow[:, 0, :], brow[:, 0, :], brow[:, 1, :], ALU.add)
            dve.tensor_tensor(b_l0b[:, :], col3[:, 0:1], col3[:, 1:2], ALU.add)
            dve.drain()
            dve.tensor_tensor(brow[:, 0, :], brow[:, 0, :], brow[:, 2, :], ALU.add)
            dve.tensor_tensor(b_l0b[:, :], b_l0b[:, :], col3[:, 2:3], ALU.add)
            dve.drain()
            dve.tensor_scalar(b_below[:, :], b_l0b[:, :], -SLOPE, None, ALU.mult)
            for i in range(3):
                dve.tensor_copy(bparts[:, i, :], brow[:, i % 2, :])
                dve.drain()
                if i < 2:
                    dve.tensor_tensor(brow[:, (i + 1) % 2, :], brow[:, i % 2, :], bparts[:, i, :], ALU.subtract)
                    dve.drain()
            dve.drain().then_inc(s_bpart, 1)

            dve.wait_ge(s_eload, 128)
            dve.tensor_copy(src_f[:, :, :], src_i[:, :, :])
            dve.tensor_copy(dst_f[:, :, :], dst_i[:, :, :])
            dve.drain()

            dve.wait_ge(s_rel_in, 16)
            dve.tensor_tensor(rel_sq, rel_in[:, :, :], rel_in[:, :, :], ALU.mult)
            dve.drain()
            dve.reduce_sum(rel_ss[:, :], rel_sq, axis=AX_X).then_inc(s_relss, 1)
            dve.wait_ge(s_relnm, 1)
            dve.tensor_scalar(rel_ss[:, :], rel_nm[:, :], 1e-6, None, ALU.max)
            dve.drain()
            dve.reciprocal(rel_nm[:, :], rel_ss[:, :])
            dve.drain()
            dve.tensor_tensor(rel_in[:, :, :], rel_in[:, :, :],
                              rel_nm[:, :].rearrange("p (r a) -> p r a", a=1).to_broadcast([91, 11, D]), ALU.mult)\
               .then_inc(s_relok, 1)

            dve.wait_ge(s_const, 7)
            dve.tensor_copy(ident_bf[:, :], ident[:, :]).then_inc(s_cdve, 1)

            def edge_stages(name):
                s = edge_s[name]
                node_f = src_f if name == "l1" else dst_f
                get_i = dst_i if name == "l1" else src_i
                numbered = name in ("l0a", "l1")

                def step_of(table, i):
                    return table[:, bass.ds(i, 1), :].rearrange("p a k -> p (a k)")

                def index(i, q, slot):
                    if later(i, 2):
                        dve.wait_ge(*s[f"got{slot}"](64 * q))
                        if name == "l1":
                            dve.wait_ge(*s["merge"](i - 1))
                    dve.tensor_copy(at_get[:, slot, :], step_of(get_i, i)).then_inc(s["index"].sem, 1)

                def target(i, q, slot):
                    if later(i, 2):
                        dve.wait_ge(*s["put"](64 * (i - 1)))
                    if name == "l0a":
                        dve.tensor_tensor(step_of(put_dst, i), sel4[:, 2, :], trash[:, :], ALU.add)
                    if numbered:
                        last = dve.tensor_tensor(at_put[:, slot, :], sel4[:, 2, :], trash[:, :], ALU.add)
                    else:
                        last = dve.tensor_copy(at_put[:, slot, :], step_of(put_dst, i))
                    last.then_inc(s["target"].sem, 1)

                def compare(i, q, slot):
                    dve.wait_ge(*s[f"ids{slot}"](16 * (q + 1)))
                    if later(i, 2):
                        dve.wait_ge(*s["merge"](i - 1))
                    if isinstance(i, int) and i == STEPS - 1:
                        dve.memset(ids[:, slot, E - i * ROWS:ROWS], -1)
                        dve.drain()
                    for k in range(K):
                        dve.tensor_scalar(same[:, slot, k, :], ids[:, slot, :],
                                          node_f[:, bass.ds(i, 1), k:k + 1].rearrange("p a k -> p (a k)"), None, ALU.is_equal)
                    dve.drain().then_inc(s["same"].sem, 1)
                    if not numbered:
                        return
                    for k in range(K):
                        dve.tensor_tensor_reduce(out=hit[:, k, :], in0=same[:, slot, k, :], in1=rev[:, :], scale=1.0, scalar=0.0,
                                                 op0=ALU.mult, op1=ALU.max, accum_out=first4[:, slot, k:k + 1])
                    dve.drain()
                    dve.tensor_tensor(sel4[:, 0, :], first4[:, slot, :], rev_own[:, :], ALU.is_equal)
                    dve.tensor_tensor(sel4[:, 1, :], node_f[:, bass.ds(i, 1), :].rearrange("p a k -> p (a k)"), trash[:, :], ALU.subtract)
                    dve.drain()
                    dve.tensor_tensor(sel4[:, 2, :], sel4[:, 0, :], sel4[:, 1, :], ALU.mult)
                    dve.drain()

                def message(i, q, slot):
                    dve.wait_ge(*s[f"got{slot}"](64 * (q + 1)))
                    if name in ("l3a", "l3b"):
                        dve.wait_ge(*s[f"keep{slot}"](16 * (q + 1)))
                    if later(i, 2):
                        dve.wait_ge(*s["merge"](i - 1))
                    if name in ("l0a", "l0b"):
                        for k in range(K):
                            dve.tensor_scalar(msg[:, slot, k, 0:D], got[:, slot, k, 0:D],
                                              weight[:, bass.ds(i, 1), k:k + 1].rearrange("p a k -> p (a k)"), None, ALU.mult)
                    else:
                        for k in range(K):
                            dve.tensor_tensor_reduce(out=prod[:, k, :], in0=got[:, slot, k, 0:D], in1=rel[:, slot, k, :], scale=-2.0,
                                                     scalar=0.0, op0=ALU.mult, op1=ALU.add, accum_out=dot4[:, slot, k:k + 1])
                        dve.drain()
                        for k in range(K):
                            dve.scalar_tensor_tensor(out=msg[:, slot, k, 0:D], in0=rel[:, slot, k, :], scalar=dot4[:, slot, k:k + 1],
                                                     in1=got[:, slot, k, 0:D], op0=ALU.mult, op1=ALU.add)
                    dve.drain().then_inc(s["msg"].sem, 1)

                return ([(target, 2)] + ([(index, 0)] if name != "l2" else []) + [(compare, 1)] +
                        ([(message, 1)] if name not in ("l1", "l2") else []))

            def edges(name):
                pipeline(dve, STEPS, 2, edge_stages(name))

            def edges_beside(name):
                pipeline(dve, GROUPS, 4, [(in_pairs(stage), 2 * lag) for stage, lag in edge_stages(name)])

            def row_stats(*items, behind=1):
                def rows(n, buf, given):
                    def stage(i, q, slot):
                        for there in given:
                            dve.wait_ge(*there(i + 1))
                        for k in range(K):
                            dve.bn_stats(stat[:, n, k, :], buf[:, slot, k, :])
                    return stage

                def halves(n):
                    def stage(i, q, slot):
                        for k in range(K):
                            dve.bn_aggr(mv[:, n, slot, k, :], stat[:, n, k, :])
                    return stage

                def parts(n, done):
                    def stage(i, q, slot):
                        dve.tensor_scalar(negmean[:, n, slot, :], mv[:, n, slot, :, 0:1].rearrange("p k a -> p (k a)"), -1.0, None, ALU.mult)
                        dve.tensor_scalar(vare[:, n, slot, :], mv[:, n, slot, :, 1:2].rearrange("p k a -> p (k a)"), EPS, None, ALU.add)\
                           .then_inc(done.sem, 1)
                    return stage

                return ([SETTLE] + [(rows(n, buf, given), lag) for lag, n, buf, done, *given in items] +
                        [(parts(n, done), lag + 1) for lag, n, buf, done, *given in items if behind] +
                        [SETTLE] + [(halves(n), lag) for lag, n, buf, done, *given in items] +
                        ([] if behind else [SETTLE] + [(parts(n, done), lag) for lag, n, buf, done, *given in items]))

            def loaded(s, q, slot, count, name="in"):
                dve.wait_ge(*s[f"{name}{slot}"](16 * count * (q + 1)))

            def rows_of(bank):
                return ps[:, bank, :].rearrange("p (k d) -> p k d", k=K)

            def per_row(table, i):
                return table[:, bass.ds(i, 1), :].rearrange("p a k -> p k a").to_broadcast([P, K, D])

            def copy_nT(s, bank=2, slots=2):
                def stage(i, q, slot):
                    dve.wait_ge(*s["tn"](i + 1))
                    if later(i, 2):
                        dve.wait_ge(*s["mm"](i - 1))
                    dve.tensor_copy(nT[:, slot % 2, :], ps[:, bank + slot % slots, :]).then_inc(s["nT"].sem, 1)
                return stage

            def d0():
                s = node_s["d0"]

                def average(i, q, slot):
                    loaded(s, q, slot, 2)
                    if later(i, 4):
                        dve.wait_ge(*s["tn"](i - 3))
                    c = cnt4[:, slot % 2, :, :]
                    count = sums[:, slot, :, D:D + 1].rearrange("p k a -> p (k a)")
                    dve.tensor_scalar(c[:, 0, :], count, 1.0, None, ALU.add)
                    dve.tensor_scalar(c[:, 1, :], count, 1.0, None, ALU.max)
                    dve.tensor_tensor(neigh[:, slot, :, :], sums[:, slot, :, 0:D], xin[:, slot, :, :], ALU.add)
                    dve.drain()
                    dve.reciprocal(inv_l0[:, bass.ds(i, 1), :].rearrange("p a k -> p (a k)"), c[:, 0, :])
                    dve.reciprocal(inv_l3[:, bass.ds(i, 1), :].rearrange("p a k -> p (a k)"), c[:, 1, :])
                    dve.drain()
                    dve.tensor_tensor(neigh[:, slot, :, :], neigh[:, slot, :, :], per_row(inv_l0, i), ALU.mult)\
                       .then_inc(s["neigh"].sem, 1)

                pipeline(dve, GROUPS, 4, [(copy_nT(s), 3), (in_pairs(edge_stages("l2")[0][0]), 4), (in_pairs(edge_stages("l2")[1][0]), 2),
                                          (average, 1)])

            def d1():
                s = node_s["d1"]

                def average(i, q, slot):
                    loaded(s, q, slot, 1)
                    if later(i, 4):
                        dve.wait_ge(*s["tn"](i - 3))
                    dve.tensor_tensor(neigh[:, slot, :, :], sums[:, slot, :, 0:D], per_row(inv_l0, i), ALU.mult)\
                       .then_inc(s["neigh"].sem, 1)

                def residual(i, q, slot):
                    dve.wait_ge(*s["y"](i + 1))
                    loaded(s, q, slot, 1, "ra")
                    if later(i, 4):
                        dve.wait_ge(*s["norm"](i - 3))
                    dve.tensor_tensor(res[:, slot, :, :], rows_of(6 + slot % 2), xres[:, slot, :, :], ALU.add).then_inc(s["res"].sem, 1)

                pipeline(dve, GROUPS, 4, [(average, 1), (residual, 8)] + row_stats((8, 0, res, s["var"])))

            def d2a():
                s = node_s["d2a"]

                def inverse(i, q, slot):
                    loaded(s, q, slot, 1)
                    if later(i, 2):
                        dve.wait_ge(*s["neigh"](i - 1))
                    if later(i, 4):
                        dve.wait_ge(*s["tn"](i - 3))
                    count = sums[:, slot, :, D:D + 1].rearrange("p k a -> p a k")
                    dve.tensor_scalar(cnt4[:, slot % 2, 0:1, :], count, 1.0, None, ALU.max)
                    dve.tensor_scalar(linked[:, slot, :, :], count.to_broadcast([P, 3, K]), 1.0, None, ALU.min)
                    dve.drain()
                    dve.reciprocal(cnt4[:, slot % 2, 1, :], cnt4[:, slot % 2, 0, :]).then_inc(s["inv"].sem, 1)

                def residual(i, q, slot):
                    dve.wait_ge(*s["mm"](i + 1))
                    loaded(s, q, slot, 1, "ra")
                    if later(i, 4):
                        dve.wait_ge(*s["norm"](i - 3))
                    dve.scalar_tensor_tensor(out=res[:, slot, :, :], in0=rows_of(4 + slot % 2), scalar=0.0,
                                             in1=xres[:, slot, :, :], op0=ALU.max, op1=ALU.add).then_inc(s["res"].sem, 1)

                pipeline(dve, GROUPS, 4, [(inverse, 1), (residual, 6)] + row_stats((6, 0, res, s["var"])))

            def d2b():
                s = node_s["d2b"]

                def hidden(i, q, slot):
                    dve.wait_ge(*s["mm"](i + 1))
                    if later(i, 4):
                        dve.wait_ge(*s["th"](i - 3))
                    dve.tensor_tensor(hid[:, slot, :, :], ps[:, 2:4, :].rearrange("p b (j d) -> p (b j) d", j=2),
                                      b_hid[:, :].rearrange("p (a d) -> p a d", a=1).to_broadcast([P, K, HID]), ALU.add)\
                       .then_inc(s["hc"].sem, 1)

                def hidden_norm(i, q, slot):
                    dve.wait_ge(*s["hrs"](i + 1))
                    for k in range(K):
                        last = dve.tensor_scalar(hid[:, slot, k, :], hid[:, slot, k, :], mv[:, 1, slot, k, 0:1],
                                          rstd[:, 1, slot, k:k + 1], ALU.subtract, ALU.mult)
                    last.then_inc(s["hn"].sem, 1)

                def residual(i, q, slot):
                    dve.wait_ge(*s["o"](i + 1))
                    loaded(s, q, slot, 1, "ra")
                    if later(i, 4):
                        dve.wait_ge(*s["norm"](i - 3))
                    dve.scalar_tensor_tensor(out=res[:, slot, :, :], in0=xres[:, slot, :, :], scalar=2.0,
                                             in1=rows_of(6 + slot % 2), op0=ALU.mult, op1=ALU.add).then_inc(s["res"].sem, 1)

                pipeline(dve, GROUPS, 4, [(copy_nT(s, 1, 1), 2), (hidden, 4), (residual, 10), (hidden_norm, 6)] +
                         row_stats((5, 1, hid, s["hst"]), (10, 0, res, s["var"]), behind=0))

            def d3(phase, layer):
                s = node_s[phase]

                def average(i, q, slot):
                    loaded(s, q, slot, 1)
                    if later(i, 4):
                        dve.wait_ge(*s["tn"](i - 3))
                    dve.tensor_tensor(neigh[:, slot, :, :], sums[:, slot, :, 0:D], per_row(inv_l3, i), ALU.mult)\
                       .then_inc(s["neigh"].sem, 1)

                def add_beta(i, q, slot):
                    dve.wait_ge(*s["scaled"](i + 1))
                    a = aff[:, slot, :, :]
                    if not layer:
                        dve.tensor_tensor(a, a, b3[:, layer:layer + 1, :].to_broadcast([P, K, D]), ALU.add).then_inc(s["norm"].sem, 1)
                        return
                    dve.wait_ge(*s["shifted"](i + 1))
                    dve.tensor_tensor(a, a, rows_of(6 + slot % 2), ALU.add).then_inc(s["res2"].sem, 1)

                pipeline(dve, GROUPS, 4, [(average, 1), (add_beta, 9)] +
                         row_stats((5, 0, products_d3, s["var"], s["mm"]), *([(9, 2, aff, s["o2"])] if layer else [])))

            edges("l0a")
            d0()
            edges_beside("l0b")
            d1()
            edges_beside("l1")
            d2a()
            d2b()
            edges("l3a")
            d3("d3a", 0)
            edges("l3b")
            d3("d3b", 1)

        @block.scalar
        def _(act):
            act.wait_ge(s_cdve, 1)

            def clear(name, pieces):
                def stage(i, q, slot):
                    at = [i * pieces + c for c in range(pieces)]
                    if isinstance(i, int) and i == 0:
                        at.append(BLOCKS - 1)
                    w = sum_d[name].shape[1]
                    for b in at:
                        act.dma_start(sum_d[name][bass.ds(b * ROWS, ROWS), :].rearrange("(p k) d -> p (k d)", k=K), zeros[:, 0:K * w])\
                            .then_inc(s_zero[name], 16)
                return stage

            def norm(phase, dest, done, free, rows=None, n=0, ready="rstd"):
                rows = res if rows is None else rows
                s = node_s[phase]

                def stage(i, q, slot):
                    act.wait_ge(*s[ready](i + 1))
                    if later(i, 4):
                        if free:
                            act.wait_ge(*s[free](i - 3))
                        else:
                            act.wait_ge(*s[f"st{slot}"](16 * q))
                    for k in range(K):
                        last = act.activation(dest[:, slot, k, :], rows[:, slot, k, :], ACT.Identity, bias=shift[:, n, slot, k:k + 1],
                                              scale=rstd[:, n, slot, k:k + 1])
                    last.then_inc(s[done].sem, 1)
                return stage

            whole = sum_d["l0a"].rearrange("(p n r) d -> p n (r d)", p=P, r=K)
            for c in range(PIECES):
                half = s_zero_odd if c % 2 else s_zero["l0a"]
                if c >= 2:
                    act.wait_ge(half, 16 * (c // 2))
                act.dma_start(whole[:, c * per_piece:(c + 1) * per_piece, :],
                              zeros[:, :].rearrange("p (a n) -> p a n", a=1).to_broadcast([P, per_piece, K * WIDE])).then_inc(half, 16)

            def edge_stages(name):
                s = edge_s[name]
                w = sum_d[name].shape[1]

                def evacuate(i, q, slot):
                    act.wait_ge(*s["merge"](i + 1))
                    if later(i, 2):
                        act.wait_ge(*s["put"](64 * (i - 1)))
                    b = 6 if name == "l2" else 2 * slot
                    act.activation(merged[:, slot, :, 0:w],
                                   ps[:, b:b + 2, :].rearrange("p b (j d) -> p (b j) d", j=2)[:, :, 0:w],
                                   ACT.Copy).then_inc(s["evac"].sem, 1)

                return [(evacuate, 0)]

            def edges(name, others=[]):
                pipeline(act, STEPS, 2, edge_stages(name) + others)

            def beside(phase, name, others=[]):
                s = node_s[phase]

                def evacuate(i, q, slot):
                    act.wait_ge(*s["mm"](i + 1))
                    if later(i, 4):
                        act.wait_ge(*s[f"st{slot}"](16 * q))
                    act.activation(xout[:, slot, :, :].rearrange("p k d -> p (k d)"), ps[:, 6 + slot % 2, :], ACT.Copy)\
                        .then_inc(s["act"].sem, 1)

                pipeline(act, GROUPS, 4, [(evacuate, 5), (in_pairs(edge_stages(name)[0][0]), 1), (copy_xT(s, 4, True), 3)] + others)

            def copy_xT(s, bank, wide):
                def stage(i, q, slot):
                    act.wait_ge(*s["tx"](i + 1))
                    if later(i, 2):
                        act.wait_ge(*s["mm"](i - 1))
                    act.activation(xT[:, slot % 2, :], ps[:, bank + (slot % 2 if wide else 0), :], ACT.Copy).then_inc(s["xT"].sem, 1)
                return stage

            def d0():
                s = node_s["d0"]

                def leaky(i, q, slot):
                    act.wait_ge(*s["mm"](i + 1))
                    if later(i, 2):
                        act.wait_ge(*s["norm"](i - 1))
                    act.activation(above[:, slot % 2, :], ps[:, 4 + slot % 2, :], ACT.Relu)
                    act.activation(below[:, slot % 2, :], ps[:, 4 + slot % 2, :], ACT.Relu, scale=-SLOPE).then_inc(s["act"].sem, 1)

                pipeline(act, GROUPS, 4, [(leaky, 5), (in_pairs(edge_stages("l2")[0][0]), 4), (copy_xT(s, 0, True), 3)])

            def d1():
                s = node_s["d1"]

                def leaky(i, q, slot):
                    act.wait_ge(*s["mm"](i + 1))
                    if later(i, 2):
                        act.wait_ge(*s["x2"](i - 1))
                    act.activation(above[:, slot % 2, :], ps[:, 4 + slot % 2, :], ACT.Relu, bias=b_l0b[:, :])
                    act.activation(below[:, slot % 2, :], ps[:, 4 + slot % 2, :], ACT.Relu, bias=b_below[:, :], scale=-SLOPE)\
                       .then_inc(s["act"].sem, 1)

                def copy_n(i, q, slot):
                    act.wait_ge(*s["tn"](i + 1))
                    if later(i, 2):
                        act.wait_ge(*s["mm"](i - 1))
                    act.activation(nT[:, slot % 2, :], ps[:, 2 + slot % 2, :], ACT.Copy).then_inc(s["nT"].sem, 1)

                pipeline(act, GROUPS, 4, [(copy_n, 3), (leaky, 5), (norm("d1", xout, "norm", None), 11)])

            def d2a():
                s = node_s["d2a"]

                def copy_turned(i, q, slot):
                    act.wait_ge(*s["tn"](i + 1))
                    if later(i, 2):
                        act.wait_ge(*s["mm"](i - 1))
                    act.activation(nT[:, slot % 2, :], ps[:, 2 + slot % 2, :], ACT.Copy).then_inc(s["nT"].sem, 1)
                    act.activation(linkedT[:, slot % 2, :], ps[0:3 * K, 6 + slot % 2, 0:P], ACT.Copy).then_inc(s["xT"].sem, 1)

                pipeline(act, GROUPS, 4, [(copy_turned, 4), (norm("d2a", xout, "norm", None), 8)])

            def d2b():
                s = node_s["d2b"]

                def silu(i, q, slot):
                    act.wait_ge(*s["th"](i + 1))
                    if later(i, 2):
                        act.wait_ge(*s["o"](i - 1))
                    for h in range(2):
                        last = act.activation(hidT[:, slot % 2, h, :], ps[:, 4 + h, :], ACT.Silu, bias=ln_b[:, h:h + 1], scale=ln_g[:, h:h + 1])
                    last.then_inc(s["hT"].sem, 1)

                pipeline(act, GROUPS, 4, [(silu, 8), (norm("d2b", xout, "norm", None), 12), (copy_xT(s, 0, False), 2),
                                          (clear("l3a", 1), 4), (clear("l3b", 1), 4)])

            def d3(phase, layer):
                s = node_s[phase]

                def copy_n(i, q, slot):
                    act.wait_ge(*s["tn"](i + 1))
                    if later(i, 2):
                        act.wait_ge(*s["mm"](i - 1))
                    act.activation(nT[:, slot % 2, :], ps[:, slot % 2, :], ACT.Copy).then_inc(s["nT"].sem, 1)

                def relu(i, q, slot):
                    act.wait_ge(*s["norm"](i + 1))
                    if later(i, 4):
                        act.wait_ge(*s[f"st{slot}"](16 * q))
                    act.activation(xout[:, slot, :, :], aff[:, slot, :, :], ACT.Relu).then_inc(s["act"].sem, 1)

                pipeline(act, GROUPS, 4, [(copy_n, 3), (norm("d3b", xout, "norm", None, aff, 2, "rstd2"), 11) if layer else (relu, 10),
                                          (norm(phase, aff, "unit", "norm" if layer else "act", products_d3), 7)])

            act.dma_start(sum_d["l0b"][XROWS:TABLE, :].rearrange("(p k) d -> p (k d)", k=K), zeros[:, 0:ROWS]).then_inc(s_zero["l0b"], 16)
            edges("l0a", [(clear("l2", 2), 0)])
            d0()
            beside("self", "l0b", [(clear("l1", 1), 3)])
            d1()
            beside("own", "l1")
            d2a()
            d2b()
            edges("l3a")
            d3("d3a", 0)
            edges("l3b")
            d3("d3b", 1)

        @block.tensor
        def _(pe):
            pe.wait_ge(s_win, 16 * len(small_loads))
            pe.matmul(ps[:, 0, 0:D], w_linT[:, :], w_upd[:, 0, :], start=True, stop=True)
            pe.matmul(ps[:, 1, 0:D], w_msgT[:, :], w_upd[:, 1, :], start=True, stop=True)
            pe.matmul(ps[0:1, 2, 0:D], b_lin[:, :], w_upd[:, 0, :], start=True, stop=True)
            pe.matmul(ps[0:1, 3, 0:D], b_msg[:, :], w_upd[:, 1, :], start=True, stop=True).then_inc(s_comb, 1)
            pe.wait_ge(s_bm, 1)
            pe.wait_ge(s_brow, 16 * (3 + 3 * K))
            pe.wait_ge(s_const, 7)
            pe.wait_ge(s_cdve, 3)

            def edge_stages(name):
                s = edge_s[name]
                w = sum_d[name].shape[1]
                rows = got if name in ("l1", "l2") else msg

                def merge(i, q, slot):
                    pe.wait_ge(*s["same"](i + 1))
                    if name == "l1":
                        pe.wait_ge(*s[f"got{slot}"](64 * (q + 1)))
                    elif name == "l2":
                        pe.wait_ge(*s[f"keep{slot}"](16 * (q + 1)))
                    else:
                        pe.wait_ge(*s["msg"](i + 1))
                    b, behind = (6, 1) if name == "l2" else (2 * slot, 2)
                    if later(i, behind):
                        pe.wait_ge(*s["evac"](i - behind + 1))
                    for k in range(K):
                        for j in range(K):
                            last = pe.matmul(ps[:, b + k // 2, (k % 2) * 256:(k % 2) * 256 + w], same[:, slot, j, k:ROWS:K],
                                             rows[:, slot, j, 0:w], start=(j == 0), stop=(j == K - 1), skip_group_check=True)
                    last.then_inc(s["merge"].sem, 1)

                return [(merge, 0)]

            def edges(name):
                pipeline(pe, STEPS, 2, edge_stages(name))

            def transposes(s, bank, rows, loaded_count, free, done, wide=True):
                def stage(i, q, slot):
                    if loaded_count:
                        pe.wait_ge(*s[f"in{slot}"](16 * loaded_count * (q + 1)))
                    else:
                        pe.wait_ge(*s["neigh"](i + 1))
                    behind = 2 if wide else 1
                    if later(i, behind):
                        for name, per in free:
                            pe.wait_ge(*s[name](per * (i - behind + 1)))
                    for k in range(K):
                        last = pe.transpose(ps[:, bank + (slot % 2 if wide else 0), k * P:(k + 1) * P], rows(slot)[:, k, 0:D], ident[:, :])
                    last.then_inc(s[done].sem, 1)
                return stage

            def bias(bank, lo, n, width):
                pe.matmul(ps[:, bank, 0:ROWS], ones_bf[:, :],
                          bias3[:, lo:lo + width].rearrange("p (a d) -> p a d", a=1).to_broadcast([P, n, width]),
                          start=True, stop=False, skip_group_check=True)

            def beside(phase, name):
                s = node_s[phase]

                def products(i, q, slot):
                    pe.wait_ge(*s["xT"](i + 1))
                    if later(i, 2):
                        pe.wait_ge(*s["act"](i - 1))
                    b = 6 + slot % 2
                    if phase == "self":
                        pe.matmul(ps[:, b, :], w_self[:, 1, :], xT[:, slot % 2, :], start=True, stop=True).then_inc(s["mm"].sem, 1)
                        return
                    bias(b, BUPD, K, D)
                    for k in range(K):
                        c = slice(k * P, (k + 1) * P)
                        last = pe.matmul(ps[:, b, c], xT[:, slot % 2, c], w_c1[:, :], start=False, stop=(k == K - 1), skip_group_check=True)
                    last.then_inc(s["mm"].sem, 1)

                pipeline(pe, GROUPS, 4, [(products, 4), (in_pairs(edge_stages(name)[0][0]), 1),
                                         (transposes(s, 4, lambda c: xin[:, c, :, :], 1, [("xT", 1)], "tx"), 2)])

            def d0():
                s = node_s["d0"]

                def products(i, q, slot):
                    pe.wait_ge(*s["xT"](i + 1))
                    pe.wait_ge(*s["nT"](i + 1))
                    if later(i, 2):
                        pe.wait_ge(*s["act"](i - 1))
                    b = 4 + slot % 2
                    bias(b, BL0, K, D)
                    for k in range(K):
                        c = slice(k * P, (k + 1) * P)
                        pe.matmul(ps[:, b, c], xT[:, slot % 2, c], w_self[:, 0, :], start=False, stop=False, skip_group_check=True)
                        last = pe.matmul(ps[:, b, c], nT[:, slot % 2, c], w_neigh[:, 0, :], start=False, stop=(k == K - 1),
                                         skip_group_check=True)
                    last.then_inc(s["mm"].sem, 1)

                pipeline(pe, GROUPS, 4, [(products, 4), (in_pairs(edge_stages("l2")[0][0]), 3),
                                         (transposes(s, 0, lambda c: xin[:, c, :, :], 2, [("xT", 1)], "tx"), 2),
                                         (transposes(s, 2, lambda c: neigh[:, c, :, :], 0, [("nT", 1)], "tn"), 2)])

            def d1():
                s = node_s["d1"]

                def products(i, q, slot):
                    pe.wait_ge(*s[f"rb{slot}"](16 * (q + 1)))
                    pe.wait_ge(*s["nT"](i + 1))
                    if later(i, 2):
                        pe.wait_ge(*s["act"](i - 1))
                    b = 4 + slot % 2
                    pe.matmul(ps[:, b, :], ident[:, :], xin[:, slot, :, :].rearrange("p k d -> p (k d)"), start=True, stop=False)
                    pe.matmul(ps[:, b, :], w_neigh[:, 1, :], nT[:, slot % 2, :], start=False, stop=True).then_inc(s["mm"].sem, 1)

                def final(i, q, slot):
                    pe.wait_ge(*s["x2"](i + 1))
                    if later(i, 2):
                        pe.wait_ge(*s["res"](i - 1))
                    b = 6 + slot % 2
                    bias(b, BAGG, K, D)
                    for k in range(K):
                        c = slice(k * P, (k + 1) * P)
                        last = pe.matmul(ps[:, b, c], x2T[:, slot % 2, c], w_agg[:, :], start=False, stop=(k == K - 1), skip_group_check=True)
                    last.then_inc(s["y"].sem, 1)

                pipeline(pe, GROUPS, 4, [(final, 7), (products, 4),
                                         (transposes(s, 2, lambda c: neigh[:, c, :, :], 0, [("nT", 1)], "tn"), 2)])

            def d2a():
                s = node_s["d2a"]

                def turn_sums(i, q, slot):
                    pe.wait_ge(*s["neigh"](i + 1))
                    if later(i, 2):
                        pe.wait_ge(*s["xT"](i - 1))
                    for k in range(K):
                        pe.transpose(ps[:, 2 + slot % 2, k * P:(k + 1) * P], neigh[:, slot, k, :], ident[:, :])
                    pe.matmul(ps[0:3 * K, 6 + slot % 2, 0:P], linked[:, slot, :, :].rearrange("p a k -> p (a k)"), ident_bf[:, :],
                              start=True, stop=True).then_inc(s["tn"].sem, 1)

                def products(i, q, slot):
                    pe.wait_ge(*s[f"rb{slot}"](16 * (q + 1)))
                    pe.wait_ge(*s["nT"](i + 1))
                    pe.wait_ge(*s["xT"](i + 1))
                    if later(i, 2):
                        pe.wait_ge(*s["res"](i - 1))
                    b = 4 + slot % 2
                    pe.matmul(ps[:, b, :], ident[:, :], xin[:, slot, :, :].rearrange("p k d -> p (k d)"), start=True, stop=False,
                              skip_group_check=True)
                    pe.matmul(ps[:, b, :], linkedT[:, slot % 2, :], bmsg_k[:, :], start=False, stop=False, skip_group_check=True)
                    for k in range(K):
                        c = slice(k * P, (k + 1) * P)
                        last = pe.matmul(ps[:, b, c], nT[:, slot % 2, c], w_c2[:, :], start=False, stop=(k == K - 1), skip_group_check=True)
                    last.then_inc(s["mm"].sem, 1)

                pipeline(pe, GROUPS, 4, [(products, 5), (turn_sums, 3)])

            def d2b():
                s = node_s["d2b"]

                def products(i, q, slot):
                    pe.wait_ge(*s["xT"](i + 1))
                    pe.wait_ge(*s["nT"](i + 1))
                    if later(i, 1):
                        pe.wait_ge(*s["hc"](i))
                    for b in range(2):
                        for j in range(2):
                            k = 2 * b + j
                            c = slice(k * P, (k + 1) * P)
                            o = ps[:, 2 + b, j * HID:(j + 1) * HID]
                            pe.matmul(o, xT[:, slot % 2, c], w_h[:, 0, :], start=(j == 0), stop=False, skip_group_check=True)
                            last = pe.matmul(o, nT[:, slot % 2, c], w_h[:, 1, :], start=False, stop=(j == 1), skip_group_check=True)
                    last.then_inc(s["mm"].sem, 1)

                def turn_hidden(i, q, slot):
                    pe.wait_ge(*s["hn"](i + 1))
                    if later(i, 1):
                        pe.wait_ge(*s["hT"](i))
                    for h in range(2):
                        for k in range(K):
                            last = pe.transpose(ps[:, 4 + h, k * P:(k + 1) * P], hid[:, slot, k, h * P:(h + 1) * P], ident[:, :])
                    last.then_inc(s["th"].sem, 1)

                def last_products(i, q, slot):
                    pe.wait_ge(*s["hT"](i + 1))
                    if later(i, 2):
                        pe.wait_ge(*s["res"](i - 1))
                    b = 6 + slot % 2
                    bias(b, BO, K, D)
                    for k in range(K):
                        c = slice(k * P, (k + 1) * P)
                        for h in range(2):
                            last = pe.matmul(ps[:, b, c], hidT[:, slot % 2, h, c], w_o[:, h, :], start=False,
                                             stop=(k == K - 1 and h == 1), skip_group_check=True)
                    last.then_inc(s["o"].sem, 1)

                pipeline(pe, GROUPS, 4, [(last_products, 9), (turn_hidden, 7),
                                         (transposes(s, 0, lambda c: xin[:, c, :, :], 2, [("xT", 1)], "tx", False), 1),
                                         (transposes(s, 1, lambda c: sums[:, c, :, :], 2, [("nT", 1)], "tn", False), 1),
                                         (products, 3)])

            def d3(phase, layer):
                s = node_s[phase]

                def products(i, q, slot):
                    pe.wait_ge(*s[f"ra{slot}"](16 * (q + 1)))
                    pe.wait_ge(*s["nT"](i + 1))
                    if later(i, 4):
                        pe.wait_ge(*s["unit"](i - 3))
                    pe.matmul(ps[:, 2 + slot, :], ident[:, :], xin[:, slot, :, :].rearrange("p k d -> p (k d)"), start=True, stop=False,
                              skip_group_check=True)
                    for k in range(K):
                        c = slice(k * P, (k + 1) * P)
                        last = pe.matmul(ps[:, 2 + slot, c], nT[:, slot % 2, c], w_r[:, layer, :], start=False, stop=(k == K - 1),
                                         skip_group_check=True)
                    last.then_inc(s["mm"].sem, 1)

                def shifted(i, q, slot):
                    pe.wait_ge(*s[f"rb{slot}"](16 * (q + 1)))
                    if later(i, 2):
                        pe.wait_ge(*s["res2"](i - 1))
                    b = 6 + slot % 2
                    bias(b, BLN, K, D)
                    pe.matmul(ps[:, b, :], ident[:, :], xres[:, slot, :, :].rearrange("p k d -> p (k d)"), start=False, stop=True,
                              skip_group_check=True).then_inc(s["shifted"].sem, 1)

                pipeline(pe, GROUPS, 4, ([(shifted, 7)] if layer else []) +
                         [(products, 4), (transposes(s, 0, lambda c: neigh[:, c, :, :], 0, [("nT", 1)], "tn"), 2)])

            edges("l0a")
            d0()
            beside("self", "l0b")
            d1()
            beside("own", "l1")
            d2a()
            d2b()
            edges("l3a")
            d3("d3a", 0)
            edges("l3b")
            d3("d3b", 1)


_TURNED = ("L0_gnn_W_self", "L0_gnn_W_neigh", "L0_gnn_W_agg", "L1_gnn_W_lin", "L1_gnn_W_msg", "L3_gnn_W1", "L3_gnn_W2")


def kernel(**inputs):
    import numpy as _np
    import concourse.bacc as _bacc
    from concourse import mybir as _mybir
    from concourse.bass_utils import run_bass_kernel_spmd as _run

    nc = _bacc.Bacc("TRN2", target_bir_lowering=False, num_devices=1)
    arrays, tensors = {}, {}
    for name, value in inputs.items():
        a = _np.asarray(value)
        if name in _TURNED:
            a = _np.swapaxes(a, -1, -2)
        a = _np.ascontiguousarray(a)
        arrays[f"in_{name}"] = a
        tensors[name] = nc.dram_tensor(f"in_{name}", a.shape, _mybir.dt.from_np(a.dtype), kind="ExternalInput").ap()
    out = nc.dram_tensor("out_0", (N, D), F32, kind="ExternalOutput").ap()
    program(nc, tensors, out)
    r = _run(nc, [arrays], core_ids=[0])
    return r.results[0]["out_0"]
```
